# Optimizing a Trainium2 kernel written in Bass

```python
import numpy as np
import jax
import jax.numpy as jnp

def _softmax(x, axis=-1):
    return jax.nn.softmax(x, axis=axis)

def _gelu(x):
    return jax.nn.gelu(x, approximate=True)

def _silu(x):
    return jax.nn.silu(x)

def _sigmoid(x):
    return jax.nn.sigmoid(x)

def _layernorm(x, axis=-1, eps=1e-05):
    m = jnp.mean(x, axis=axis, keepdims=True)
    v = jnp.var(x, axis=axis, keepdims=True)
    return (x - m) / jnp.sqrt(v + eps)

def _scatter_add(tgt, idx, src, axis=0):
    return tgt.at[idx].add(src)

def _segment_sum(src, seg, n):
    return jax.ops.segment_sum(src, seg, n)
kernel_name = 'mk_flamingo_gated_d4_seqx_r4_b9c0dd'

def setup_inputs(seed: int=0):
    np.random.seed(seed)
    _w = jnp.asarray

    def _rec_inputs():
        import jax
        import jax.numpy as jnp
        _rk = jax.random.key(seed)
        x = -0.0005146 + 1 * jax.random.normal(jax.random.fold_in(_rk, 1), (4, 1024, 256), jnp.float32)
        _lenS = 1024 - jax.random.randint(jax.random.fold_in(_rk, 7), (4,), 0, max(1, 1024 // 4) + 1, jnp.int32)
        _lenS2 = 77 - jax.random.randint(jax.random.fold_in(_rk, 8), (4,), 0, max(1, 77 // 4) + 1, jnp.int32)
        _ctx_768P = jax.random.normal(jax.random.fold_in(_rk, 11), (4, 16, 192), jnp.float32)
        _ctx_768c = jax.random.dirichlet(jax.random.fold_in(_rk, 511), 0.3 * jnp.ones((16,), jnp.float32), (4, 77))
        _ctx_768t = jnp.einsum('bsk,bkd->bsd', _ctx_768c, _ctx_768P)
        _ctx_768t = _ctx_768t * jax.lax.rsqrt(jnp.mean(jnp.square(_ctx_768t)) + 1e-12) * 0.953939
        ctx_768 = -0.00040386 + 0.999972 * (_ctx_768t + 0.3 * jax.random.normal(jax.random.fold_in(_rk, 611), (4, 77, 192), jnp.float32))
        _validS = jnp.arange(1024)[None, :] < _lenS[:, None]
        _validS2 = jnp.arange(77)[None, :] < _lenS2[:, None]
        _causal = jnp.tril(jnp.ones((1024, 1024), dtype=bool))
        mask_BxS2_bk0 = jnp.logical_not(jnp.broadcast_to(_validS2[:, :], (4, 77)))
        _g = jax.random.normal(jax.random.fold_in(_rk, 9001), (2, 4), jnp.float32)
        _g = jnp.sign(_g) * jnp.maximum(jnp.abs(_g), 1.0) + (_g == 0) * 1.0
        g_xattn = _g[0]
        g_ffn = _g[1]
        return (x, ctx_768, mask_BxS2_bk0, g_xattn, g_ffn)
    x, ctx_768, mask_BxS2_bk0, g_xattn, g_ffn = _rec_inputs()

    def _L0_xattn_setup():
        import jax, jax.numpy as jnp
        import numpy as np
        DIM_IN, DIM_LAT, DIM_HEAD = (192, 256, 64)
        INNER = max(DIM_LAT, DIM_IN)
        HEADS = INNER // DIM_HEAD
        SCALE = DIM_HEAD ** (-0.5)
        RMS_EPS = 1e-08
        LN_EPS = 1e-05

        def layernorm(x, g, b):
            mu = jnp.mean(x, axis=-1, keepdims=True)
            var = jnp.mean((x - mu) ** 2, axis=-1, keepdims=True)
            return (x - mu) * jax.lax.rsqrt(var + LN_EPS) * g + b

        def rmsnorm(x, gamma):
            norm = jnp.sqrt(jnp.sum(x * x, axis=-1, keepdims=True)) * x.shape[-1] ** (-0.5)
            return x / jnp.maximum(norm, RMS_EPS) * gamma
        key = jax.random.key(seed)
        ks = jax.random.split(key, 12)
        b, n, m = (4, 1024, 128)
        x = jax.random.normal(ks[0], (b, n, DIM_IN), jnp.float32)
        latents = jax.random.normal(ks[1], (b, m, DIM_LAT), jnp.float32)
        mask = jax.random.randint(ks[2], (b, n), 0, 2).astype(bool)
        s = lambda k, sh, fan: jax.random.normal(k, sh, jnp.float32) * fan ** (-0.5)
        return {'x': x, 'latents': latents, 'mask': mask, 'ln_x_g': jnp.ones((DIM_IN,), jnp.float32), 'ln_x_b': jnp.zeros((DIM_IN,), jnp.float32), 'ln_l_g': jnp.ones((DIM_LAT,), jnp.float32), 'ln_l_b': jnp.zeros((DIM_LAT,), jnp.float32), 'qn_g': jnp.ones((DIM_HEAD,), jnp.float32), 'kn_g': jnp.ones((DIM_HEAD,), jnp.float32), 'Wq': s(ks[3], (INNER, DIM_LAT), DIM_LAT), 'Wkv': s(ks[4], (2 * INNER, DIM_IN), DIM_IN), 'Wlkv': s(ks[5], (2 * INNER, DIM_LAT), DIM_LAT), 'Wo': s(ks[6], (DIM_LAT, INNER), INNER), 'bo': jnp.zeros((DIM_LAT,), jnp.float32)}
    _L0_xattn_all = _L0_xattn_setup()
    _L0_xattn_in = {k: v for k, v in _L0_xattn_all.items() if k in ('ln_x_g', 'ln_x_b', 'ln_l_g', 'ln_l_b', 'qn_g', 'kn_g', 'Wq', 'Wkv', 'Wlkv', 'Wo', 'bo')}
    del _L0_xattn_all

    def _L0_ffn_setup():
        import jax, jax.numpy as jnp
        import numpy as np
        B, S, H, E = (4, 512, 256, 8)
        key = jax.random.key(seed)
        k1, k2, k3 = jax.random.split(key, 3)
        scale_w = 1.0 / np.sqrt(H)
        return {'x': jax.random.normal(k1, (B, S, H), dtype=jnp.float32), 'router_w': jax.random.normal(k2, (H, E), dtype=jnp.float32) * scale_w, 'router_b': jnp.zeros((E,), dtype=jnp.float32), 'expert_w': jax.random.normal(k3, (E, H, H), dtype=jnp.float32) * scale_w, 'expert_b': jnp.zeros((E, H), dtype=jnp.float32)}
    _L0_ffn_all = _L0_ffn_setup()
    _L0_ffn_in = {k: v for k, v in _L0_ffn_all.items() if k in ('router_w', 'router_b', 'expert_w', 'expert_b')}
    del _L0_ffn_all

    def _L1_xattn_setup():
        import jax, jax.numpy as jnp
        import numpy as np
        NUM_HEADS = 16
        CLAMP = 10000.0
        key = jax.random.key(seed)
        ks = jax.random.split(key, 8)
        B, Nq, Nkv, Cq, Ckv = (4, 512, 512, 256, 192)
        s_q = 1.0 / np.sqrt(Cq)
        s_kv = 1.0 / np.sqrt(Ckv)
        return {'query': jax.random.normal(ks[0], (B, Nq, Cq), jnp.float32), 'key_value': jax.random.normal(ks[1], (B, Nkv, Ckv), jnp.float32), 'Wq': jax.random.normal(ks[2], (Cq, Cq), jnp.float32) * s_q, 'bq': jnp.zeros((Cq,), jnp.float32), 'Wk': jax.random.normal(ks[3], (Ckv, Cq), jnp.float32) * s_kv, 'bk': jnp.zeros((Cq,), jnp.float32), 'Wv': jax.random.normal(ks[4], (Ckv, Cq), jnp.float32) * s_kv, 'bv': jnp.zeros((Cq,), jnp.float32), 'Wo': jax.random.normal(ks[5], (Cq, Cq), jnp.float32) * s_q, 'bo': jnp.zeros((Cq,), jnp.float32)}
    _L1_xattn_all = _L1_xattn_setup()
    _L1_xattn_in = {k: v for k, v in _L1_xattn_all.items() if k in ('Wq', 'bq', 'Wk', 'bk', 'Wv', 'bv', 'Wo', 'bo')}
    del _L1_xattn_all

    def _L1_ffn_setup():
        import jax, jax.numpy as jnp
        import numpy as np
        TOP_K = 2
        key = jax.random.key(seed)
        k_x, k_g, k_w1, k_w2, k_w3 = jax.random.split(key, 5)
        B, S, D, H, E = (2, 128, 256, 128, 8)
        x = jax.random.normal(k_x, (B, S, D), dtype=jnp.float32)
        gate_w = jax.random.normal(k_g, (D, E), dtype=jnp.float32) * D ** (-0.5)
        w1 = jax.random.normal(k_w1, (E, D, H), dtype=jnp.float32) * 0.02
        w2 = jax.random.normal(k_w2, (E, H, D), dtype=jnp.float32) * 0.02
        w3 = jax.random.normal(k_w3, (E, D, H), dtype=jnp.float32) * 0.02
        return {'x': x, 'gate_w': gate_w, 'w1': w1, 'w2': w2, 'w3': w3}
    _L1_ffn_all = _L1_ffn_setup()
    _L1_ffn_in = {k: v for k, v in _L1_ffn_all.items() if k in ('gate_w', 'w1', 'w2', 'w3')}
    del _L1_ffn_all

    def _L2_xattn_setup():
        import jax, jax.numpy as jnp
        import numpy as np
        B, LQ, LKV = (2, 512, 512)
        C, CTX, H, DK = (256, 192, 16, 64)
        SCALE = DK ** (-0.5)
        key = jax.random.key(seed)
        kx, ky, kq, kkv, kp, kb = jax.random.split(key, 6)
        return {'x': jax.random.normal(kx, (B, LQ, C), dtype=jnp.float32), 'y': jax.random.normal(ky, (B, LKV, CTX), dtype=jnp.float32), 'Wq': jax.random.normal(kq, (C, H * DK), dtype=jnp.float32) * C ** (-0.5), 'Wkv': jax.random.normal(kkv, (CTX, 2 * H * DK), dtype=jnp.float32) * CTX ** (-0.5), 'Wproj': jax.random.normal(kp, (H * DK, C), dtype=jnp.float32) * (H * DK) ** (-0.5), 'bproj': jax.random.normal(kb, (C,), dtype=jnp.float32) * 0.01}
    _L2_xattn_all = _L2_xattn_setup()
    _L2_xattn_in = {k: v for k, v in _L2_xattn_all.items() if k in ('Wq', 'Wkv', 'Wproj', 'bproj')}
    del _L2_xattn_all

    def _L2_ffn_setup():
        import jax, jax.numpy as jnp
        import numpy as np
        INT4_QMAX = 7.0

        def simulate_quantize_int4(w):
            scale = jnp.max(jnp.abs(w)) / INT4_QMAX
            q = jnp.clip(jnp.round(w / scale), -8.0, 7.0)
            return q * scale
        key = jax.random.key(seed)
        k_x, k_w, k_bias, k_a, k_b = jax.random.split(key, 5)
        d_in, features, rank = (256, 256, 16)
        x = jax.random.normal(k_x, (4, 2048, d_in), dtype=jnp.float32)
        kernel = jax.random.normal(k_w, (d_in, features), dtype=jnp.float32)
        bias = jax.random.normal(k_bias, (features,), dtype=jnp.float32)
        a = jax.random.normal(k_a, (d_in, rank), dtype=jnp.float32) * (1.0 / np.sqrt(d_in))
        b = jax.random.normal(k_b, (rank, features), dtype=jnp.float32) * 0.01
        return {'x': x, 'kernel': kernel, 'bias': bias, 'a': a, 'b': b}
    _L2_ffn_all = _L2_ffn_setup()
    _L2_ffn_in = {k: v for k, v in _L2_ffn_all.items() if k in ('kernel', 'bias', 'a', 'b')}
    del _L2_ffn_all

    def _L3_xattn_setup():
        import jax, jax.numpy as jnp
        import numpy as np
        IMAGE_DIM = 256
        TEXT_DIM = 192
        NUM_HEADS = 16
        HEAD_DIM = IMAGE_DIM // NUM_HEADS
        key = jax.random.key(seed)
        ks = jax.random.split(key, 14)
        B, N, M = (4, 1024, 128)
        s_img = 1.0 / np.sqrt(IMAGE_DIM)
        s_txt = 1.0 / np.sqrt(TEXT_DIM)
        s_ff = 1.0 / np.sqrt(2 * IMAGE_DIM)
        return {'x': jax.random.normal(ks[0], (B, N, IMAGE_DIM), jnp.float32), 'y': jax.random.normal(ks[1], (B, M, TEXT_DIM), jnp.float32), 'Wq': jax.random.normal(ks[2], (IMAGE_DIM, IMAGE_DIM), jnp.float32) * s_img, 'bq': jax.random.normal(ks[3], (IMAGE_DIM,), jnp.float32) * s_img, 'Wk': jax.random.normal(ks[4], (TEXT_DIM, IMAGE_DIM), jnp.float32) * s_txt, 'bk': jax.random.normal(ks[5], (IMAGE_DIM,), jnp.float32) * s_txt, 'Wv': jax.random.normal(ks[6], (TEXT_DIM, IMAGE_DIM), jnp.float32) * s_txt, 'bv': jax.random.normal(ks[7], (IMAGE_DIM,), jnp.float32) * s_txt, 'W1': jax.random.normal(ks[8], (IMAGE_DIM, 2 * IMAGE_DIM), jnp.float32) * s_img, 'b1': jax.random.normal(ks[9], (2 * IMAGE_DIM,), jnp.float32) * s_img, 'W2': jax.random.normal(ks[10], (2 * IMAGE_DIM, IMAGE_DIM), jnp.float32) * s_ff, 'b2': jax.random.normal(ks[11], (IMAGE_DIM,), jnp.float32) * s_ff}
    _L3_xattn_all = _L3_xattn_setup()
    _L3_xattn_in = {k: v for k, v in _L3_xattn_all.items() if k in ('Wq', 'bq', 'Wk', 'bk', 'Wv', 'bv', 'W1', 'b1', 'W2', 'b2')}
    del _L3_xattn_all

    def _L3_ffn_setup():
        import math
        import jax, jax.numpy as jnp
        import numpy as np
        NUM_EXPERTS = 8
        CAPACITY_FACTOR = 1.5
        key = jax.random.key(seed)
        ks = jax.random.split(key, 4)
        B, T, D, F, E = (4, 512, 256, 1024, NUM_EXPERTS)
        scale = 0.02
        return {'x': jax.random.normal(ks[0], (B, T, D), dtype=jnp.float32), 'router_w': jax.random.normal(ks[1], (E, D), dtype=jnp.float32) * scale, 'w1': jax.random.normal(ks[2], (E, D, F), dtype=jnp.float32) * scale, 'b1': jnp.zeros((E, F), dtype=jnp.float32), 'w2': jax.random.normal(ks[3], (E, F, D), dtype=jnp.float32) * scale, 'b2': jnp.zeros((E, D), dtype=jnp.float32)}
    _L3_ffn_all = _L3_ffn_setup()
    _L3_ffn_in = {k: v for k, v in _L3_ffn_all.items() if k in ('router_w', 'w1', 'b1', 'w2', 'b2')}
    del _L3_ffn_all
    return {'x': x, 'ctx_768': ctx_768, 'mask_BxS2_bk0': mask_BxS2_bk0, 'g_xattn': g_xattn, 'g_ffn': g_ffn, 'L0_xattn_ln_x_g': _L0_xattn_in['ln_x_g'], 'L0_xattn_ln_x_b': _L0_xattn_in['ln_x_b'], 'L0_xattn_ln_l_g': _L0_xattn_in['ln_l_g'], 'L0_xattn_ln_l_b': _L0_xattn_in['ln_l_b'], 'L0_xattn_qn_g': _L0_xattn_in['qn_g'], 'L0_xattn_kn_g': _L0_xattn_in['kn_g'], 'L0_xattn_Wq': _L0_xattn_in['Wq'], 'L0_xattn_Wkv': _L0_xattn_in['Wkv'], 'L0_xattn_Wlkv': _L0_xattn_in['Wlkv'], 'L0_xattn_Wo': _L0_xattn_in['Wo'], 'L0_xattn_bo': _L0_xattn_in['bo'], 'L0_ffn_router_w': _L0_ffn_in['router_w'], 'L0_ffn_router_b': _L0_ffn_in['router_b'], 'L0_ffn_expert_w': _L0_ffn_in['expert_w'], 'L0_ffn_expert_b': _L0_ffn_in['expert_b'], 'L1_xattn_Wq': _L1_xattn_in['Wq'], 'L1_xattn_bq': _L1_xattn_in['bq'], 'L1_xattn_Wk': _L1_xattn_in['Wk'], 'L1_xattn_bk': _L1_xattn_in['bk'], 'L1_xattn_Wv': _L1_xattn_in['Wv'], 'L1_xattn_bv': _L1_xattn_in['bv'], 'L1_xattn_Wo': _L1_xattn_in['Wo'], 'L1_xattn_bo': _L1_xattn_in['bo'], 'L1_ffn_gate_w': _L1_ffn_in['gate_w'], 'L1_ffn_w1': _L1_ffn_in['w1'], 'L1_ffn_w2': _L1_ffn_in['w2'], 'L1_ffn_w3': _L1_ffn_in['w3'], 'L2_xattn_Wq': _L2_xattn_in['Wq'], 'L2_xattn_Wkv': _L2_xattn_in['Wkv'], 'L2_xattn_Wproj': _L2_xattn_in['Wproj'], 'L2_xattn_bproj': _L2_xattn_in['bproj'], 'L2_ffn_kernel': _L2_ffn_in['kernel'], 'L2_ffn_bias': _L2_ffn_in['bias'], 'L2_ffn_a': _L2_ffn_in['a'], 'L2_ffn_b': _L2_ffn_in['b'], 'L3_xattn_Wq': _L3_xattn_in['Wq'], 'L3_xattn_bq': _L3_xattn_in['bq'], 'L3_xattn_Wk': _L3_xattn_in['Wk'], 'L3_xattn_bk': _L3_xattn_in['bk'], 'L3_xattn_Wv': _L3_xattn_in['Wv'], 'L3_xattn_bv': _L3_xattn_in['bv'], 'L3_xattn_W1': _L3_xattn_in['W1'], 'L3_xattn_b1': _L3_xattn_in['b1'], 'L3_xattn_W2': _L3_xattn_in['W2'], 'L3_xattn_b2': _L3_xattn_in['b2'], 'L3_ffn_router_w': _L3_ffn_in['router_w'], 'L3_ffn_w1': _L3_ffn_in['w1'], 'L3_ffn_b1': _L3_ffn_in['b1'], 'L3_ffn_w2': _L3_ffn_in['w2'], 'L3_ffn_b2': _L3_ffn_in['b2']}

def reference(x, ctx_768, mask_BxS2_bk0, g_xattn, g_ffn, L0_xattn_ln_x_g, L0_xattn_ln_x_b, L0_xattn_ln_l_g, L0_xattn_ln_l_b, L0_xattn_qn_g, L0_xattn_kn_g, L0_xattn_Wq, L0_xattn_Wkv, L0_xattn_Wlkv, L0_xattn_Wo, L0_xattn_bo, L0_ffn_router_w, L0_ffn_router_b, L0_ffn_expert_w, L0_ffn_expert_b, L1_xattn_Wq, L1_xattn_bq, L1_xattn_Wk, L1_xattn_bk, L1_xattn_Wv, L1_xattn_bv, L1_xattn_Wo, L1_xattn_bo, L1_ffn_gate_w, L1_ffn_w1, L1_ffn_w2, L1_ffn_w3, L2_xattn_Wq, L2_xattn_Wkv, L2_xattn_Wproj, L2_xattn_bproj, L2_ffn_kernel, L2_ffn_bias, L2_ffn_a, L2_ffn_b, L3_xattn_Wq, L3_xattn_bq, L3_xattn_Wk, L3_xattn_bk, L3_xattn_Wv, L3_xattn_bv, L3_xattn_W1, L3_xattn_b1, L3_xattn_W2, L3_xattn_b2, L3_ffn_router_w, L3_ffn_w1, L3_ffn_b1, L3_ffn_w2, L3_ffn_b2):
    import jax
    import jax.numpy as jnp

    def _L0_xattn_ref(x, latents, mask, ln_x_g, ln_x_b, ln_l_g, ln_l_b, qn_g, kn_g, Wq, Wkv, Wlkv, Wo, bo):
        import jax, jax.numpy as jnp
        import numpy as np
        DIM_IN, DIM_LAT, DIM_HEAD = (192, 256, 64)
        INNER = max(DIM_LAT, DIM_IN)
        HEADS = INNER // DIM_HEAD
        SCALE = DIM_HEAD ** (-0.5)
        RMS_EPS = 1e-08
        LN_EPS = 1e-05

        def layernorm(x, g, b):
            mu = jnp.mean(x, axis=-1, keepdims=True)
            var = jnp.mean((x - mu) ** 2, axis=-1, keepdims=True)
            return (x - mu) * jax.lax.rsqrt(var + LN_EPS) * g + b

        def rmsnorm(x, gamma):
            norm = jnp.sqrt(jnp.sum(x * x, axis=-1, keepdims=True)) * x.shape[-1] ** (-0.5)
            return x / jnp.maximum(norm, RMS_EPS) * gamma
        b, n, _ = x.shape
        m = latents.shape[1]
        xn = layernorm(x, ln_x_g, ln_x_b)
        ln = layernorm(latents, ln_l_g, ln_l_b)
        q = ln @ Wq.T
        kv = jnp.concatenate([xn @ Wkv.T, ln @ Wlkv.T], axis=1)
        k, v = (kv[..., :INNER], kv[..., INNER:])
        split_heads = lambda t: t.reshape(t.shape[0], t.shape[1], HEADS, DIM_HEAD).transpose(0, 2, 1, 3)
        q, k, v = (split_heads(q), split_heads(k), split_heads(v))
        qn = rmsnorm(q, qn_g) * SCALE
        kn = rmsnorm(k, kn_g)
        attn = jnp.einsum('bhid,bhjd->bhij', qn, kn)
        full_mask = jnp.pad(mask, ((0, 0), (0, m)), constant_values=True)
        attn = jnp.where(full_mask[:, None, None, :], attn, -jnp.finfo(attn.dtype).max)
        attn = jax.nn.softmax(attn, axis=-1)
        out = jnp.einsum('bhij,bhjd->bhid', attn, v)
        out = out.transpose(0, 2, 1, 3).reshape(b, m, INNER)
        return out @ Wo.T + bo

    def _L0_ffn_ref(x, router_w, router_b, expert_w, expert_b):
        import jax, jax.numpy as jnp
        import numpy as np
        B, S, H, E = (4, 512, 256, 8)
        b, s, h = x.shape
        xt = x.reshape(b * s, h)
        logits = xt @ router_w + router_b
        probs = jax.nn.softmax(logits, axis=-1)
        gate = jnp.max(probs, axis=-1)
        idx = jnp.argmax(probs, axis=-1)
        out_all = jnp.einsum('th,ehd->ted', xt, expert_w) + expert_b[None, :, :]
        e_out = jnp.take_along_axis(out_all, idx[:, None, None], axis=1)[:, 0, :]
        y = gate[:, None] * e_out
        return y.reshape(b, s, h)

    def _L1_xattn_ref(query, key_value, Wq, bq, Wk, bk, Wv, bv, Wo, bo):
        import jax, jax.numpy as jnp
        import numpy as np
        NUM_HEADS = 16
        CLAMP = 10000.0
        B, Nq, Cq = query.shape
        Nkv = key_value.shape[1]
        H = NUM_HEADS
        D = Cq // H
        scale = D ** (-0.5)
        q = (query @ Wq + bq).reshape(B, Nq, H, D).transpose(0, 2, 1, 3)
        k = (key_value @ Wk + bk).reshape(B, Nkv, H, D).transpose(0, 2, 1, 3)
        v = (key_value @ Wv + bv).reshape(B, Nkv, H, D).transpose(0, 2, 1, 3)
        attn = jnp.einsum('bhqd,bhkd->bhqk', q, k) * scale
        attn = jnp.clip(attn, -CLAMP, CLAMP)
        attn = jax.nn.softmax(attn, axis=-1)
        attn = jnp.where(jnp.any(jnp.isnan(attn)), jnp.asarray(1.0 / Nkv, attn.dtype), attn)
        x = jnp.einsum('bhqk,bhkd->bqhd', attn, v).reshape(B, Nq, Cq)
        return x @ Wo + bo

    def _L1_ffn_ref(x, gate_w, w1, w2, w3):
        import jax, jax.numpy as jnp
        import numpy as np
        TOP_K = 2
        B, S, D = x.shape
        E = gate_w.shape[1]
        xf = x.reshape(B * S, D)
        T = B * S
        logits = xf @ gate_w
        scores = jax.nn.softmax(logits, axis=-1)
        top_scores, top_idx = jax.lax.top_k(scores, TOP_K)
        scale = jnp.zeros((T, E), dtype=x.dtype).at[jnp.arange(T)[:, None], top_idx].set(top_scores)
        xs = scale.T[:, :, None] * xf[None, :, :]
        h = jax.nn.silu(jnp.einsum('etd,edh->eth', xs, w1)) * jnp.einsum('etd,edh->eth', xs, w3)
        y = jnp.einsum('eth,ehd->etd', h, w2)
        out = y.sum(axis=0)
        return out.reshape(B, S, D)

    def _L2_xattn_ref(x, y, Wq, Wkv, Wproj, bproj):
        import jax, jax.numpy as jnp
        import numpy as np
        B, LQ, LKV = (2, 512, 512)
        C, CTX, H, DK = (256, 192, 16, 64)
        SCALE = DK ** (-0.5)
        b, lq, _ = x.shape
        lkv = y.shape[1]
        q = (x @ Wq).reshape(b, lq, H, DK).transpose(0, 2, 1, 3)
        kv = (y @ Wkv).reshape(b, lkv, 2, H, DK).transpose(2, 0, 3, 1, 4)
        k, v = (kv[0], kv[1])
        atten = jax.nn.softmax(jnp.einsum('bhid,bhjd->bhij', q, k) * SCALE, axis=-1)
        res = jnp.einsum('bhij,bhjd->bhid', atten, v)
        res = res.transpose(0, 2, 1, 3).reshape(b, lq, H * DK)
        out = res @ Wproj + bproj
        return out

    def _L2_ffn_ref(x, kernel, bias, a, b):
        import jax, jax.numpy as jnp
        import numpy as np
        INT4_QMAX = 7.0

        def simulate_quantize_int4(w):
            scale = jnp.max(jnp.abs(w)) / INT4_QMAX
            q = jnp.clip(jnp.round(w / scale), -8.0, 7.0)
            return q * scale
        w = simulate_quantize_int4(kernel)
        y = jnp.einsum('bsd,df->bsf', x, w) + bias
        lora = jnp.einsum('bsr,rf->bsf', jnp.einsum('bsd,dr->bsr', x, a), b)
        return y + lora

    def _L3_xattn_ref(x, y, Wq, bq, Wk, bk, Wv, bv, W1, b1, W2, b2):
        import jax, jax.numpy as jnp
        import numpy as np
        IMAGE_DIM = 256
        TEXT_DIM = 192
        NUM_HEADS = 16
        HEAD_DIM = IMAGE_DIM // NUM_HEADS
        B, N, _ = x.shape
        M = y.shape[1]
        q = (x @ Wq + bq).reshape(B, N, NUM_HEADS, HEAD_DIM)
        k = (y @ Wk + bk).reshape(B, M, NUM_HEADS, HEAD_DIM)
        v = (y @ Wv + bv).reshape(B, M, NUM_HEADS, HEAD_DIM)
        scale = 1.0 / np.sqrt(HEAD_DIM)
        scores = jnp.einsum('bnhd,bmhd->bhnm', q, k) * scale
        attn = jax.nn.softmax(scores, axis=-1)
        out = jnp.einsum('bhnm,bmhd->bnhd', attn, v).reshape(B, N, IMAGE_DIM)
        h = jax.nn.relu(out @ W1 + b1)
        return h @ W2 + b2

    def _L3_ffn_ref(x, router_w, w1, b1, w2, b2):
        import math
        import jax, jax.numpy as jnp
        import numpy as np
        NUM_EXPERTS = 8
        CAPACITY_FACTOR = 1.5
        B, T, D = x.shape
        E = router_w.shape[0]
        N = B * T
        C = max(math.ceil(CAPACITY_FACTOR * N / E), 1)
        x_flat = x.reshape(N, D)
        logits = x_flat @ router_w.T
        probs = jax.nn.softmax(logits, axis=-1)
        chosen_e = jnp.argmax(probs, axis=-1)
        chosen_p = jnp.max(probs, axis=-1)
        onehot = jax.nn.one_hot(chosen_e, E, dtype=jnp.float32)
        pos = jnp.take_along_axis(jnp.cumsum(onehot, axis=0), chosen_e[:, None], axis=1)[:, 0] - 1.0
        pos = pos.astype(jnp.int32)
        kept = pos < C
        pos_c = jnp.clip(pos, 0, C - 1)
        buf = jnp.zeros((E, C, D), dtype=x.dtype).at[chosen_e, pos_c].add(x_flat * kept[:, None].astype(x.dtype))
        h = jax.nn.gelu(jnp.einsum('ecd,edf->ecf', buf, w1) + b1[:, None, :], approximate=False)
        eo = jnp.einsum('ecf,efd->ecd', h, w2) + b2[:, None, :]
        y = eo[chosen_e, pos_c] * (chosen_p * kept.astype(x.dtype))[:, None]
        return y.reshape(B, T, D)
    x = x + jnp.tanh(g_xattn[0]) * _L0_xattn_ref(ctx_768, _layernorm(x, axis=-1), mask_BxS2_bk0, L0_xattn_ln_x_g, L0_xattn_ln_x_b, L0_xattn_ln_l_g, L0_xattn_ln_l_b, L0_xattn_qn_g, L0_xattn_kn_g, L0_xattn_Wq, L0_xattn_Wkv, L0_xattn_Wlkv, L0_xattn_Wo, L0_xattn_bo)
    x = x + jnp.tanh(g_ffn[0]) * _L0_ffn_ref(_layernorm(x, axis=-1), L0_ffn_router_w, L0_ffn_router_b, L0_ffn_expert_w, L0_ffn_expert_b)
    x = x + jnp.tanh(g_xattn[1]) * _L1_xattn_ref(_layernorm(x, axis=-1), ctx_768, L1_xattn_Wq, L1_xattn_bq, L1_xattn_Wk, L1_xattn_bk, L1_xattn_Wv, L1_xattn_bv, L1_xattn_Wo, L1_xattn_bo)
    x = x + jnp.tanh(g_ffn[1]) * _L1_ffn_ref(_layernorm(x, axis=-1), L1_ffn_gate_w, L1_ffn_w1, L1_ffn_w2, L1_ffn_w3)
    x = x + jnp.tanh(g_xattn[2]) * _L2_xattn_ref(_layernorm(x, axis=-1), ctx_768, L2_xattn_Wq, L2_xattn_Wkv, L2_xattn_Wproj, L2_xattn_bproj)
    x = x + jnp.tanh(g_ffn[2]) * _L2_ffn_ref(_layernorm(x, axis=-1), L2_ffn_kernel, L2_ffn_bias, L2_ffn_a, L2_ffn_b)
    x = x + jnp.tanh(g_xattn[3]) * _L3_xattn_ref(_layernorm(x, axis=-1), ctx_768, L3_xattn_Wq, L3_xattn_bq, L3_xattn_Wk, L3_xattn_bk, L3_xattn_Wv, L3_xattn_bv, L3_xattn_W1, L3_xattn_b1, L3_xattn_W2, L3_xattn_b2)
    x = x + jnp.tanh(g_ffn[3]) * _L3_ffn_ref(_layernorm(x, axis=-1), L3_ffn_router_w, L3_ffn_w1, L3_ffn_b1, L3_ffn_w2, L3_ffn_b2)
    return x

_drawn_inputs = setup_inputs


def setup_inputs(seed=0):
    import zlib

    import numpy as np

    out = dict(_drawn_inputs(seed))
    spreads = {'L0_xattn_ln_x_g': (1.0, 0.6),
     'L0_xattn_ln_x_b': (0.0, 0.8),
     'L0_xattn_ln_l_g': (1.0, 0.2),
     'L0_xattn_ln_l_b': (0.0, 0.1),
     'L0_xattn_qn_g': (1.0, 0.6),
     'L0_xattn_kn_g': (1.0, 0.6),
     'L0_xattn_bo': (0.0, 0.1),
     'L0_ffn_router_b': (0.0, 0.1),
     'L0_ffn_expert_b': (0.0, 0.329),
     'L1_xattn_bq': (0.0, 0.422),
     'L1_xattn_bk': (0.0, 2.0),
     'L1_xattn_bv': (0.0, 0.1),
     'L1_xattn_bo': (0.0, 0.1),
     'L3_ffn_b1': (0.0, 0.8),
     'L3_ffn_b2': (0.0, 2.0)}
    factors = {'g_ffn': 8.0,
     'L0_xattn_Wkv': 3.379,
     'L1_ffn_gate_w': 8.0,
     'L1_ffn_w1': 8.0,
     'L1_ffn_w2': 8.0,
     'L1_ffn_w3': 8.0,
     'L2_xattn_bproj': 8.0,
     'L2_ffn_a': 8.0,
     'L2_ffn_b': 8.0,
     'L3_xattn_Wq': 6.258,
     'L3_xattn_bq': 8.0,
     'L3_xattn_Wk': 6.195,
     'L3_xattn_bk': 64.0,
     'L3_xattn_Wv': 2.847,
     'L3_xattn_bv': 8.0,
     'L3_xattn_W1': 2.988,
     'L3_xattn_b1': 8.0,
     'L3_xattn_b2': 8.0,
     'L3_ffn_router_w': 8.0,
     'L3_ffn_w1': 8.0,
     'L3_ffn_w2': 8.0}
    for name, (base, spread) in spreads.items():
        noise = np.random.default_rng([zlib.crc32(name.encode()), seed]).standard_normal(out[name].shape)
        drawn = base * np.exp(spread * noise) if base else spread * noise
        out[name] = jnp.asarray(drawn.astype(out[name].dtype))
    for name, factor in factors.items():
        out[name] = (out[name] * factor).astype(out[name].dtype)
    return out
```

```python
from contextlib import ExitStack, contextmanager

import concourse.bass as bass
from concourse import mybir

F32 = mybir.dt.float32
BF16 = mybir.dt.bfloat16
U8 = mybir.dt.uint8
U32 = mybir.dt.uint32
ALU = mybir.AluOpType
ACT = mybir.ActivationFunctionType
AX = mybir.AxisListType

P = 128
B, S, D = 4, 1024, 256
T = S // P
DK = D // P
BLK = 512
NB = S // BLK
TB = BLK // P
M = 77
C = 192
C1 = C - P
E = 8
H0, DH0 = 4, 64
H1, DH1 = 16, 16
H2, DH2 = 16, 64
G = DK
HG = H1 // G
GM = HG * M
CH = [(c * P, min(P, GM - c * P)) for c in range((GM + P - 1) // P)]
F3 = 1024
CAP = 768
CT = CAP // P
FC = F3 // P
SLOTS = E * CAP
FAR = 1.0e6
EPS = 1e-5
LOW = 1.0e30


COLS, at = {}, 0
for name, n in (("gates", 8), ("rb0", E), ("ln_x_g", 2), ("ln_x_b", 2), ("ln_l_g", 2), ("ln_l_b", 2), ("qn_g", 1),
                ("kn_g", 1), ("bq1", 2), ("bq3", 2), ("b1_3", 4)):
    COLS[name] = at
    at += n
GATED = (("bo0", 0), ("bo1", 1), ("bproj", 2), ("bias2", 6), ("b2_3", 3))
ROWS = {name: i for i, (name, _) in enumerate(GATED)}
CLAMP = 10000.0


def flamingo_kernel(nc, a, out, upto=8):
    ctx = ExitStack()
    with ctx:
        named = []

        def sb(name, shape, dt=F32, stack=ctx):
            named.append(name)
            name = name if stack is ctx else f"{name}_{len(named)}"
            return stack.enter_context(nc.sbuf_tensor(name, shape, dt))

        def sem(name):
            return ctx.enter_context(nc.semaphore(name))

        psum = ctx.enter_context(nc.psum_tensor("psum", [P, 8 * 512], F32))

        def bank(i, n=512):
            return psum[:, 512 * i:512 * i + n]

        residual = nc.dram_tensor("residual", [B * S, D], F32, kind="Internal").ap()
        slots_in = nc.dram_tensor("slots_in", [SLOTS, D], F32, kind="Internal").ap()
        slots_out = nc.dram_tensor("slots_out", [SLOTS, D], F32, kind="Internal").ap()

        NSEM = 40
        sem_banks = [[sem(f"stage_{i}_{j}") for j in range(NSEM)] for i in range(2)]
        turn = [1]

        @contextmanager
        def stage(name, count):
            turn[0] ^= 1
            old = sem_banks[1 - turn[0]]
            named.append(name)
            with nc.Block(f"{name}_{len(named)}") as block:
                @block.sync
                def _(sp):
                    sp.sem_clear(range(old[0].num, old[-1].num + 1))
                yield block, sem_banks[turn[0]][:count]

        sent = sem("rows_sent")
        fetched = [sem(f"row_fetched_{t}") for t in range(T)]

        loads = {}

        ident = sb("ident", [P, P])
        ones_bf = sb("ones_bf", [1, P], BF16)
        ones_f = sb("ones_f", [P, P])
        upper = sb("upper", [P, P])
        cols = sb("cols", list(a["cols"].shape))
        rows = sb("rows", list(a["rows"].shape))
        tg = sb("tg", [P, 8])
        neg_half = sb("neg_half", [P, 16])
        rank = sb("rank", [P, T, E])
        head_of_feature = sb("head_of_feature", [P, HG])
        head_of_row = sb("head_of_row", [P, len(CH), HG])
        pick_row = sb("pick_row", [H1, G, GM], BF16)
        pick0 = sb("pick0", [H0, H0, P], BF16)
        pick2 = sb("pick2", [H2, H2, M], BF16)
        mask_col = sb("mask_col", [M, 1])
        mask_row = sb("mask_row", [1, M], BF16)
        slot = sb("slot", [P, B * T], U32)
        prob = sb("prob", [P, B * T])
        taken = sb("taken", [P, E])

        x = sb("x", [P, T, D])
        xn = sb("xn", [P, T, D])
        xT = sb("xT", [P, DK, S])
        ctxT = sb("ctxT", [P, 2, M])
        cnT = sb("cnT", [P, 2, M])
        ctx_rep = sb("ctx_rep", [P, 2, GM])

        zeros = xn

        arena = ExitStack()
        ctx.enter_context(arena)

        def wsb(name, shape):
            return arena.enter_context(nc.sbuf_tensor(name, shape, F32))

        w0_qkv = wsb("w0_qkv", [P, DK, 3 * D])
        w0_ckv = wsb("w0_ckv", [P, 2, 2 * D])
        w0_o = wsb("w0_o", [P, DK, D])
        r0 = wsb("r0", [P, DK, E])
        e0 = wsb("e0", [P, DK, E * D])
        e0_b = wsb("e0_b", [E, D])
        w1_q = wsb("w1_q", [P, DK, D])
        w1_k = wsb("w1_k", [P, 2, D])
        w1_v = wsb("w1_v", [P, 2, D])
        w1_o = wsb("w1_o", [P, DK, D])
        r1 = wsb("r1", [P, DK, E])
        e1_up = wsb("e1_up", [P, DK, E * D])
        e1_down = wsb("e1_down", [P, E, D])
        w2_q = wsb("w2_q", [P, DK, H2 * DH2])
        w2_kv = wsb("w2_kv", [P, 2, 2 * H2 * DH2])
        w2_o = wsb("w2_o", [P, H2 * DH2 // P, D])
        wq8 = wsb("wq8", [P, DK, D])
        lora_a = wsb("lora_a", [P, DK, 16])
        lora_b = wsb("lora_b", [16, D])
        w3_q = wsb("w3_q", [P, DK, D])
        w3_k = wsb("w3_k", [P, 2, D])
        w3_v = wsb("w3_v", [P, 2, D])
        w3_1 = wsb("w3_1", [P, DK, 2 * D])
        w3_2 = wsb("w3_2", [P, 2 * DK, D])
        r3 = wsb("r3", [P, DK, E])

        def col(name, k=0):
            return cols[:, COLS[name] + k:COLS[name] + k + 1]

        def row(name):
            return rows[:, ROWS[name] * D:(ROWS[name] + 1) * D]

        def load(eng, group, *pairs):
            loads[group] = (sem("load_" + group), 16 * len(pairs))
            for dst, src in pairs:
                eng.dma_start(dst, src).then_inc(loads[group][0], 16)

        def loaded(eng, group):
            eng.wait_ge(*loads[group])

        def chunked(dst, src):
            n = src.shape[0]
            if n % P == 0:
                return [(dst[:, :, :], src.rearrange("(k p) n -> p k n", p=P))]
            return [(dst[:, 0, :], src[0:P, :]), (dst[0:n - P, 1, :], src[P:n, :])]

        with stage("prepare", 9) as (block, (zeroed, selected, tanhed, maxed, absmax, scaled,
                                              rounded, gates, cleared)):
            quant_tmp = ExitStack()
            kern = sb("kern", [P, DK, D], stack=quant_tmp)
            kscale = sb("kscale", [P, 4], stack=quant_tmp)

            @block.sync
            def _(sp):
                load(sp, "cols", (cols[:, :], a["cols"]))
                load(sp, "rows", (rows[:, :], a["rows"]))
                load(sp, "kern", *chunked(kern, a["L2_ffn_kernel"]))
                load(sp, "w0", *chunked(w0_qkv, a["w0_qkv"]), *chunked(w0_ckv, a["w0_ckv"]),
                     *chunked(w0_o, a["w0_o"]))
                load(sp, "e0", *chunked(r0, a["L0_ffn_router_w"]), (e0_b[:, :], a["L0_ffn_expert_b"]),
                     *[(e0[:, :, e * D:(e + 1) * D],
                        a["L0_ffn_expert_w"][e].rearrange("(k p) n -> p k n", p=P)) for e in range(E)])
                load(sp, "w1", *chunked(w1_q, a["L1_xattn_Wq"]), *chunked(w1_k, a["w1_k"]),
                     *chunked(w1_v, a["w1_v"]), *chunked(w1_o, a["L1_xattn_Wo"]))
                load(sp, "e1", *chunked(r1, a["L1_ffn_gate_w"]),
                     *[(e1_up[:, :, e * D + i * P:e * D + (i + 1) * P],
                        a[w][e].rearrange("(k p) n -> p k n", p=P))
                       for e in range(E) for i, w in enumerate(("L1_ffn_w1", "L1_ffn_w3"))],
                     (e1_down[:, :, :], a["L1_ffn_w2"].rearrange("e p n -> p e n")))
                load(sp, "w2", *chunked(w2_q, a["L2_xattn_Wq"]), *chunked(w2_kv, a["L2_xattn_Wkv"]),
                     *chunked(w2_o, a["L2_xattn_Wproj"]))
                load(sp, "lora", *chunked(lora_a, a["L2_ffn_a"]), (lora_b[:, :], a["L2_ffn_b"]))
                load(sp, "w3", *chunked(w3_q, a["L3_xattn_Wq"]), *chunked(w3_k, a["w3_k"]),
                     *chunked(w3_v, a["w3_v"]), *chunked(w3_1, a["L3_xattn_W1"]),
                     *chunked(w3_2, a["L3_xattn_W2"]), *chunked(r3, a["r3"]))
                sp.wait_ge(cleared, 1)
                zrows = slots_in.rearrange("(n p r) d -> n p (r d)", p=P, r=T)
                load(sp, "zero", *[(zrows[n], zeros[:, :, :].rearrange("p t d -> p (t d)"))
                                   for n in range(SLOTS // (P * T))])
                loaded(sp, "zero")

            @block.gpsimd
            def _(pool):
                n = [0]

                def fill(ap, value):
                    pool.memset(ap, value).then_inc(zeroed, 1)
                    n[0] += 1
                fill(ident[:, :], 0.0)
                fill(upper[:, :], 1.0)
                fill(head_of_feature[:, :], 1.0)
                fill(head_of_row[:, :, :], 1.0)
                fill(pick_row[:, :, :], 0.0)
                fill(pick0[:, :, :], 0.0)
                fill(pick2[:, :, :], 0.0)
                fill(ones_bf[:, :], 1.0)
                fill(ones_f[:, :], 1.0)
                fill(neg_half[:, :], -0.5)
                fill(taken[:, :], 0.0)
                fill(ctxT[:, :, :], 1.0)
                for e in range(E):
                    fill(rank[:, :, e:e + 1], float(E - e))
                pool.wait_ge(zeroed, n[0])

                def choose(ap, op, value, base, pattern, mult):
                    pool.affine_select(out=ap, in_=ap, compare_op=op, fill=value, base=base, pattern=pattern,
                                       channel_multiplier=mult).then_inc(selected, 1)
                choose(ident[:, :], ALU.not_equal, 1.0, 0, [[-1, P]], 1)
                choose(upper[:, :], ALU.is_ge, 0.0, 0, [[1, P]], -1)
                choose(head_of_feature[:, :], ALU.is_ge, 0.0, 0, [[-DH1, HG]], 1)
                choose(head_of_row[:, :, :], ALU.is_ge, 0.0, 0, [[P, len(CH)], [-M, HG]], 1)
                choose(pick_row[:, :, :].rearrange("p g (h m) -> p g h m", m=M), ALU.not_equal, 1.0, 0,
                       [[-HG, G], [-1, HG], [0, M]], 1)
                choose(pick0[:, :, :], ALU.not_equal, 1.0, 0, [[-1, H0], [0, P]], 1)
                choose(pick2[:, :, :], ALU.not_equal, 1.0, 0, [[-1, H2], [0, M]], 1)
                pool.wait_ge(selected, 7)
                choose(head_of_feature[:, :], ALU.is_ge, 0.0, DH1 - 1, [[DH1, HG]], -1)
                choose(head_of_row[:, :, :], ALU.is_ge, 0.0, M - 1, [[-P, len(CH)], [M, HG]], -1)
                pool.wait_ge(maxed, 1)
                pool.partition_all_reduce(kscale[:, 1:2], kscale[:, 0:1], P,
                                          bass.bass_isa.ReduceOp.max).then_inc(absmax, 1)

            @block.scalar
            def _(act):
                loaded(act, "cols")
                act.activation(tg[:, :], cols[:, COLS["gates"]:COLS["gates"] + 8], ACT.Tanh).then_inc(tanhed, 1)

            @block.vector
            def _(dve):
                dve.memset(zeros[:, :, :], 0.0).then_inc(cleared, 1)
                loaded(dve, "rows")
                dve.wait_ge(tanhed, 1)
                for name, g in GATED:
                    dve.tensor_scalar(row(name), row(name), tg[:, g:g + 1], None, ALU.mult).then_inc(gates, 1)
                loaded(dve, "kern")
                dve.tensor_reduce(kscale[:, 0:1], kern[:, :, :], AX.XY, ALU.max,
                                  apply_absolute_value=True).then_inc(maxed, 1)
                dve.wait_ge(absmax, 1)
                dve.tensor_scalar(kscale[:, 2:3], kscale[:, 1:2], 1.0 / 7.0, None, ALU.mult).then_inc(scaled, 1)
                dve.wait_ge(scaled, 1)
                dve.reciprocal(kscale[:, 3:4], kscale[:, 2:3]).then_inc(scaled, 1)
                dve.wait_ge(scaled, 2)
                dve.tensor_scalar(wq8[:, :, :], kern[:, :, :], kscale[:, 3:4], None, ALU.mult).then_inc(scaled, 1)
                dve.wait_ge(scaled, 3)
                magic = 1.5 * 2.0 ** 23
                dve.tensor_scalar(wq8[:, :, :], wq8[:, :, :], magic, None, ALU.add).then_inc(rounded, 1)
                dve.wait_ge(rounded, 1)
                dve.tensor_scalar(wq8[:, :, :], wq8[:, :, :], magic, None, ALU.subtract).then_inc(rounded, 1)
                dve.wait_ge(rounded, 2)
                dve.tensor_scalar(wq8[:, :, :], wq8[:, :, :], -8.0, 7.0, ALU.max, ALU.min).then_inc(rounded, 1)
                dve.wait_ge(rounded, 3)
                dve.tensor_scalar(wq8[:, :, :], wq8[:, :, :], kscale[:, 2:3], None, ALU.mult).then_inc(rounded, 1)
            quant_tmp.close()

        def tiles_of(c):
            return range(c * TB, (c + 1) * TB)

        def tok(t):
            return slice(t * P, (t + 1) * P)

        def blk(c):
            return slice(c * BLK, (c + 1) * BLK)

        def norm_stage(name, bias_row=None, double=False):
            with stage(name, 10) as (block, (stated, varied, added, powed, normed, turned, evac,
                                             biased, s2, s3)), ExitStack() as tmp:
                st = sb("st", [P, T, 6], stack=tmp)
                mv = sb("mv", [P, T, 2], stack=tmp)
                rs = sb("rs", [P, 2, T], stack=tmp)
                rounds = 2 if double else 1

                @block.vector
                def _(dve):
                    for r in range(rounds):
                        src = x if r == 0 else xn
                        if r:
                            dve.wait_ge(normed, T * r)
                        for t in range(T):
                            dve.bn_stats(st[:, t, :], src[:, t, :]).then_inc(stated, 1)
                        for t in range(T):
                            dve.wait_ge(stated, T * r + t + 1)
                            dve.bn_aggr(mv[:, t, :], st[:, t, :]).then_inc(varied, 1)
                        dve.wait_ge(powed, r + 1)
                        for t in range(T):
                            dve.tensor_scalar(xn[:, t, :], src[:, t, :], mv[:, t, 0:1], rs[:, 1, t:t + 1],
                                              ALU.subtract, ALU.mult).then_inc(normed, 1)

                @block.gpsimd
                def _(pool):
                    for r in range(rounds):
                        pool.wait_ge(varied, T * (r + 1))
                        pool.tensor_scalar(rs[:, 0, :], mv[:, :, 1], EPS, None, ALU.add).then_inc(added, 1)
                        pool.wait_ge(added, r + 1)
                        pool.tensor_tensor(rs[:, 1, :], rs[:, 0, :], neg_half[:, 0:T], ALU.pow).then_inc(powed, 1)
                    if bias_row is not None:
                        pool.wait_ge(normed, T)
                        for t in range(T):
                            pool.tensor_tensor(x[:, t, :], x[:, t, :], row(bias_row),
                                               ALU.add).then_inc(biased, 1)

                @block.tensor
                def _(pe):
                    for c in range(NB):
                        for t in tiles_of(c):
                            pe.wait_ge(normed, T * (rounds - 1) + t + 1)
                            for k in range(DK):
                                pe.transpose(bank(DK * c + k)[:, tok(t % TB)], xn[:, t, tok(k)],
                                             ident[:, :]).then_inc(turned, 1)

                @block.scalar
                def _(act):
                    for c in range(NB):
                        act.wait_ge(turned, DK * TB * (c + 1))
                        for k in range(DK):
                            if double:
                                act.activation(xT[:, k, blk(c)], bank(DK * c + k), ACT.Identity,
                                               bias=col("ln_l_b", k), scale=col("ln_l_g", k)).then_inc(evac, 1)
                            else:
                                act.activation(xT[:, k, blk(c)], bank(DK * c + k), ACT.Copy).then_inc(evac, 1)

        def project_stage(name, o_tok, w, group, chunks, gate, c0=0, count=T):
            with stage(name, 4) as (block, (turned, evac, summed, updated)), ExitStack() as tmp:
                oT = sb("oT", [P, 2, chunks, P], stack=tmp)
                per = (chunks + 3) // 4

                @block.tensor
                def _(pe):
                    loaded(pe, group)

                    def turn_tile(t):
                        if t >= 2:
                            pe.wait_ge(evac, per * (t - 1))
                        for k in range(chunks):
                            pe.transpose(bank(per * (t % 2) + k // 4)[:, tok(k % 4)], o_tok[:, t, tok(k)],
                                         ident[:, :]).then_inc(turned, 1)
                    turn_tile(0)
                    for t in range(count):
                        if t + 1 < count:
                            turn_tile(t + 1)
                        pe.wait_ge(evac, per * (t + 1))
                        if t >= 2:
                            pe.wait_ge(updated, t - 1)
                        for k in range(chunks):
                            mm = pe.matmul(bank(6 + t % 2, D), oT[:, t % 2, k, :], w[:, k, :],
                                           start=(k == 0), stop=(k == chunks - 1))
                        mm.then_inc(summed, 1)

                @block.scalar
                def _(act):
                    for t in range(count):
                        act.wait_ge(turned, chunks * (t + 1))
                        if t >= 2:
                            act.wait_ge(summed, t - 1)
                        for i in range(per):
                            n = min(4, chunks - 4 * i)
                            act.activation(oT[:, t % 2, 4 * i:4 * i + n, :],
                                           bank(per * (t % 2) + i, n * P).rearrange("p (k q) -> p k q", q=P),
                                           ACT.Copy).then_inc(evac, 1)

                @block.vector
                def _(dve):
                    for t in range(count):
                        dve.wait_ge(summed, t + 1)
                        dve.scalar_tensor_tensor(out=x[:, c0 + t, :], in0=bank(6 + t % 2, D), scalar=tg[:, gate:gate + 1],
                                                 in1=x[:, c0 + t, :], op0=ALU.mult, op1=ALU.add).then_inc(updated, 1)

        def load_stage(b):
            with stage("load", 11) as (block, (xs, cs, ms, stated, added, powed, normed, masked, turned,
                                               evac, rep)), ExitStack() as tmp:
                c_tok = sb("c_tok", [M, C], stack=tmp)
                c_nrm = sb("c_nrm", [M, C], stack=tmp)
                st = sb("cst", [M, 6], stack=tmp)
                mv = sb("cmv", [M, 2], stack=tmp)
                rs = sb("crs", [M, 2], stack=tmp)
                col_u8 = sb("col_u8", [M, 1], U8, stack=tmp)
                row_u8 = sb("row_u8", [1, M], U8, stack=tmp)

                @block.sync
                def _(sp):
                    sp.dma_start(c_tok[:, :], a["ctx_768"][bass.ds(b, 1), :, :].rearrange("o m c -> (o m) c")
                                 ).then_inc(cs, 16)
                    sp.dma_start(col_u8[:, :], a["mask"][bass.ds(b, 1), :].rearrange("o m -> m o")
                                 ).then_inc(ms, 16)
                    sp.dma_start(row_u8[:, :], a["mask"][bass.ds(b, 1), :]).then_inc(ms, 16)
                    sp.dma_start(x[:, :, :], a["x"][bass.ds(b, 1), :, :].rearrange("o (t p) d -> p (o t) d", p=P)
                                 ).then_inc(xs, 16)
                    sp.wait_ge(xs, 16)

                @block.vector
                def _(dve):
                    dve.wait_ge(cs, 16)
                    dve.bn_stats(st[:, :], c_tok[:, :]).then_inc(stated, 1)
                    dve.wait_ge(stated, 1)
                    dve.bn_aggr(mv[:, :], st[:, :]).then_inc(stated, 1)
                    dve.wait_ge(powed, 1)
                    dve.tensor_scalar(c_nrm[:, :], c_tok[:, :], mv[:, 0:1], rs[:, 1:2], ALU.subtract,
                                      ALU.mult).then_inc(normed, 1)
                    dve.wait_ge(ms, 32)
                    dve.tensor_scalar(mask_col[:, :], col_u8[:, :], 1.0, LOW, ALU.subtract,
                                      ALU.mult).then_inc(masked, 1)
                    dve.tensor_scalar(mask_row[:, :], row_u8[:, :], 1.0, LOW, ALU.subtract,
                                      ALU.mult).then_inc(masked, 1)
                    dve.wait_ge(evac, 2)
                    dve.tensor_copy(ctx_rep[:, 0, :].rearrange("p (h m) -> p h m", m=M),
                                    ctxT[:, 0, :].unsqueeze(1).to_broadcast([P, HG, M])).then_inc(rep, 1)
                    dve.tensor_copy(ctx_rep[0:C1 + 1, 1, :].rearrange("p (h m) -> p h m", m=M),
                                    ctxT[0:C1 + 1, 1, :].unsqueeze(1).to_broadcast([C1 + 1, HG, M])
                                    ).then_inc(rep, 1)

                @block.gpsimd
                def _(pool):
                    pool.wait_ge(stated, 2)
                    pool.tensor_scalar(rs[:, 0:1], mv[:, 1:2], EPS, None, ALU.add).then_inc(added, 1)
                    pool.wait_ge(added, 1)
                    pool.tensor_tensor(rs[:, 1:2], rs[:, 0:1], neg_half[0:M, 0:1], ALU.pow).then_inc(powed, 1)

                @block.tensor
                def _(pe):
                    pe.wait_ge(cs, 16)
                    pe.transpose(bank(0, M), c_tok[:, 0:P], ident[0:M, 0:M])
                    pe.transpose(bank(1, M)[0:C1, :], c_tok[:, P:C], ident[0:M, 0:M]).then_inc(turned, 1)
                    pe.wait_ge(normed, 1)
                    pe.transpose(bank(2, M), c_nrm[:, 0:P], ident[0:M, 0:M])
                    pe.transpose(bank(3, M)[0:C1, :], c_nrm[:, P:C], ident[0:M, 0:M]).then_inc(turned, 1)

                @block.scalar
                def _(act):
                    act.wait_ge(turned, 1)
                    act.activation(ctxT[:, 0, :], bank(0, M), ACT.Copy).then_inc(evac, 1)
                    act.activation(ctxT[0:C1, 1, :], bank(1, M)[0:C1, :], ACT.Copy).then_inc(evac, 1)
                    act.wait_ge(turned, 2)
                    act.activation(cnT[:, 0, :], bank(2, M), ACT.Identity, bias=col("ln_x_b", 0),
                                   scale=col("ln_x_g", 0)).then_inc(evac, 1)
                    act.activation(cnT[0:C1, 1, :], bank(3, M)[0:C1, :], ACT.Identity,
                                   bias=col("ln_x_b", 1)[0:C1, :], scale=col("ln_x_g", 1)[0:C1, :]).then_inc(evac, 1)

        NK0 = T + 1
        KEYS0 = S + M

        def key_rows(j):
            return P if j < T else M

        def qkv0_stage(qT, kT, qTb, kTb, v_aug):
            with stage("qkv0", 10) as (block, (qk_done, v_done, squared, summed, floored, powed, normed, turned,
                                               evac, v_evac)), ExitStack() as tmp:
                sq = sb("sq", [P, 2, 2 * D], stack=tmp)
                ss = sb("ss", [P, NK0, 2 * H0], stack=tmp)
                fl = sb("fl", [P, NK0, 2 * H0], stack=tmp)
                ri = sb("ri", [P, NK0, 2 * H0], stack=tmp)
                qk = sb("qk", [P, 2, 2 * D], stack=tmp)

                @block.tensor
                def _(pe):
                    loaded(pe, "w0")

                    def turn_tile(j):
                        n = key_rows(j)
                        pe.wait_ge(normed, j + 1)
                        if j >= 2:
                            pe.wait_ge(evac, 2 * (j - 1))
                        first = 0 if j < T else DK
                        for i in range(first, 2 * DK):
                            mm = pe.transpose(bank(4 + j % 2)[:, i * P:i * P + n], qk[0:n, j % 2, tok(i)],
                                              ident[0:n, 0:n])
                        mm.then_inc(turned, 1)
                    for j in range(NK0):
                        n = key_rows(j)
                        if j >= 2:
                            pe.wait_ge(normed, j - 1)
                            pe.wait_ge(squared, j - 1)
                            pe.wait_ge(v_evac, j - 1)
                        if j < T:
                            for k in range(DK):
                                mm = pe.matmul(bank(j % 2), xT[:, k, tok(j)], w0_qkv[:, k, 0:2 * D],
                                               start=(k == 0), stop=(k == DK - 1))
                            mm.then_inc(qk_done, 1)
                            for k in range(DK):
                                mm = pe.matmul(bank(2 + j % 2, D), xT[:, k, tok(j)], w0_qkv[:, k, 2 * D:3 * D],
                                               start=(k == 0), stop=(k == DK - 1))
                            mm.then_inc(v_done, 1)
                        else:
                            for k, r in enumerate((P, C1)):
                                mm = pe.matmul(bank(j % 2)[0:M, D:2 * D], cnT[0:r, k, :], w0_ckv[0:r, k, 0:D],
                                               start=(k == 0), stop=(k == 1))
                            mm.then_inc(qk_done, 1)
                            for k, r in enumerate((P, C1)):
                                mm = pe.matmul(bank(2 + j % 2)[0:M, 0:D], cnT[0:r, k, :], w0_ckv[0:r, k, D:2 * D],
                                               start=(k == 0), stop=(k == 1))
                            mm.then_inc(v_done, 1)
                        if j:
                            turn_tile(j - 1)
                    turn_tile(NK0 - 1)

                @block.scalar
                def _(act):
                    def evacuate(j):
                        act.wait_ge(turned, j + 1)
                        n = key_rows(j)
                        for i in range(2 * DK):
                            src = bank(4 + j % 2)[:, i * P:i * P + n]
                            if i < DK and j < T:
                                act.activation(qT[:, i, tok(j)], src, ACT.Identity,
                                               scale=col("qn_g"), bias=0.0)
                            elif i >= DK:
                                mm = act.activation(kT[:, i - DK, j * P:j * P + n], src, ACT.Identity,
                                                    scale=col("kn_g"), bias=0.0)
                                mm.then_inc(evac, 1)
                    for j in range(NK0):
                        n = key_rows(j)
                        lo = 0 if j < T else D
                        act.wait_ge(qk_done, j + 1)
                        if j >= 2:
                            act.wait_ge(summed, j - 1)
                        act.activation(sq[0:n, j % 2, lo:], bank(j % 2)[0:n, lo:], ACT.Square).then_inc(squared, 1)
                        act.wait_ge(v_done, j + 1)
                        act.activation(v_aug[0:n, j, :, 0:DH0],
                                       bank(2 + j % 2, D)[0:n, :].rearrange("p (h d) -> p h d", d=DH0),
                                       ACT.Copy).then_inc(v_evac, 1)
                        if j:
                            evacuate(j - 1)
                    evacuate(NK0 - 1)

                @block.vector
                def _(dve):
                    dve.memset(v_aug[:, :, :, DH0:DH0 + 1], 1.0)
                    for j in range(NK0):
                        n = key_rows(j)
                        h = 0 if j < T else H0
                        dve.wait_ge(squared, j + 1)
                        dve.tensor_reduce(ss[0:n, j, h:], sq[0:n, j % 2, h * DH0:].rearrange("p (h d) -> p h d", d=DH0),
                                          AX.X, ALU.add).then_inc(summed, 1)
                        dve.wait_ge(powed, j + 1)
                        if j >= 2:
                            dve.wait_ge(turned, j - 1)
                        dve.tensor_tensor(qk[0:n, j % 2, h * DH0:].rearrange("p (h d) -> p h d", d=DH0),
                                          bank(j % 2)[0:n, h * DH0:].rearrange("p (h d) -> p h d", d=DH0),
                                          ri[0:n, j, h:].unsqueeze(2).to_broadcast([n, 2 * H0 - h, DH0]),
                                          ALU.mult).then_inc(normed, 1)

                @block.gpsimd
                def _(pool):
                    for j in range(NK0):
                        n = key_rows(j)
                        h = 0 if j < T else H0
                        pool.wait_ge(summed, j + 1)
                        pool.tensor_scalar(fl[0:n, j, h:], ss[0:n, j, h:], 1.0 / DH0, 1e-16, ALU.mult,
                                           ALU.max).then_inc(floored, 1)
                        pool.wait_ge(floored, j + 1)
                        pool.tensor_tensor(ri[0:n, j, h:], fl[0:n, j, h:], neg_half[0:n, h:2 * H0],
                                           ALU.pow).then_inc(powed, 1)
                    pool.wait_ge(evac, 2 * NK0)
                    for k in range(DK):
                        pool.tensor_copy(qTb[:, k, :], qT[:, k, :])
                        pool.tensor_copy(kTb[:, k, 0:KEYS0], kT[:, k, 0:KEYS0])

        def attend0_stage(qT, kT, qTb, kTb, v_aug, o_tok):
            with stage("attend0", 9) as (block, (scored, maxed, turned, shifted, sdone, edone, pv, ok,
                                                 recd)), ExitStack() as tmp:
                mx = sb("mx", [P, T, H0], stack=tmp)
                shift = sb("shift", [H0, NB, BLK], BF16, stack=tmp)
                NPT = 4
                pt = sb("pt", [P, NPT, BLK], stack=tmp)
                rc = sb("rc", [P, 2, TB], stack=tmp)

                def head(h):
                    return slice(DH0 * (h % 2), DH0 * (h % 2) + DH0), h // 2
                N = H0 * NK0

                @block.tensor
                def _(pe):
                    def score_max(t, h):
                        r, k = head(h)
                        n = H0 * t + h
                        if n:
                            pe.wait_ge(maxed, n)
                        for lo in range(0, KEYS0, 512):
                            w = min(512, KEYS0 - lo)
                            mm = pe.matmul(psum[:, lo:lo + w], qTb[r, k, tok(t)], kTb[r, k, lo:lo + w],
                                           start=True, stop=(w == 512))
                        mm = pe.matmul(psum[:, S:S + M], ones_bf[0:1, :], mask_row[0:1, :],
                                       start=False, stop=True)
                        mm.then_inc(scored, 1)

                    def turn_max(c):
                        pe.wait_ge(maxed, H0 * TB * (c + 1))
                        for t in tiles_of(c):
                            mm = pe.transpose(bank(3, BLK)[0:H0, tok(t % TB)], mx[:, t, :], ident[:, :])
                        mm.then_inc(turned, 1)

                    def scores(c, i):
                        h, j = divmod(i, NK0)
                        r, k = head(h)
                        n = c * N + i
                        w = key_rows(j)
                        if i == 0:
                            pe.wait_ge(shifted, c + 1)
                        if n >= 3:
                            pe.wait_ge(edone, n - 2)
                        pe.matmul(bank(3 + n % 3)[0:w, :], kT[r, k, j * P:j * P + w], qT[r, k, blk(c)],
                                  start=True, stop=False)
                        pe.matmul(bank(3 + n % 3)[0:w, :], pick0[:, h, 0:w], shift[:, c, :],
                                  start=False, stop=True).then_inc(sdone, 1)

                    def values(c, i):
                        h, j = divmod(i, NK0)
                        n = c * N + i
                        w = key_rows(j)
                        pe.wait_ge(edone, n + 1)
                        g = c * H0 + h
                        if j == 0 and g >= 2:
                            pe.wait_ge(ok, g - 1)
                        for q in range(TB):
                            mm = pe.matmul(bank(6 + g % 2)[:, q * (DH0 + 1):(q + 1) * (DH0 + 1)],
                                           pt[0:w, n % NPT, tok(q)], v_aug[0:w, j, h, :],
                                           start=(j == 0 and q == 0), stop=(j == NK0 - 1), skip_group_check=True)
                        mm.then_inc(pv, 1)
                    for t in tiles_of(0):
                        for h in range(H0):
                            score_max(t, h)
                    turn_max(0)
                    ahead = [(t, h) for t in tiles_of(1) for h in range(H0)]
                    for c in range(NB):
                        for i in range(N + 2):
                            if i < N:
                                scores(c, i)
                            if i >= 2:
                                values(c, i - 2)
                            if c == 0 and i % 2 == 0 and ahead:
                                score_max(*ahead.pop(0))
                        if c == 0:
                            pe.wait_ge(edone, N)
                            turn_max(1)

                @block.scalar
                def _(act):
                    for c in range(NB):
                        for i in range(N):
                            h, j = divmod(i, NK0)
                            n = c * N + i
                            w = key_rows(j)
                            act.wait_ge(sdone, n + 1)
                            if n >= NPT:
                                act.wait_ge(pv, n - NPT + 1)
                            act.activation(pt[0:w, n % NPT, :], bank(3 + n % 3)[0:w, :], ACT.Exp,
                                           scale=float(DH0) ** -0.5,
                                           bias=(mask_col[:, 0:1] if j == T else 0.0)).then_inc(edone, 1)

                @block.vector
                def _(dve):
                    def largest(t, h):
                        dve.wait_ge(scored, H0 * t + h + 1)
                        dve.tensor_reduce(mx[:, t, h:h + 1], psum[:, 0:KEYS0], AX.X, ALU.max).then_inc(maxed, 1)

                    def shift_rows(c):
                        dve.wait_ge(turned, c + 1)
                        dve.tensor_scalar(shift[:, c, :], bank(3)[0:H0, :], -1.0, None, ALU.mult).then_inc(shifted, 1)

                    def outputs(c, h):
                        g = c * H0 + h
                        dve.wait_ge(pv, NK0 * (g + 1))
                        o = bank(6 + g % 2, TB * (DH0 + 1)).rearrange("p (q d) -> p q d", d=DH0 + 1)
                        dve.reciprocal(rc[:, g % 2, :].unsqueeze(2), o[:, :, DH0:DH0 + 1]).then_inc(recd, 1)
                        dve.wait_ge(recd, g + 1)
                        dve.tensor_tensor(o_tok[:, c * TB:(c + 1) * TB, h * DH0:(h + 1) * DH0], o[:, :, 0:DH0],
                                          rc[:, g % 2, :].unsqueeze(2).to_broadcast([P, TB, DH0]),
                                          ALU.mult).then_inc(ok, 1)
                    for t in tiles_of(0):
                        for h in range(H0):
                            largest(t, h)
                    shift_rows(0)
                    ahead = [(t, h) for t in tiles_of(1) for h in range(H0)]
                    for h in range(H0):
                        for _ in range(5 if ahead else 0):
                            if ahead:
                                largest(*ahead.pop(0))
                        outputs(0, h)
                    shift_rows(1)
                    for h in range(H0):
                        outputs(1, h)

        def first_largest(chain, dve, value, onehot, best, order):
            def over(v):
                return v.unsqueeze(2).to_broadcast([P, T, E])
            chain(dve.tensor_reduce(best, value, AX.X, ALU.max))
            chain(dve.tensor_tensor(onehot, value, over(best), ALU.is_equal))
            chain(dve.tensor_tensor(onehot, onehot, rank[:, :, :], ALU.mult))
            chain(dve.tensor_reduce(order, onehot, AX.X, ALU.max))
            chain(dve.tensor_tensor(onehot, onehot, over(order), ALU.is_equal))

        def over(v):
            return v.unsqueeze(2).to_broadcast([P, T, E])

        def chained(dve, step):
            count = [0]

            def chain(op):
                count[0] += 1
                op.then_inc(step, 1)
                dve.wait_ge(step, count[0])
                return count[0]
            return chain

        def moe0_stage():
            with stage("moe0", 10) as (block, (logged, centred, exped, step, weighted, turned, wt_ready,
                                               mm_done, added, bias_done)), ExitStack() as tmp:
                lg = sb("lg", [P, T, E], stack=tmp)
                ex = sb("ex", [P, T, E], stack=tmp)
                onehot = sb("onehot", [P, T, E], stack=tmp)
                wt = sb("wt", [P, T, E], stack=tmp)
                s1 = sb("s1", [P, 5, T], stack=tmp)
                wT = sb("wT", [E, T, P], stack=tmp)
                PAIRS = E // 2
                NBK = 5

                @block.tensor
                def _(pe):
                    loaded(pe, "e0")
                    for t in range(T):
                        for k in range(DK):
                            mm = pe.matmul(bank(6)[:, E * t:E * (t + 1)], xT[:, k, tok(t)], r0[:, k, :],
                                           start=(k == 0), stop=(k == DK - 1))
                    mm.then_inc(logged, 1)
                    for t in range(T):
                        for p in range(PAIRS):
                            n = t * PAIRS + p
                            if n >= NBK:
                                pe.wait_ge(added, 2 * (n - NBK + 1))
                            for k in range(DK):
                                mm = pe.matmul(bank(n % NBK), xT[:, k, tok(t)], e0[:, k, 512 * p:512 * (p + 1)],
                                               start=(k == 0), stop=(k == DK - 1))
                            mm.then_inc(mm_done, 1)
                        if t == 0:
                            pe.wait_ge(weighted, 1)
                            for u in range(T):
                                mm = pe.transpose(bank(5 if u < TB else 7)[0:E, tok(u % TB)], wt[:, u, :],
                                                  ident[:, :])
                            mm.then_inc(turned, 1)
                    pe.wait_ge(wt_ready, 2)
                    for t in range(T):
                        if t >= 2:
                            pe.wait_ge(added, 2 * T * PAIRS + t - 1)
                        pe.matmul(bank(5 + t % 2, D), wT[:, t, :], e0_b[:, :], start=True,
                                  stop=True).then_inc(bias_done, 1)

                @block.scalar
                def _(act):
                    act.wait_ge(centred, 1)
                    act.activation(ex[:, :, :], lg[:, :, :], ACT.Exp).then_inc(exped, 1)
                    act.wait_ge(turned, 1)
                    act.activation(wT[:, 0:TB, :], bank(5)[0:E, :].rearrange("p (t q) -> p t q", q=P),
                                   ACT.Copy).then_inc(wt_ready, 1)
                    act.activation(wT[:, TB:T, :], bank(7)[0:E, :].rearrange("p (t q) -> p t q", q=P),
                                   ACT.Copy).then_inc(wt_ready, 1)

                @block.vector
                def _(dve):
                    chain = chained(dve, step)
                    total, inverse, best, order, gate = (s1[:, i, :] for i in range(5))
                    dve.wait_ge(logged, 1)
                    chain(dve.tensor_tensor(lg[:, :, :], bank(6, T * E).rearrange("p (t e) -> p t e", e=E),
                                            cols[:, COLS["rb0"]:COLS["rb0"] + E].unsqueeze(1).to_broadcast([P, T, E]),
                                            ALU.add))
                    chain(dve.tensor_reduce(total, lg[:, :, :], AX.X, ALU.max))
                    dve.tensor_tensor(lg[:, :, :], lg[:, :, :], over(total), ALU.subtract).then_inc(centred, 1)
                    dve.wait_ge(exped, 1)
                    chain(dve.tensor_reduce(total, ex[:, :, :], AX.X, ALU.add))
                    chain(dve.reciprocal(inverse, total))
                    first_largest(chain, dve, ex[:, :, :], onehot[:, :, :], best, order)
                    chain(dve.tensor_tensor(gate, inverse, best, ALU.mult))
                    chain(dve.tensor_scalar(gate, gate, tg[:, 4:5], None, ALU.mult))
                    dve.tensor_tensor(wt[:, :, :], onehot[:, :, :], over(gate), ALU.mult).then_inc(weighted, 1)
                    dve.wait_ge(weighted, 1)
                    for t in range(T):
                        for e in range(E):
                            n = t * E + e
                            dve.wait_ge(mm_done, n // 2 + 1)
                            if e:
                                dve.wait_ge(added, n)
                            dve.scalar_tensor_tensor(out=x[:, t, :], in0=bank(n // 2 % NBK)[:, e % 2 * D:(e % 2 + 1) * D],
                                                     scalar=wt[:, t, e:e + 1], in1=x[:, t, :],
                                                     op0=ALU.mult, op1=ALU.add).then_inc(added, 1)
                    dve.wait_ge(added, T * E)
                    for t in range(T):
                        dve.wait_ge(bias_done, t + 1)
                        dve.tensor_tensor(x[:, t, :], bank(5 + t % 2, D), x[:, t, :], ALU.add).then_inc(added, 1)

        def moe1_stage():
            with stage("moe1", 12) as (block, (logged, centred, exped, step, weighted, up_done, silued, gated_h,
                                               turned, evac, down, updated)), ExitStack() as tmp:
                lg = sb("lg", [P, T, E], stack=tmp)
                ex = sb("ex", [P, T, E], stack=tmp)
                one1 = sb("one1", [P, T, E], stack=tmp)
                one2 = sb("one2", [P, T, E], stack=tmp)
                wt = sb("wt", [P, T, E], stack=tmp)
                s1 = sb("s1", [P, 5, T], stack=tmp)
                sl = sb("sl", [P, 2, 2, P], stack=tmp)
                gh = sb("gh", [P, 2, 2, P], stack=tmp)
                gT = sb("gT", [P, 2, 2, P], stack=tmp)
                PAIRS = E // 2
                N = T * PAIRS

                @block.tensor
                def _(pe):
                    loaded(pe, "e1")
                    for t in range(T):
                        for k in range(DK):
                            mm = pe.matmul(bank(7)[:, E * t:E * (t + 1)], xT[:, k, tok(t)], r1[:, k, :],
                                           start=(k == 0), stop=(k == DK - 1))
                    mm.then_inc(logged, 1)

                    def up(n):
                        t, p = divmod(n, PAIRS)
                        if n >= 3:
                            pe.wait_ge(gated_h, n - 2)
                        for k in range(DK):
                            mm = pe.matmul(bank(n % 3), xT[:, k, tok(t)], e1_up[:, k, 512 * p:512 * (p + 1)],
                                           start=(k == 0), stop=(k == DK - 1))
                        mm.then_inc(up_done, 1)

                    def turn_pair(n):
                        pe.wait_ge(gated_h, n + 1)
                        if n >= 2:
                            pe.wait_ge(evac, n - 1)
                        for i in range(2):
                            mm = pe.transpose(bank(3 + n % 2)[:, tok(i)], gh[:, n % 2, i, :], ident[:, :])
                        mm.then_inc(turned, 1)

                    def down_pair(n):
                        t, p = divmod(n, PAIRS)
                        pe.wait_ge(evac, n + 1)
                        if p == 0 and t >= 2:
                            pe.wait_ge(updated, t - 1)
                        for i in range(2):
                            mm = pe.matmul(bank(5 + t % 2, D), gT[:, n % 2, i, :], e1_down[:, 2 * p + i, :],
                                           start=(p == 0 and i == 0), stop=(p == PAIRS - 1 and i == 1))
                        mm.then_inc(down, 1)
                    for n in range(N + 3):
                        if n < N:
                            up(n)
                        if 2 <= n < N + 2:
                            turn_pair(n - 2)
                        if n >= 3:
                            down_pair(n - 3)

                @block.scalar
                def _(act):
                    act.wait_ge(centred, 1)
                    act.activation(ex[:, :, :], lg[:, :, :], ACT.Exp).then_inc(exped, 1)
                    act.wait_ge(weighted, 1)

                    def evacuate(n):
                        act.wait_ge(turned, n + 1)
                        if n >= 2:
                            act.wait_ge(down, n - 1)
                        act.activation(gT[:, n % 2, :, :], bank(3 + n % 2, D).rearrange("p (i q) -> p i q", q=P),
                                       ACT.Copy).then_inc(evac, 1)
                    for n in range(N + 2):
                        if n < N:
                            t, p = divmod(n, PAIRS)
                            act.wait_ge(up_done, n + 1)
                            if n >= 2:
                                act.wait_ge(gated_h, n - 1)
                            for i in range(2):
                                e = 2 * p + i
                                act.activation(sl[:, n % 2, i, :], bank(n % 3)[:, i * D:i * D + P], ACT.Silu,
                                               scale=wt[:, t, e:e + 1]).then_inc(silued, 1)
                        if n >= 2:
                            evacuate(n - 2)

                @block.vector
                def _(dve):
                    chain = chained(dve, step)
                    total, inverse, best, order, gate = (s1[:, i, :] for i in range(5))
                    dve.wait_ge(logged, 1)
                    chain(dve.tensor_copy(lg[:, :, :], bank(7, T * E).rearrange("p (t e) -> p t e", e=E)))
                    chain(dve.tensor_reduce(total, lg[:, :, :], AX.X, ALU.max))
                    dve.tensor_tensor(lg[:, :, :], lg[:, :, :], over(total), ALU.subtract).then_inc(centred, 1)
                    dve.wait_ge(exped, 1)
                    chain(dve.tensor_reduce(total, ex[:, :, :], AX.X, ALU.add))
                    chain(dve.reciprocal(inverse, total))
                    first_largest(chain, dve, ex[:, :, :], one1[:, :, :], best, order)
                    chain(dve.scalar_tensor_tensor(out=lg[:, :, :], in0=one1[:, :, :], scalar=-4.0,
                                                   in1=ex[:, :, :], op0=ALU.mult, op1=ALU.add))
                    first_largest(chain, dve, lg[:, :, :], one2[:, :, :], best, order)
                    chain(dve.tensor_tensor(one1[:, :, :], one1[:, :, :], one2[:, :, :], ALU.add))
                    chain(dve.tensor_tensor(one1[:, :, :], one1[:, :, :], ex[:, :, :], ALU.mult))
                    dve.tensor_tensor(wt[:, :, :], one1[:, :, :], over(inverse), ALU.mult).then_inc(weighted, 1)
                    dve.wait_ge(weighted, 1)

                    def update(t):
                        dve.wait_ge(down, PAIRS * (t + 1))
                        dve.scalar_tensor_tensor(out=x[:, t, :], in0=bank(5 + t % 2, D), scalar=tg[:, 5:6],
                                                 in1=x[:, t, :], op0=ALU.mult, op1=ALU.add).then_inc(updated, 1)
                    for n in range(N):
                        t, p = divmod(n, PAIRS)
                        dve.wait_ge(silued, 2 * (n + 1))
                        if n >= 2:
                            dve.wait_ge(turned, n - 1)
                        for i in range(2):
                            e = 2 * p + i
                            op = dve.scalar_tensor_tensor(out=gh[:, n % 2, i, :],
                                                          in0=bank(n % 3)[:, i * D + P:(i + 1) * D],
                                                          scalar=wt[:, t, e:e + 1], in1=sl[:, n % 2, i, :],
                                                          op0=ALU.mult, op1=ALU.mult)
                        op.then_inc(gated_h, 1)
                        if n >= PAIRS + 2 and n % PAIRS == 2:
                            update(t - 1)
                    update(T - 1)

        VW = HG * (DH1 + 1)

        def small_prepare_stage(name, group, wq, wk, wv, bq, qT, qTb, kbd, kbdb, vbig):
            with stage(name, 7) as (block, (q_done, q_evac, k_done, k_evac, v_done, v_evac, ones_done)), \
                    ExitStack() as tmp:
                @block.tensor
                def _(pe):
                    loaded(pe, group)
                    for g in range(G):
                        for kc, r in enumerate((P, C1 + 1)):
                            mm = pe.matmul(bank(6 + g, M), wk[0:r, kc, tok(g)], ctxT[0:r, kc, :],
                                           start=(kc == 0), stop=(kc == 1))
                        mm.then_inc(k_done, 1)
                    for i in range(G * NB):
                        g, c = divmod(i, NB)
                        if i >= 2:
                            pe.wait_ge(q_evac, i - 1)
                        for k in range(DK):
                            mm = pe.matmul(bank(i % 2), wq[:, k, tok(g)], xT[:, k, blk(c)],
                                           start=(k == 0), stop=(k == DK - 1))
                        mm.then_inc(q_done, 1)
                    for ch, (lo, w) in enumerate(CH):
                        if ch >= 2:
                            pe.wait_ge(v_evac, ch - 1)
                        for kc, r in enumerate((P, C1 + 1)):
                            mm = pe.matmul(bank(2 + ch % 2)[0:w, 0:D], ctx_rep[0:r, kc, lo:lo + w], wv[0:r, kc, :],
                                           start=(kc == 0), stop=(kc == 1))
                        mm.then_inc(v_done, 1)

                @block.scalar
                def _(act):
                    for i in range(G * NB):
                        g, c = divmod(i, NB)
                        act.wait_ge(q_done, i + 1)
                        act.activation(qT[:, g, blk(c)], bank(i % 2), ACT.Identity,
                                       bias=col(bq, g)).then_inc(q_evac, 1)

                @block.vector
                def _(dve):
                    for g in range(G):
                        dve.wait_ge(k_done, g + 1)
                        dve.tensor_tensor(kbd[:, g, :].rearrange("p (h m) -> p h m", m=M),
                                          bank(6 + g, M).unsqueeze(1).to_broadcast([P, HG, M]),
                                          head_of_feature[:, :].unsqueeze(2).to_broadcast([P, HG, M]),
                                          ALU.mult).then_inc(k_evac, 1)
                    for ch, (lo, w) in enumerate(CH):
                        dve.wait_ge(v_done, ch + 1)
                        v = vbig[0:w, ch, :, :].rearrange("p g (h d) -> p g h d", d=DH1 + 1)
                        for g in range(G):
                            op = dve.tensor_tensor(v[:, g, :, 0:DH1],
                                                   bank(2 + ch % 2)[0:w, g * P:(g + 1) * P].rearrange(
                                                       "p (h d) -> p h d", d=DH1),
                                                   head_of_row[0:w, ch, :].unsqueeze(2).to_broadcast([w, HG, DH1]),
                                                   ALU.mult)
                        op.then_inc(v_evac, 1)
                    dve.wait_ge(k_evac, G)
                    for g in range(G):
                        dve.tensor_copy(kbdb[:, g, :], kbd[:, g, :])

                @block.gpsimd
                def _(pool):
                    for g in range(G):
                        pool.tensor_copy(vbig[:, :, g, DH1::DH1 + 1], head_of_row[:, :, :])
                    for i in range(G * NB):
                        g, c = divmod(i, NB)
                        pool.wait_ge(q_evac, i + 1)
                        pool.tensor_copy(qTb[:, g, blk(c)], qT[:, g, blk(c)])

        def small_shift_stage(name, qTb, kbdb, shift, clip):
            with stage(name, 5) as (block, (scored, maxed, capped, turned, shifted)), ExitStack() as tmp:
                mx = sb("mx", [P, T, H1], stack=tmp)
                HALF = GM // 2

                @block.tensor
                def _(pe):
                    for t in range(T):
                        for g in range(G):
                            n = G * t + g
                            if n >= 3:
                                pe.wait_ge(maxed, n - 2)
                            for i in range(2):
                                mm = pe.matmul(bank(2 * (n % 3) + i, HALF), qTb[:, g, tok(t)],
                                               kbdb[:, g, i * HALF:(i + 1) * HALF], start=True, stop=True)
                            mm.then_inc(scored, 1)
                        if t % TB == TB - 1:
                            c = t // TB
                            pe.wait_ge(capped if clip else maxed, c + 1 if clip else G * (t + 1))
                            for u in tiles_of(c):
                                mm = pe.transpose(bank(6 + c)[0:H1, tok(u % TB)], mx[:, u, :], ident[:, :])
                            mm.then_inc(turned, 1)

                @block.vector
                def _(dve):
                    for t in range(T):
                        for g in range(G):
                            n = G * t + g
                            dve.wait_ge(scored, n + 1)
                            r = psum[:, 1024 * (n % 3):1024 * (n % 3) + 1024].rearrange("p (i z) -> p i z", i=2)
                            dve.tensor_reduce(mx[:, t, HG * g:HG * (g + 1)].rearrange("p (i h) -> p i h", i=2),
                                              r[:, :, 0:HALF].rearrange("p i (h m) -> p i h m", m=M),
                                              AX.X, ALU.max).then_inc(maxed, 1)
                        if clip and t % TB == TB - 1:
                            bound = CLAMP * float(DH1) ** 0.5
                            now = mx[:, t - TB + 1:t + 1, :]
                            dve.wait_ge(maxed, G * (t + 1))
                            dve.tensor_scalar(now, now, bound, -bound, ALU.min, ALU.max).then_inc(capped, 1)

                @block.scalar
                def _(act):
                    for c in range(NB):
                        act.wait_ge(turned, c + 1)
                        act.activation(shift[:, blk(c)], bank(6 + c)[0:H1, :], ACT.Copy,
                                       scale=-1.0).then_inc(shifted, 1)

        def small_attend_stage(name, qT, kbd, vbig, shift, o_tok):
            with stage(name, 5) as (block, (sdone, edone, pv, recd, ok)), ExitStack() as tmp:
                NPT = 4
                pt = sb("pt", [P, NPT, BLK], stack=tmp)
                rc = sb("rc", [P, 2, TB, HG], stack=tmp)
                N = G * len(CH)

                def where(n):
                    c, i = divmod(n, N)
                    g, ch = divmod(i, len(CH))
                    return c, g, ch

                @block.tensor
                def _(pe):
                    def scores(n):
                        c, g, ch = where(n)
                        lo, w = CH[ch]
                        if n >= 4:
                            pe.wait_ge(edone, n - 3)
                        pe.matmul(bank(n % 4)[0:w, :], kbd[:, g, lo:lo + w], qT[:, g, blk(c)],
                                  start=True, stop=False)
                        pe.matmul(bank(n % 4)[0:w, :], pick_row[:, g, lo:lo + w], shift[:, blk(c)],
                                  start=False, stop=True).then_inc(sdone, 1)

                    def values(n):
                        c, g, ch = where(n)
                        lo, w = CH[ch]
                        u = c * G + g
                        pe.wait_ge(edone, n + 1)
                        if ch == 0 and u >= 2:
                            pe.wait_ge(ok, u - 1)
                        for q in range(TB):
                            mm = pe.matmul(bank(4 + 2 * (u % 2) + q // 2)[:, VW * (q % 2):VW * (q % 2 + 1)],
                                           pt[0:w, n % NPT, tok(q)], vbig[0:w, ch, g, :],
                                           start=(ch == 0 and q % 2 == 0), stop=(ch == len(CH) - 1),
                                           skip_group_check=True)
                        mm.then_inc(pv, 1)
                    for n in range(NB * N + 2):
                        if n < NB * N:
                            scores(n)
                        if n >= 2:
                            values(n - 2)

                @block.scalar
                def _(act):
                    for n in range(NB * N):
                        c, g, ch = where(n)
                        w = CH[ch][1]
                        act.wait_ge(sdone, n + 1)
                        if n >= NPT:
                            act.wait_ge(pv, n - NPT + 1)
                        act.activation(pt[0:w, n % NPT, :], bank(n % 4)[0:w, :], ACT.Exp,
                                       scale=float(DH1) ** -0.5).then_inc(edone, 1)

                @block.vector
                def _(dve):
                    for u in range(NB * G):
                        c, g = divmod(u, G)
                        dve.wait_ge(pv, len(CH) * (u + 1))
                        for i in range(2):
                            o = bank(4 + 2 * (u % 2) + i, 2 * VW).rearrange("p (q h d) -> p q h d", q=2, d=DH1 + 1)
                            r = rc[:, u % 2, 2 * i:2 * i + 2, :]
                            dve.reciprocal(r.unsqueeze(3), o[:, :, :, DH1:]).then_inc(recd, 1)
                            dve.wait_ge(recd, 2 * u + i + 1)
                            for q in range(2):
                                op = dve.tensor_tensor(
                                    o_tok[:, c * TB + 2 * i + q, g * P:(g + 1) * P].rearrange(
                                        "p (h d) -> p h d", d=DH1),
                                    o[:, q, :, 0:DH1], r[:, q, :].unsqueeze(2).to_broadcast([P, HG, DH1]), ALU.mult)
                        op.then_inc(ok, 1)

        def clipped_attend_stage(name, qT, kbd, vbig, shift, o_tok):
            with stage(name, 7) as (block, (sdone, clipped, shifted, edone, pv, recd, ok)), ExitStack() as tmp:
                NPT = 4
                sc = sb("sc", [P, NPT, BLK], stack=tmp)
                pt = sb("pt", [P, NPT, BLK], stack=tmp)
                rc = sb("rc", [P, 2, TB, HG], stack=tmp)
                N = G * len(CH)
                BOUND = CLAMP * float(DH1) ** 0.5

                def where(n):
                    c, i = divmod(n, N)
                    g, ch = divmod(i, len(CH))
                    return c, g, ch

                @block.tensor
                def _(pe):
                    def scores(n):
                        c, g, ch = where(n)
                        lo, w = CH[ch]
                        if n >= 2:
                            pe.wait_ge(shifted, n - 1)
                        pe.matmul(bank(n % 2)[0:w, :], kbd[:, g, lo:lo + w], qT[:, g, blk(c)],
                                  start=True, stop=True)
                        pe.matmul(bank(2 + n % 2)[0:w, :], pick_row[:, g, lo:lo + w], shift[:, blk(c)],
                                  start=True, stop=True).then_inc(sdone, 1)

                    def values(n):
                        c, g, ch = where(n)
                        lo, w = CH[ch]
                        u = c * G + g
                        pe.wait_ge(edone, n + 1)
                        if ch == 0 and u >= 2:
                            pe.wait_ge(ok, u - 1)
                        for q in range(TB):
                            mm = pe.matmul(bank(4 + 2 * (u % 2) + q // 2)[:, VW * (q % 2):VW * (q % 2 + 1)],
                                           pt[0:w, n % NPT, tok(q)], vbig[0:w, ch, g, :],
                                           start=(ch == 0 and q % 2 == 0), stop=(ch == len(CH) - 1),
                                           skip_group_check=True)
                        mm.then_inc(pv, 1)
                    for n in range(NB * N + 3):
                        if n < NB * N:
                            scores(n)
                        if n >= 3:
                            values(n - 3)

                @block.scalar
                def _(act):
                    for n in range(NB * N):
                        c, g, ch = where(n)
                        w = CH[ch][1]
                        act.wait_ge(shifted, n + 1)
                        if n >= NPT:
                            act.wait_ge(pv, n - NPT + 1)
                        act.activation(pt[0:w, n % NPT, :], sc[0:w, n % NPT, :], ACT.Exp,
                                       scale=float(DH1) ** -0.5).then_inc(edone, 1)

                @block.vector
                def _(dve):
                    def normalise(u):
                        c, g = divmod(u, G)
                        dve.wait_ge(pv, len(CH) * (u + 1))
                        for i in range(2):
                            o = bank(4 + 2 * (u % 2) + i, 2 * VW).rearrange("p (q h d) -> p q h d", q=2, d=DH1 + 1)
                            r = rc[:, u % 2, 2 * i:2 * i + 2, :]
                            dve.reciprocal(r.unsqueeze(3), o[:, :, :, DH1:]).then_inc(recd, 1)
                            dve.wait_ge(recd, 2 * u + i + 1)
                            for q in range(2):
                                op = dve.tensor_tensor(
                                    o_tok[:, c * TB + 2 * i + q, g * P:(g + 1) * P].rearrange(
                                        "p (h d) -> p h d", d=DH1),
                                    o[:, q, :, 0:DH1], r[:, q, :].unsqueeze(2).to_broadcast([P, HG, DH1]), ALU.mult)
                        op.then_inc(ok, 1)
                    total = NB * N

                    def subtract(n):
                        w = CH[where(n)[2]][1]
                        dve.wait_ge(clipped, n + 1)
                        dve.tensor_tensor(sc[0:w, n % NPT, :], sc[0:w, n % NPT, :], bank(2 + n % 2)[0:w, :],
                                          ALU.add).then_inc(shifted, 1)
                    for n in range(total):
                        w = CH[where(n)[2]][1]
                        dve.wait_ge(sdone, n + 1)
                        if n >= NPT:
                            dve.wait_ge(edone, n - NPT + 1)
                        dve.tensor_scalar(sc[0:w, n % NPT, :], bank(n % 2)[0:w, :], BOUND, -BOUND,
                                          ALU.min, ALU.max).then_inc(clipped, 1)
                        if n:
                            subtract(n - 1)
                        if n >= len(CH) + 3 and (n - 3) % len(CH) == 0:
                            normalise((n - 3) // len(CH) - 1)
                    subtract(total - 1)
                    normalise(NB * G - 1)

        KC2 = H2 * DH2 // P

        def kv2_stage(kT, kTb, v_aug):
            with stage("kv2", 4) as (block, (k_done, k_evac, v_done, v_evac)):
                @block.tensor
                def _(pe):
                    loaded(pe, "w2")
                    for j in range(KC2):
                        for kc, r in enumerate((P, C1)):
                            mm = pe.matmul(bank(j // 4)[:, (j % 4) * M:(j % 4 + 1) * M], w2_kv[0:r, kc, tok(j)],
                                           ctxT[0:r, kc, :], start=(kc == 0), stop=(kc == 1))
                    mm.then_inc(k_done, 1)
                    for i in range(2):
                        for kc, r in enumerate((P, C1)):
                            mm = pe.matmul(bank(2 + i)[0:M, :], ctxT[0:r, kc, :],
                                           w2_kv[0:r, kc, H2 * DH2 + 512 * i:H2 * DH2 + 512 * (i + 1)],
                                           start=(kc == 0), stop=(kc == 1))
                        mm.then_inc(v_done, 1)

                @block.scalar
                def _(act):
                    act.wait_ge(k_done, 1)
                    for i in range(2):
                        act.activation(kT[:, 4 * i:4 * i + 4, :], bank(i, 4 * M).rearrange("p (j m) -> p j m", m=M),
                                       ACT.Copy).then_inc(k_evac, 1)

                @block.vector
                def _(dve):
                    dve.memset(v_aug[:, :, DH2:DH2 + 1], 1.0)
                    for i in range(2):
                        dve.wait_ge(v_done, i + 1)
                        dve.tensor_copy(v_aug[:, 8 * i:8 * i + 8, 0:DH2],
                                        bank(2 + i)[0:M, :].rearrange("p (h d) -> p h d", d=DH2)).then_inc(v_evac, 1)

                @block.gpsimd
                def _(pool):
                    pool.wait_ge(k_evac, 2)
                    pool.tensor_copy(kTb[:, :, :], kT[:, :, :])

        def attend2_stage(c, qT, qTb, kT, kTb, v_aug, o_tok):
            with stage("attend2", 12) as (block, (q_done, q_evac, q_bf, scored, maxed, turned, shifted, sdone,
                                                  edone, pv, recd, ok)), ExitStack() as tmp:
                mx = sb("mx", [P, TB, H2], stack=tmp)
                shift = sb("shift", [H2, BLK], BF16, stack=tmp)
                NPT = 2
                pt = sb("pt", [M, NPT, BLK], stack=tmp)
                rc = sb("rc", [P, 2, TB], stack=tmp)
                HB = 4

                def head(h):
                    return slice(DH2 * (h % 2), DH2 * (h % 2) + DH2), h // 2

                def heads_of(i):
                    return range(2 * HB * (i % 2) + i // 2, 2 * HB * (i % 2) + i // 2 + 2 * HB, 2)

                @block.tensor
                def _(pe):
                    for j in range(KC2):
                        if j >= 2:
                            pe.wait_ge(q_evac, j - 1)
                        for k in range(DK):
                            mm = pe.matmul(bank(4 + j % 2), w2_q[:, k, tok(j)], xT[:, k, blk(c)],
                                           start=(k == 0), stop=(k == DK - 1))
                        mm.then_inc(q_done, 1)
                    pe.wait_ge(q_bf, KC2)
                    for t in range(TB):
                        for i in range(H2 // HB):
                            n = t * (H2 // HB) + i
                            if n >= 4:
                                pe.wait_ge(maxed, n - 3)
                            for s, h in enumerate(heads_of(i)):
                                r, k = head(h)
                                mm = pe.matmul(bank(i)[:, s * M:(s + 1) * M], qTb[r, k, tok(t)],
                                               kTb[r, k, :], start=True, stop=True, skip_group_check=True)
                            mm.then_inc(scored, 1)
                    pe.wait_ge(maxed, TB * (H2 // HB))
                    for t in range(TB):
                        mm = pe.transpose(bank(0)[0:H2, tok(t)], mx[:, t, :], ident[:, :])
                    mm.then_inc(turned, 1)
                    pe.wait_ge(shifted, 1)
                    pe.wait_ge(q_evac, KC2)

                    def scores(h):
                        r, k = head(h)
                        if h >= 2:
                            pe.wait_ge(edone, h - 1)
                        pe.matmul(bank(6 + h % 2)[0:M, :], kT[r, k, :], qT[r, k, :], start=True, stop=False)
                        pe.matmul(bank(6 + h % 2)[0:M, :], pick2[:, h, :], shift[:, :], start=False,
                                  stop=True).then_inc(sdone, 1)

                    def values(h):
                        pe.wait_ge(edone, h + 1)
                        if h >= 2:
                            pe.wait_ge(ok, h - 1)
                        for q in range(TB):
                            mm = pe.matmul(bank(4 + h % 2)[:, q * (DH2 + 1):(q + 1) * (DH2 + 1)],
                                           pt[:, h % NPT, tok(q)], v_aug[:, h, :], start=True, stop=True)
                        mm.then_inc(pv, 1)
                    for h in range(H2 + 1):
                        if h < H2:
                            scores(h)
                        if h:
                            values(h - 1)

                @block.scalar
                def _(act):
                    for j in range(KC2):
                        act.wait_ge(q_done, j + 1)
                        act.activation(qT[:, j, :], bank(4 + j % 2), ACT.Copy).then_inc(q_evac, 1)
                    for h in range(H2):
                        act.wait_ge(sdone, h + 1)
                        if h >= NPT:
                            act.wait_ge(pv, h - NPT + 1)
                        act.activation(pt[:, h % NPT, :], bank(6 + h % 2)[0:M, :], ACT.Exp,
                                       scale=float(DH2) ** -0.5).then_inc(edone, 1)

                @block.vector
                def _(dve):
                    for j in range(KC2):
                        dve.wait_ge(q_evac, j + 1)
                        dve.tensor_copy(qTb[:, j, :], qT[:, j, :]).then_inc(q_bf, 1)
                    for t in range(TB):
                        for i in range(H2 // HB):
                            dve.wait_ge(scored, t * (H2 // HB) + i + 1)
                            hs = heads_of(i)
                            dve.tensor_reduce(mx[:, t, hs[0]:hs[-1] + 1:2],
                                              bank(i, HB * M).rearrange("p (h m) -> p h m", m=M),
                                              AX.X, ALU.max).then_inc(maxed, 1)
                    dve.wait_ge(turned, 1)
                    dve.tensor_scalar(shift[:, :], bank(0)[0:H2, :], -1.0, None, ALU.mult).then_inc(shifted, 1)
                    for h in range(H2):
                        dve.wait_ge(pv, h + 1)
                        o = bank(4 + h % 2, TB * (DH2 + 1)).rearrange("p (q d) -> p q d", d=DH2 + 1)
                        dve.reciprocal(rc[:, h % 2, :].unsqueeze(2), o[:, :, DH2:]).then_inc(recd, 1)
                        dve.wait_ge(recd, h + 1)
                        dve.tensor_tensor(o_tok[:, :, h * DH2:(h + 1) * DH2], o[:, :, 0:DH2],
                                          rc[:, h % 2, :].unsqueeze(2).to_broadcast([P, TB, DH2]),
                                          ALU.mult).then_inc(ok, 1)

        def lora_stage():
            with stage("lora", 4) as (block, (a_done, a_evac, summed, updated)), ExitStack() as tmp:
                lowT = sb("lowT", [16, NB, BLK], stack=tmp)

                @block.tensor
                def _(pe):
                    loaded(pe, "lora")
                    for c in range(NB):
                        for k in range(DK):
                            mm = pe.matmul(bank(c)[0:16, :], lora_a[:, k, :], xT[:, k, blk(c)],
                                           start=(k == 0), stop=(k == DK - 1))
                        mm.then_inc(a_done, 1)
                    for t in range(T):
                        if t >= 4:
                            pe.wait_ge(updated, t - 3)
                        for k in range(DK):
                            pe.matmul(bank(2 + t % 4, D), xT[:, k, tok(t)], wq8[:, k, :], start=(k == 0), stop=False)
                        pe.wait_ge(a_evac, t // TB + 1)
                        pe.matmul(bank(2 + t % 4, D), lowT[:, t // TB, tok(t % TB)], lora_b[:, :], start=False,
                                  stop=True).then_inc(summed, 1)

                @block.scalar
                def _(act):
                    for c in range(NB):
                        act.wait_ge(a_done, c + 1)
                        act.activation(lowT[:, c, :], bank(c)[0:16, :], ACT.Copy).then_inc(a_evac, 1)

                @block.vector
                def _(dve):
                    for t in range(T):
                        dve.wait_ge(summed, t + 1)
                        dve.scalar_tensor_tensor(out=x[:, t, :], in0=bank(2 + t % 4, D), scalar=tg[:, 6:7],
                                                 in1=x[:, t, :], op0=ALU.mult, op1=ALU.add).then_inc(updated, 1)

        def mlp3_stage(o_tok):
            with stage("mlp3", 6) as (block, (turned, evac, h_done, h_evac, summed, updated)), ExitStack() as tmp:
                oT = sb("oT", [P, DK, S], stack=tmp)
                hT = sb("hT", [P, 2 * DK, BLK], stack=tmp)
                HC = 2 * DK

                @block.tensor
                def _(pe):
                    loaded(pe, "w3")
                    for c in range(NB):
                        for k in range(DK):
                            for t in tiles_of(c):
                                mm = pe.transpose(bank(DK * c + k)[:, tok(t % TB)], o_tok[:, t, tok(k)], ident[:, :])
                            mm.then_inc(turned, 1)
                    for c in range(NB):
                        pe.wait_ge(evac, DK * (c + 1))
                        for m in range(HC):
                            n = c * HC + m
                            if n >= 2:
                                pe.wait_ge(h_evac, n - 1)
                            for k in range(DK):
                                mm = pe.matmul(bank(4 + n % 2), w3_1[:, k, tok(m)], oT[:, k, blk(c)],
                                               start=(k == 0), stop=(k == DK - 1))
                            mm.then_inc(h_done, 1)
                        pe.wait_ge(h_evac, HC * (c + 1))
                        for t in tiles_of(c):
                            if t >= 2:
                                pe.wait_ge(updated, t - 1)
                            for m in range(HC):
                                mm = pe.matmul(bank(6 + t % 2, D), hT[:, m, tok(t % TB)], w3_2[:, m, :],
                                               start=(m == 0), stop=(m == HC - 1))
                            mm.then_inc(summed, 1)

                @block.scalar
                def _(act):
                    for c in range(NB):
                        for k in range(DK):
                            act.wait_ge(turned, DK * c + k + 1)
                            act.activation(oT[:, k, blk(c)], bank(DK * c + k), ACT.Copy).then_inc(evac, 1)
                    for c in range(NB):
                        if c:
                            act.wait_ge(summed, TB * c)
                        for m in range(HC):
                            n = c * HC + m
                            act.wait_ge(h_done, n + 1)
                            act.activation(hT[:, m, :], bank(4 + n % 2), ACT.Relu, bias=col("b1_3", m)
                                           ).then_inc(h_evac, 1)

                @block.vector
                def _(dve):
                    for t in range(T):
                        dve.wait_ge(summed, t + 1)
                        dve.scalar_tensor_tensor(out=x[:, t, :], in0=bank(6 + t % 2, D), scalar=tg[:, 3:4],
                                                 in1=x[:, t, :], op0=ALU.mult, op1=ALU.add).then_inc(updated, 1)

        def dispatch_stage(b):
            with stage("dispatch", 9) as (block, (logged, centred, exped, step, chosen, counted, kept_x, placed,
                                                   saved)), ExitStack() as tmp:
                lg = sb("lg", [P, T, E], stack=tmp)
                ex = sb("ex", [P, T, E], stack=tmp)
                onehot = sb("onehot", [P, T, E], stack=tmp)
                before = sb("before", [P, T + 1, E], stack=tmp)
                cum = sb("cum", [P, T, E], stack=tmp)
                s1 = sb("s1", [P, 8, T], stack=tmp)
                to = sb("to", [P, T], U32, stack=tmp)

                @block.sync
                def _(sp):
                    sp.dma_start(residual.rearrange("(b t p) d -> b p t d", p=P, t=T)[bass.ds(b, 1)]
                                 .rearrange("o p t d -> p (o t) d"), x[:, :, :]).then_inc(saved, 16)
                    sp.wait_ge(saved, 16)

                @block.tensor
                def _(pe):
                    loaded(pe, "w3")
                    for t in range(T):
                        for k in range(DK):
                            mm = pe.matmul(bank(6)[:, E * t:E * (t + 1)], xT[:, k, tok(t)], r3[:, k, :],
                                           start=(k == 0), stop=(k == DK - 1))
                    mm.then_inc(logged, 1)
                    pe.wait_ge(chosen, 1)
                    flat = onehot[:, :, :].rearrange("p t e -> p (t e)")
                    pe.matmul(bank(0, T * E), upper[:, :], flat, start=True, stop=True)
                    pe.matmul(bank(1, T * E), ones_f[:, :], flat, start=True, stop=True).then_inc(counted, 1)

                @block.scalar
                def _(act):
                    act.wait_ge(centred, 1)
                    act.activation(ex[:, :, :], lg[:, :, :], ACT.Exp).then_inc(exped, 1)

                @block.vector
                def _(dve):
                    chain = chained(dve, step)
                    total, inverse, best, order, base, pos, kept, far = (s1[:, i, :] for i in range(8))
                    dve.wait_ge(logged, 1)
                    chain(dve.tensor_copy(lg[:, :, :], bank(6, T * E).rearrange("p (t e) -> p t e", e=E)))
                    chain(dve.tensor_reduce(total, lg[:, :, :], AX.X, ALU.max))
                    dve.tensor_tensor(lg[:, :, :], lg[:, :, :], over(total), ALU.subtract).then_inc(centred, 1)
                    dve.wait_ge(exped, 1)
                    chain(dve.tensor_reduce(total, ex[:, :, :], AX.X, ALU.add))
                    chain(dve.reciprocal(inverse, total))
                    first_largest(chain, dve, ex[:, :, :], onehot[:, :, :], best, order)
                    dve.tensor_copy(before[:, 0, :], taken[:, :]).then_inc(chosen, 1)
                    dve.wait_ge(chosen, 1)
                    dve.wait_ge(counted, 1)
                    for t in range(T):
                        chain(dve.tensor_tensor(before[:, t + 1, :], before[:, t, :], bank(1)[:, E * t:E * (t + 1)],
                                                ALU.add))
                    chain(dve.tensor_copy(taken[:, :], before[:, T, :]))
                    chain(dve.tensor_tensor(cum[:, :, :], before[:, 0:T, :],
                                            bank(0, T * E).rearrange("p (t e) -> p t e", e=E), ALU.add))
                    chain(dve.tensor_tensor(cum[:, :, :], cum[:, :, :], onehot[:, :, :], ALU.mult))
                    chain(dve.tensor_reduce(pos, cum[:, :, :], AX.X, ALU.add))
                    chain(dve.tensor_scalar(pos, pos, 1.0, None, ALU.subtract))
                    chain(dve.tensor_scalar(base, order, -float(CAP), float(E * CAP), ALU.mult, ALU.add))
                    chain(dve.tensor_scalar(kept, pos, float(CAP), None, ALU.is_lt))
                    chain(dve.tensor_scalar(far, kept, -FAR, FAR, ALU.mult, ALU.add))
                    chain(dve.tensor_tensor(far, far, base, ALU.add))
                    chain(dve.tensor_tensor(far, far, pos, ALU.add))
                    dve.tensor_copy(to[:, :], far).then_inc(placed, 1)
                    chain(dve.tensor_scalar(pos, pos, float(CAP - 1), None, ALU.min))
                    chain(dve.tensor_tensor(pos, pos, base, ALU.add))
                    dve.tensor_copy(slot[:, bass.ds(b * T, T)], pos).then_inc(kept_x, 1)
                    chain(dve.tensor_tensor(best, best, inverse, ALU.mult))
                    chain(dve.tensor_tensor(best, best, kept, ALU.mult))
                    chain(dve.tensor_scalar(best, best, tg[:, 7:8], None, ALU.mult))
                    dve.tensor_copy(prob[:, bass.ds(b * T, T)], best).then_inc(kept_x, 1)

                @block.gpsimd
                def _(pool):
                    pool.wait_ge(placed, 1)
                    for t in range(T):
                        pool.indirect_dma_start(out=slots_in, out_offset=bass.IndirectOffsetOnAxis(
                            ap=to[:, t:t + 1], axis=0), in_=xn[:, t, :], in_offset=None,
                            bounds_check=SLOTS - 1, oob_is_err=False).then_inc(sent, 16)
                    pool.wait_ge(sent, b * (16 * T) + 16 * T)

        def expert_stage(e, bufs, mine, nxt):
            w1, w2, b1, b2, tk = bufs[mine]
            with stage("expert", 8) as (block, (loading, turned, evac, up_done, gelued, down, biased, stored)), \
                    ExitStack() as tmp:
                tT = sb("tT", [P, DK, CAP], stack=tmp)
                hT = sb("hT", [P, FC, CAP], stack=tmp)
                eo = sb("eo", [P, CT, D], stack=tmp)
                HALF = CAP // 2
                HT = HALF // P

                @block.sync
                def _(sp):
                    if nxt is not None:
                        expert_loads(sp, nxt, bufs[1 - mine], loading)
                    for t in range(CT):
                        sp.wait_ge(biased, t + 1)
                        sp.dma_start(slots_out.rearrange("(e t p) d -> e t p d", e=E, p=P)[bass.ds(e, 1), t]
                                     .rearrange("o p d -> (o p) d"), eo[:, t, :]).then_inc(stored, 16)
                    sp.wait_ge(stored, 16 * CT)
                    if nxt is not None:
                        sp.wait_ge(loading, 16 * 5)

                @block.tensor
                def _(pe):
                    for half in range(2):
                        for k in range(DK):
                            for t in range(HT):
                                mm = pe.transpose(bank(2 * half + k)[:, tok(t)], tk[:, half * HT + t, tok(k)],
                                                  ident[:, :])
                            mm.then_inc(turned, 1)
                    for half in range(2):
                        pe.wait_ge(evac, DK * (half + 1))
                        for f in range(FC):
                            n = half * FC + f
                            if n >= 2:
                                pe.wait_ge(gelued, n - 1)
                            for k in range(DK):
                                mm = pe.matmul(bank(4 + n % 2, HALF), w1[:, k, tok(f)],
                                               tT[:, k, half * HALF:(half + 1) * HALF],
                                               start=(k == 0), stop=(k == DK - 1))
                            mm.then_inc(up_done, 1)
                    for t in range(CT):
                        pe.wait_ge(gelued, FC * (t // HT + 1))
                        if t >= 2:
                            pe.wait_ge(biased, t - 1)
                        for f in range(FC):
                            mm = pe.matmul(bank(6 + t % 2, D), hT[:, f, tok(t)], w2[:, f, :],
                                           start=(f == 0), stop=(f == FC - 1))
                        mm.then_inc(down, 1)

                @block.scalar
                def _(act):
                    for n in range(2 * FC):
                        half, f = divmod(n, FC)
                        act.wait_ge(up_done, n + 1)
                        act.activation(hT[:, f, half * HALF:(half + 1) * HALF], bank(4 + n % 2, HALF), ACT.Gelu,
                                       bias=b1[:, f:f + 1]).then_inc(gelued, 1)

                @block.vector
                def _(dve):
                    for i in range(2 * DK):
                        half, k = divmod(i, DK)
                        dve.wait_ge(turned, i + 1)
                        dve.tensor_copy(tT[:, k, half * HALF:(half + 1) * HALF], bank(i, HALF)).then_inc(evac, 1)
                    for t in range(CT):
                        dve.wait_ge(down, t + 1)
                        dve.tensor_tensor(eo[:, t, :], bank(6 + t % 2, D), b2[:, :], ALU.add).then_inc(biased, 1)

        def expert_loads(sp, e, buf, loading):
            w1, w2, b1, b2, tk = buf
            def of(ap):
                return ap[bass.ds(e, 1)] if not isinstance(e, int) else ap[e:e + 1]
            sp.dma_start(tk[:, :, :], of(slots_in.rearrange("(e t p) d -> e p t d", e=E, p=P))
                         .rearrange("o p t d -> p (o t) d")).then_inc(loading, 16)
            sp.dma_start(w1[:, :, :], of(a["L3_ffn_w1"]).rearrange("o (k p) f -> p (o k) f", p=P)).then_inc(loading, 16)
            sp.dma_start(b1[:, :], of(a["b1_cols"]).rearrange("o p f -> (o p) f")).then_inc(loading, 16)
            sp.dma_start(w2[:, :, :], of(a["L3_ffn_w2"]).rearrange("o (f p) d -> p (o f) d", p=P)).then_inc(loading, 16)
            sp.dma_start(b2[:, :], of(a["L3_ffn_b2"]).to_broadcast([P, D])).then_inc(loading, 16)

        def combine_stage(b):
            with stage("combine", 4) as (block, (xs, indexed, summed, stored)), ExitStack() as tmp:
                got = sb("got", [P, T, D], stack=tmp)
                idx = sb("idx", [P, T], U32, stack=tmp)
                pr = sb("pr", [P, T], stack=tmp)
                of_batch = "(b t p) d -> b p t d"

                @block.sync
                def _(sp):
                    sp.dma_start(x[:, :, :], residual.rearrange(of_batch, p=P, t=T)[bass.ds(b, 1)]
                                 .rearrange("o p t d -> p (o t) d")).then_inc(xs, 16)
                    sp.wait_ge(summed, T)
                    sp.dma_start(out.rearrange(of_batch, p=P, t=T)[bass.ds(b, 1)]
                                 .rearrange("o p t d -> p (o t) d"), x[:, :, :]).then_inc(stored, 16)
                    sp.wait_ge(stored, 16)

                @block.vector
                def _(dve):
                    dve.tensor_copy(idx[:, :], slot[:, bass.ds(b * T, T)]).then_inc(indexed, 1)
                    dve.tensor_copy(pr[:, :], prob[:, bass.ds(b * T, T)]).then_inc(indexed, 1)
                    dve.wait_ge(indexed, 2)
                    dve.wait_ge(xs, 16)
                    for t in range(T):
                        dve.wait_ge(fetched[t], b * 16 + 16)
                        dve.scalar_tensor_tensor(out=x[:, t, :], in0=got[:, t, :], scalar=pr[:, t:t + 1],
                                                 in1=x[:, t, :], op0=ALU.mult, op1=ALU.add).then_inc(summed, 1)

                @block.gpsimd
                def _(pool):
                    pool.wait_ge(indexed, 1)
                    for t in range(T):
                        pool.indirect_dma_start(out=got[:, t, :], out_offset=None, in_=slots_out,
                                                in_offset=bass.IndirectOffsetOnAxis(ap=idx[:, t:t + 1], axis=0),
                                                bounds_check=SLOTS - 1, oob_is_err=True).then_inc(fetched[t], 16)

        def small_buffers(stack):
            return (sb("qT1", [P, G, S], stack=stack), sb("qTb1", [P, G, S], BF16, stack=stack),
                    sb("kbd", [P, G, GM], stack=stack), sb("kbdb", [P, G, GM], BF16, stack=stack),
                    sb("vbig", [P, len(CH), G, VW], stack=stack), sb("shift1", [H1, S], BF16, stack=stack))

        with nc.Fori(0, B) as b:
            at_start = turn[0]
            load_stage(b)
            norm_stage("norm0", bias_row="bo0", double=True)
            with ExitStack() as tmp:
                qT = sb("qT0", [P, DK, S], stack=tmp)
                kT = sb("kT0", [P, DK, KEYS0 + 3], stack=tmp)
                qTb = sb("qTb0", [P, DK, S], BF16, stack=tmp)
                kTb = sb("kTb0", [P, DK, KEYS0 + 3], BF16, stack=tmp)
                v_aug = sb("v0", [P, NK0, H0, DH0 + 1], stack=tmp)
                qkv0_stage(qT, kT, qTb, kTb, v_aug)
                attend0_stage(qT, kT, qTb, kTb, v_aug, xn)
            project_stage("project0", xn, w0_o, "w0", DK, 0)
            if upto > 1:
                norm_stage("norm1")
                moe0_stage()
            if upto > 2:
                norm_stage("norm2", bias_row="bo1")
                with ExitStack() as tmp:
                    small = small_buffers(tmp)
                    small_prepare_stage("prepare1", "w1", w1_q, w1_k, w1_v, "bq1", *small[:5])
                    small_shift_stage("shift1", small[1], small[3], small[5], True)
                    clipped_attend_stage("attend1", small[0], small[2], small[4], small[5], xn)
                project_stage("project1", xn, w1_o, "w1", DK, 1)
            if upto > 3:
                norm_stage("norm3")
                moe1_stage()
            if upto > 4:
                norm_stage("norm4", bias_row="bproj")
                with ExitStack() as tmp:
                    kT = sb("kT2", [P, KC2, M], stack=tmp)
                    kTb = sb("kTb2", [P, KC2, M], BF16, stack=tmp)
                    v_aug = sb("v2", [M, H2, DH2 + 1], stack=tmp)
                    qT = sb("qT2", [P, KC2, BLK], stack=tmp)
                    o_tok = sb("o2", [P, TB, H2 * DH2], stack=tmp)
                    kv2_stage(kT, kTb, v_aug)
                    for c in range(NB):
                        with ExitStack() as tmp2:
                            qTb = sb("qTb2", [P, KC2, BLK], BF16, stack=tmp2)
                            attend2_stage(c, qT, qTb, kT, kTb, v_aug, o_tok)
                        project_stage("project2", o_tok, w2_o, "w2", KC2, 2, c * TB, TB)
            if upto > 5:
                norm_stage("norm5", bias_row="bias2")
                lora_stage()
            if upto > 6:
                norm_stage("norm6", bias_row="b2_3")
                with ExitStack() as tmp:
                    small = small_buffers(tmp)
                    small_prepare_stage("prepare3", "w3", w3_q, w3_k, w3_v, "bq3", *small[:5])
                    small_shift_stage("shift3", small[1], small[3], small[5], False)
                    small_attend_stage("attend3", small[0], small[2], small[4], small[5], xn)
                mlp3_stage(xn)
            if upto > 7:
                norm_stage("norm7")
                dispatch_stage(b)
            else:
                with stage("dump", 1) as (block, (dumped,)):
                    @block.sync
                    def _(sp):
                        sp.dma_start(out.rearrange("(b t p) d -> b p t d", p=P, t=T)[bass.ds(b, 1)]
                                     .rearrange("o p t d -> p (o t) d"), x[:, :, :]).then_inc(dumped, 16)
                        sp.wait_ge(dumped, 16)
                        for group in loads:
                            loaded(sp, group)
            if turn[0] != at_start:
                with stage("even", 0):
                    pass
        if upto > 7:
            arena.close()
            with ExitStack() as tmp:
                bufs = [(sb(f"ew1_{i}", [P, DK, F3], stack=tmp), sb(f"ew2_{i}", [P, FC, D], stack=tmp),
                         sb(f"eb1_{i}", [P, FC], stack=tmp), sb(f"eb2_{i}", [P, D], stack=tmp),
                         sb(f"etk_{i}", [P, CT, D], stack=tmp)) for i in range(2)]
                with stage("first_expert", 1) as (block, (loading,)):
                    @block.sync
                    def _(sp):
                        expert_loads(sp, 0, bufs[0], loading)
                        sp.wait_ge(loading, 16 * 5)
                with nc.Fori(0, E // 2 - 1) as i:
                    expert_stage(i * 2, bufs, 0, i * 2 + 1)
                    expert_stage(i * 2 + 1, bufs, 1, i * 2 + 2)
                expert_stage(E - 2, bufs, 0, E - 1)
                expert_stage(E - 1, bufs, 1, None)
                with nc.Fori(0, B) as b:
                    combine_stage(b)
                    with stage("even2", 0):
                        pass


def kernel(**inputs):
    import numpy as np
    import concourse.bacc as bacc
    from concourse.bass_utils import run_bass_kernel_spmd

    arrays = layout(inputs)
    nc = bacc.Bacc("TRN2", target_bir_lowering=False, num_devices=1)
    args = {n: nc.dram_tensor("in_" + n, v.shape, mybir.dt.from_np(v.dtype), kind="ExternalInput").ap()
            for n, v in arrays.items()}
    out = nc.dram_tensor("out", [B * S, D], F32, kind="ExternalOutput").ap()
    flamingo_kernel(nc, args, out)
    r = run_bass_kernel_spmd(nc, [{"in_" + n: v for n, v in arrays.items()}], core_ids=[0])
    return r.results[0]["out"].reshape(B, S, D)


def layout(inputs):
    import numpy as np

    v = {n: np.asarray(i) for n, i in inputs.items()}
    out = {n: v[n] for n in (
        "x", "ctx_768", "L0_ffn_router_w", "L0_ffn_expert_w", "L0_ffn_expert_b", "L1_xattn_Wq", "L1_xattn_Wo",
        "L1_ffn_gate_w", "L1_ffn_w1", "L1_ffn_w2", "L1_ffn_w3", "L2_xattn_Wq", "L2_xattn_Wkv", "L2_xattn_Wproj",
        "L2_ffn_kernel", "L2_ffn_a", "L2_ffn_b", "L3_xattn_Wq", "L3_xattn_W1", "L3_xattn_W2", "L3_ffn_w1",
        "L3_ffn_w2", "L3_ffn_b2")}
    out["mask"] = v["mask_BxS2_bk0"]
    out["w0_qkv"] = np.concatenate([v["L0_xattn_Wq"], v["L0_xattn_Wlkv"]]).T
    out["w0_ckv"] = v["L0_xattn_Wkv"].T
    out["w0_o"] = v["L0_xattn_Wo"].T
    for i in (1, 3):
        for w in "kv":
            out[f"w{i}_{w}"] = np.concatenate([v[f"L{i}_xattn_W{w}"], v[f"L{i}_xattn_b{w}"][None]])
    out["r3"] = v["L3_ffn_router_w"].T
    out["b1_cols"] = v["L3_ffn_b1"].reshape(E, FC, P).transpose(0, 2, 1)

    def columns(vector):
        return np.pad(vector, (0, -len(vector) % P)).reshape(-1, P).T

    def same(vector):
        return np.broadcast_to(vector, (P, len(vector)))

    out["cols"] = np.concatenate([
        same(v["g_xattn"]), same(v["g_ffn"]), same(v["L0_ffn_router_b"]), columns(v["L0_xattn_ln_x_g"]),
        columns(v["L0_xattn_ln_x_b"]), columns(v["L0_xattn_ln_l_g"]), columns(v["L0_xattn_ln_l_b"]),
        columns(np.tile(v["L0_xattn_qn_g"], 2)), columns(np.tile(v["L0_xattn_kn_g"], 2)),
        columns(v["L1_xattn_bq"]), columns(v["L3_xattn_bq"]), columns(v["L3_xattn_b1"])], axis=1)
    out["rows"] = np.concatenate([same(v[n]) for n in (
        "L0_xattn_bo", "L1_xattn_bo", "L2_xattn_bproj", "L2_ffn_bias", "L3_xattn_b2")], axis=1)
    return {n: np.ascontiguousarray(i) for n, i in out.items()}
```

```python
from contextlib import ExitStack, contextmanager

import concourse.bass as bass
from concourse import mybir

F32 = mybir.dt.float32
BF16 = mybir.dt.bfloat16
U8 = mybir.dt.uint8
U32 = mybir.dt.uint32
ALU = mybir.AluOpType
ACT = mybir.ActivationFunctionType
AX = mybir.AxisListType

P = 128
B, S, D = 4, 1024, 256
T = S // P
DK = D // P
BLK = 512
NB = S // BLK
TB = BLK // P
M = 77
C = 192
C1 = C - P
E = 8
H0, DH0 = 4, 64
H1, DH1 = 16, 16
H2, DH2 = 16, 64
G = DK
HG = H1 // G
GM = HG * M
CH = [(c * P, min(P, GM - c * P)) for c in range((GM + P - 1) // P)]
F3 = 1024
CAP = 768
CT = CAP // P
FC = F3 // P
SLOTS = E * CAP
FAR = 1.0e6
EPS = 1e-5
LOW = 1.0e30


COLS, at = {}, 0
for name, n in (("gates", 8), ("rb0", E), ("ln_x_g", 2), ("ln_x_b", 2), ("ln_l_g", 2), ("ln_l_b", 2), ("qn_g", 1),
                ("kn_g", 1), ("bq1", 2), ("bq3", 2), ("b1_3", 4)):
    COLS[name] = at
    at += n
GATED = (("bo0", 0), ("bo1", 1), ("bproj", 2), ("bias2", 6), ("b2_3", 3))
ROWS = {name: i for i, (name, _) in enumerate(GATED)}
CLAMP = 10000.0


def flamingo_kernel(nc, a, out, upto=8):
    ctx = ExitStack()
    with ctx:
        named = []

        def sb(name, shape, dt=F32, stack=ctx):
            named.append(name)
            name = name if stack is ctx else f"{name}_{len(named)}"
            return stack.enter_context(nc.sbuf_tensor(name, shape, dt))

        def sem(name):
            return ctx.enter_context(nc.semaphore(name))

        psum = ctx.enter_context(nc.psum_tensor("psum", [P, 8 * 512], F32))

        def bank(i, n=512):
            return psum[:, 512 * i:512 * i + n]

        residual = nc.dram_tensor("residual", [B * S, D], F32, kind="Internal").ap()
        slots_in = nc.dram_tensor("slots_in", [SLOTS, D], F32, kind="Internal").ap()
        slots_out = nc.dram_tensor("slots_out", [SLOTS, D], F32, kind="Internal").ap()

        NSEM = 40
        sem_banks = [[sem(f"stage_{i}_{j}") for j in range(NSEM)] for i in range(2)]
        turn = [1]

        @contextmanager
        def stage(name, count):
            turn[0] ^= 1
            old = sem_banks[1 - turn[0]]
            named.append(name)
            with nc.Block(f"{name}_{len(named)}") as block:
                @block.sync
                def _(sp):
                    sp.sem_clear(range(old[0].num, old[-1].num + 1))
                yield block, sem_banks[turn[0]][:count]

        sent = sem("rows_sent")
        fetched = [sem(f"row_fetched_{t}") for t in range(T)]

        loads = {}

        ident = sb("ident", [P, P])
        ones_bf = sb("ones_bf", [1, P], BF16)
        ones_f = sb("ones_f", [P, P])
        upper = sb("upper", [P, P])
        cols = sb("cols", list(a["cols"].shape))
        rows = sb("rows", list(a["rows"].shape))
        tg = sb("tg", [P, 8])
        neg_half = sb("neg_half", [P, 16])
        rank = sb("rank", [P, T, E])
        head_of_feature = sb("head_of_feature", [P, HG])
        head_of_row = sb("head_of_row", [P, len(CH), HG])
        pick_row = sb("pick_row", [H1, G, GM], BF16)
        pick2 = sb("pick2", [2, 2, M], BF16)
        mask_col = sb("mask_col", [M, 1])
        mask_row = sb("mask_row", [1, M], BF16)
        slot = sb("slot", [P, B * T], U32)
        prob = sb("prob", [P, B * T])
        taken = sb("taken", [P, E])

        x = sb("x", [P, T, D])
        xn = sb("xn", [P, T, D])
        xT = sb("xT", [P, DK, S])
        ctxT = sb("ctxT", [P, 2, M])
        cnT = sb("cnT", [P, 2, M])
        ctx_rep = sb("ctx_rep", [P, 2, GM])

        zeros = xn

        arena = ExitStack()
        ctx.enter_context(arena)

        def wsb(name, shape):
            return arena.enter_context(nc.sbuf_tensor(name, shape, F32))

        w0_qkv = wsb("w0_qkv", [P, DK, 3 * D])
        w0_ckv = wsb("w0_ckv", [P, 2, 2 * D])
        w0_o = wsb("w0_o", [P, DK, D])
        r0 = wsb("r0", [P, DK, E])
        e0 = wsb("e0", [P, DK, E * D])
        e0_b = wsb("e0_b", [E, D])
        w1_q = wsb("w1_q", [P, DK, D])
        w1_k = wsb("w1_k", [P, 2, D])
        w1_v = wsb("w1_v", [P, 2, D])
        w1_o = wsb("w1_o", [P, DK, D])
        r1 = wsb("r1", [P, DK, E])
        e1_up = wsb("e1_up", [P, DK, E * D])
        e1_down = wsb("e1_down", [P, E, D])
        w2_q = wsb("w2_q", [P, DK, H2 * DH2])
        w2_kv = wsb("w2_kv", [P, 2, 2 * H2 * DH2])
        w2_o = wsb("w2_o", [P, H2 * DH2 // P, D])
        wq8 = wsb("wq8", [P, DK, D])
        lora_a = wsb("lora_a", [P, DK, 16])
        lora_b = wsb("lora_b", [16, D])
        w3_q = wsb("w3_q", [P, DK, D])
        w3_k = wsb("w3_k", [P, 2, D])
        w3_v = wsb("w3_v", [P, 2, D])
        w3_1 = wsb("w3_1", [P, DK, 2 * D])
        w3_2 = wsb("w3_2", [P, 2 * DK, D])
        r3 = wsb("r3", [P, DK, E])

        def col(name, k=0):
            return cols[:, COLS[name] + k:COLS[name] + k + 1]

        def row(name):
            return rows[:, ROWS[name] * D:(ROWS[name] + 1) * D]

        def load(eng, group, *pairs):
            loads[group] = (sem("load_" + group), 16 * len(pairs))
            for dst, src in pairs:
                eng.dma_start(dst, src).then_inc(loads[group][0], 16)

        def loaded(eng, group):
            eng.wait_ge(*loads[group])

        def chunked(dst, src):
            n = src.shape[0]
            if n % P == 0:
                return [(dst[:, :, :], src.rearrange("(k p) n -> p k n", p=P))]
            return [(dst[:, 0, :], src[0:P, :]), (dst[0:n - P, 1, :], src[P:n, :])]

        with stage("prepare", 9) as (block, (zeroed, selected, tanhed, maxed, absmax, scaled,
                                              rounded, gates, cleared)):
            quant_tmp = ExitStack()
            kern = sb("kern", [P, DK, D], stack=quant_tmp)
            kscale = sb("kscale", [P, 4], stack=quant_tmp)

            @block.sync
            def _(sp):
                load(sp, "cols", (cols[:, :], a["cols"]))
                load(sp, "rows", (rows[:, :], a["rows"]))
                load(sp, "kern", *chunked(kern, a["L2_ffn_kernel"]))
                load(sp, "w0", *chunked(w0_qkv, a["w0_qkv"]), *chunked(w0_ckv, a["w0_ckv"]),
                     *chunked(w0_o, a["w0_o"]))
                load(sp, "e0", *chunked(r0, a["L0_ffn_router_w"]), (e0_b[:, :], a["L0_ffn_expert_b"]),
                     *[(e0[:, :, e * D:(e + 1) * D],
                        a["L0_ffn_expert_w"][e].rearrange("(k p) n -> p k n", p=P)) for e in range(E)])
                load(sp, "w1", *chunked(w1_q, a["L1_xattn_Wq"]), *chunked(w1_k, a["w1_k"]),
                     *chunked(w1_v, a["w1_v"]), *chunked(w1_o, a["L1_xattn_Wo"]))
                load(sp, "e1", *chunked(r1, a["L1_ffn_gate_w"]),
                     *[(e1_up[:, :, e * D + i * P:e * D + (i + 1) * P],
                        a[w][e].rearrange("(k p) n -> p k n", p=P))
                       for e in range(E) for i, w in enumerate(("L1_ffn_w1", "L1_ffn_w3"))],
                     (e1_down[:, :, :], a["L1_ffn_w2"].rearrange("e p n -> p e n")))
                load(sp, "w2", *chunked(w2_q, a["L2_xattn_Wq"]), *chunked(w2_kv, a["L2_xattn_Wkv"]),
                     *chunked(w2_o, a["L2_xattn_Wproj"]))
                load(sp, "lora", *chunked(lora_a, a["L2_ffn_a"]), (lora_b[:, :], a["L2_ffn_b"]))
                load(sp, "w3", *chunked(w3_q, a["L3_xattn_Wq"]), *chunked(w3_k, a["w3_k"]),
                     *chunked(w3_v, a["w3_v"]), *chunked(w3_1, a["L3_xattn_W1"]),
                     *chunked(w3_2, a["L3_xattn_W2"]), *chunked(r3, a["r3"]))
                sp.wait_ge(cleared, 1)
                zrows = slots_in.rearrange("(n p r) d -> n p (r d)", p=P, r=T)
                load(sp, "zero", *[(zrows[n], zeros[:, :, :].rearrange("p t d -> p (t d)"))
                                   for n in range(SLOTS // (P * T))])
                loaded(sp, "zero")

            @block.gpsimd
            def _(pool):
                n = [0]

                def fill(ap, value):
                    pool.memset(ap, value).then_inc(zeroed, 1)
                    n[0] += 1
                fill(ident[:, :], 0.0)
                fill(upper[:, :], 1.0)
                fill(head_of_feature[:, :], 1.0)
                fill(head_of_row[:, :, :], 1.0)
                fill(pick_row[:, :, :], 0.0)
                fill(pick2[:, :, :], 0.0)
                fill(ones_bf[:, :], 1.0)
                fill(ones_f[:, :], 1.0)
                fill(neg_half[:, :], -0.5)
                fill(taken[:, :], 0.0)
                fill(ctxT[:, :, :], 1.0)
                for e in range(E):
                    fill(rank[:, :, e:e + 1], float(E - e))
                pool.wait_ge(zeroed, n[0])

                def choose(ap, op, value, base, pattern, mult):
                    pool.affine_select(out=ap, in_=ap, compare_op=op, fill=value, base=base, pattern=pattern,
                                       channel_multiplier=mult).then_inc(selected, 1)
                choose(ident[:, :], ALU.not_equal, 1.0, 0, [[-1, P]], 1)
                choose(upper[:, :], ALU.is_ge, 0.0, 0, [[1, P]], -1)
                choose(head_of_feature[:, :], ALU.is_ge, 0.0, 0, [[-DH1, HG]], 1)
                choose(head_of_row[:, :, :], ALU.is_ge, 0.0, 0, [[P, len(CH)], [-M, HG]], 1)
                choose(pick_row[:, :, :].rearrange("p g (h m) -> p g h m", m=M), ALU.not_equal, 1.0, 0,
                       [[-HG, G], [-1, HG], [0, M]], 1)
                choose(pick2[:, :, :], ALU.not_equal, 1.0, 0, [[-1, 2], [0, M]], 1)
                pool.wait_ge(selected, 6)
                choose(head_of_feature[:, :], ALU.is_ge, 0.0, DH1 - 1, [[DH1, HG]], -1)
                choose(head_of_row[:, :, :], ALU.is_ge, 0.0, M - 1, [[-P, len(CH)], [M, HG]], -1)
                pool.wait_ge(maxed, 1)
                pool.partition_all_reduce(kscale[:, 1:2], kscale[:, 0:1], P,
                                          bass.bass_isa.ReduceOp.max).then_inc(absmax, 1)

            @block.scalar
            def _(act):
                loaded(act, "cols")
                act.activation(tg[:, :], cols[:, COLS["gates"]:COLS["gates"] + 8], ACT.Tanh).then_inc(tanhed, 1)

            @block.vector
            def _(dve):
                dve.memset(zeros[:, :, :], 0.0).then_inc(cleared, 1)
                loaded(dve, "rows")
                dve.wait_ge(tanhed, 1)
                for name, g in GATED:
                    dve.tensor_scalar(row(name), row(name), tg[:, g:g + 1], None, ALU.mult).then_inc(gates, 1)
                loaded(dve, "kern")
                dve.tensor_reduce(kscale[:, 0:1], kern[:, :, :], AX.XY, ALU.max,
                                  apply_absolute_value=True).then_inc(maxed, 1)
                dve.wait_ge(absmax, 1)
                dve.tensor_scalar(kscale[:, 2:3], kscale[:, 1:2], 1.0 / 7.0, None, ALU.mult).then_inc(scaled, 1)
                dve.wait_ge(scaled, 1)
                dve.reciprocal(kscale[:, 3:4], kscale[:, 2:3]).then_inc(scaled, 1)
                dve.wait_ge(scaled, 2)
                dve.tensor_scalar(wq8[:, :, :], kern[:, :, :], kscale[:, 3:4], None, ALU.mult).then_inc(scaled, 1)
                dve.wait_ge(scaled, 3)
                magic = 1.5 * 2.0 ** 23
                dve.tensor_scalar(wq8[:, :, :], wq8[:, :, :], magic, None, ALU.add).then_inc(rounded, 1)
                dve.wait_ge(rounded, 1)
                dve.tensor_scalar(wq8[:, :, :], wq8[:, :, :], magic, None, ALU.subtract).then_inc(rounded, 1)
                dve.wait_ge(rounded, 2)
                dve.tensor_scalar(wq8[:, :, :], wq8[:, :, :], -8.0, 7.0, ALU.max, ALU.min).then_inc(rounded, 1)
                dve.wait_ge(rounded, 3)
                dve.tensor_scalar(wq8[:, :, :], wq8[:, :, :], kscale[:, 2:3], None, ALU.mult).then_inc(rounded, 1)
            quant_tmp.close()

        def tiles_of(c):
            return range(c * TB, (c + 1) * TB)

        def tok(t):
            return slice(t * P, (t + 1) * P)

        def blk(c):
            return slice(c * BLK, (c + 1) * BLK)

        def norm_stage(name, bias_row=None, double=False):
            with stage(name, 10) as (block, (stated, varied, added, powed, normed, turned, evac,
                                             biased, s2, s3)), ExitStack() as tmp:
                st = sb("st", [P, T, 6], stack=tmp)
                mv = sb("mv", [P, T, 2], stack=tmp)
                rs = sb("rs", [P, 2, T], stack=tmp)
                rounds = 2 if double else 1

                @block.vector
                def _(dve):
                    for r in range(rounds):
                        src = x if r == 0 else xn
                        if r:
                            dve.wait_ge(normed, T * r)
                        for t in range(T):
                            dve.bn_stats(st[:, t, :], src[:, t, :]).then_inc(stated, 1)
                        for t in range(T):
                            dve.wait_ge(stated, T * r + t + 1)
                            dve.bn_aggr(mv[:, t, :], st[:, t, :]).then_inc(varied, 1)
                        dve.wait_ge(powed, r + 1)
                        for t in range(T):
                            dve.tensor_scalar(xn[:, t, :], src[:, t, :], mv[:, t, 0:1], rs[:, 1, t:t + 1],
                                              ALU.subtract, ALU.mult).then_inc(normed, 1)

                @block.gpsimd
                def _(pool):
                    for r in range(rounds):
                        pool.wait_ge(varied, T * (r + 1))
                        pool.tensor_scalar(rs[:, 0, :], mv[:, :, 1], EPS, None, ALU.add).then_inc(added, 1)
                        pool.wait_ge(added, r + 1)
                        pool.tensor_tensor(rs[:, 1, :], rs[:, 0, :], neg_half[:, 0:T], ALU.pow).then_inc(powed, 1)
                    if bias_row is not None:
                        pool.wait_ge(normed, T)
                        for t in range(T):
                            pool.tensor_tensor(x[:, t, :], x[:, t, :], row(bias_row),
                                               ALU.add).then_inc(biased, 1)

                @block.tensor
                def _(pe):
                    for c in range(NB):
                        for t in tiles_of(c):
                            pe.wait_ge(normed, T * (rounds - 1) + t + 1)
                            for k in range(DK):
                                pe.transpose(bank(DK * c + k)[:, tok(t % TB)], xn[:, t, tok(k)],
                                             ident[:, :]).then_inc(turned, 1)

                @block.scalar
                def _(act):
                    for c in range(NB):
                        act.wait_ge(turned, DK * TB * (c + 1))
                        for k in range(DK):
                            if double:
                                act.activation(xT[:, k, blk(c)], bank(DK * c + k), ACT.Identity,
                                               bias=col("ln_l_b", k), scale=col("ln_l_g", k)).then_inc(evac, 1)
                            else:
                                act.activation(xT[:, k, blk(c)], bank(DK * c + k), ACT.Copy).then_inc(evac, 1)

        def project_stage(name, o_tok, w, group, chunks, gate, c0=0, count=T):
            with stage(name, 4) as (block, (turned, evac, summed, updated)), ExitStack() as tmp:
                oT = sb("oT", [P, 2, chunks, P], stack=tmp)
                per = (chunks + 3) // 4

                @block.tensor
                def _(pe):
                    loaded(pe, group)

                    def turn_tile(t):
                        if t >= 2:
                            pe.wait_ge(evac, per * (t - 1))
                        for k in range(chunks):
                            pe.transpose(bank(per * (t % 2) + k // 4)[:, tok(k % 4)], o_tok[:, t, tok(k)],
                                         ident[:, :]).then_inc(turned, 1)
                    turn_tile(0)
                    for t in range(count):
                        if t + 1 < count:
                            turn_tile(t + 1)
                        pe.wait_ge(evac, per * (t + 1))
                        if t >= 2:
                            pe.wait_ge(updated, t - 1)
                        for k in range(chunks):
                            mm = pe.matmul(bank(6 + t % 2, D), oT[:, t % 2, k, :], w[:, k, :],
                                           start=(k == 0), stop=(k == chunks - 1))
                        mm.then_inc(summed, 1)

                @block.scalar
                def _(act):
                    for t in range(count):
                        act.wait_ge(turned, chunks * (t + 1))
                        if t >= 2:
                            act.wait_ge(summed, t - 1)
                        for i in range(per):
                            n = min(4, chunks - 4 * i)
                            act.activation(oT[:, t % 2, 4 * i:4 * i + n, :],
                                           bank(per * (t % 2) + i, n * P).rearrange("p (k q) -> p k q", q=P),
                                           ACT.Copy).then_inc(evac, 1)

                @block.vector
                def _(dve):
                    for t in range(count):
                        dve.wait_ge(summed, t + 1)
                        dve.scalar_tensor_tensor(out=x[:, c0 + t, :], in0=bank(6 + t % 2, D), scalar=tg[:, gate:gate + 1],
                                                 in1=x[:, c0 + t, :], op0=ALU.mult, op1=ALU.add).then_inc(updated, 1)

        def project_T_stage(name, oT, w, group, chunks, gate):
            with stage(name, 2) as (block, (summed, updated)):
                @block.tensor
                def _(pe):
                    loaded(pe, group)
                    for t in range(T):
                        if t >= 4:
                            pe.wait_ge(updated, t - 3)
                        for k in range(chunks):
                            mm = pe.matmul(bank(t % 4, D), oT[:, k, tok(t)], w[:, k, :],
                                           start=(k == 0), stop=(k == chunks - 1))
                        mm.then_inc(summed, 1)

                @block.vector
                def _(dve):
                    for t in range(T):
                        dve.wait_ge(summed, t + 1)
                        dve.scalar_tensor_tensor(out=x[:, t, :], in0=bank(t % 4, D), scalar=tg[:, gate:gate + 1],
                                                 in1=x[:, t, :], op0=ALU.mult, op1=ALU.add).then_inc(updated, 1)

        def halves(h):
            return (slice(64 * (h % 2), 64 * (h % 2) + 64), slice(64 - 64 * (h % 2), 128 - 64 * (h % 2)))

        NPT = 4

        def probs(n):
            return xn[:, 2 * (n % NPT):2 * (n % NPT) + 2, :].rearrange("p t d -> p (t d)")

        def load_stage(b):
            with stage("load", 11) as (block, (xs, cs, ms, stated, added, powed, normed, masked, turned,
                                               evac, rep)), ExitStack() as tmp:
                c_tok = sb("c_tok", [M, C], stack=tmp)
                c_nrm = sb("c_nrm", [M, C], stack=tmp)
                st = sb("cst", [M, 6], stack=tmp)
                mv = sb("cmv", [M, 2], stack=tmp)
                rs = sb("crs", [M, 2], stack=tmp)
                col_u8 = sb("col_u8", [M, 1], U8, stack=tmp)
                row_u8 = sb("row_u8", [1, M], U8, stack=tmp)

                @block.sync
                def _(sp):
                    sp.dma_start(c_tok[:, :], a["ctx_768"][bass.ds(b, 1), :, :].rearrange("o m c -> (o m) c")
                                 ).then_inc(cs, 16)
                    sp.dma_start(col_u8[:, :], a["mask"][bass.ds(b, 1), :].rearrange("o m -> m o")
                                 ).then_inc(ms, 16)
                    sp.dma_start(row_u8[:, :], a["mask"][bass.ds(b, 1), :]).then_inc(ms, 16)
                    sp.dma_start(x[:, :, :], a["x"][bass.ds(b, 1), :, :].rearrange("o (t p) d -> p (o t) d", p=P)
                                 ).then_inc(xs, 16)
                    sp.wait_ge(xs, 16)

                @block.vector
                def _(dve):
                    dve.wait_ge(cs, 16)
                    dve.bn_stats(st[:, :], c_tok[:, :]).then_inc(stated, 1)
                    dve.wait_ge(stated, 1)
                    dve.bn_aggr(mv[:, :], st[:, :]).then_inc(stated, 1)
                    dve.wait_ge(powed, 1)
                    dve.tensor_scalar(c_nrm[:, :], c_tok[:, :], mv[:, 0:1], rs[:, 1:2], ALU.subtract,
                                      ALU.mult).then_inc(normed, 1)
                    dve.wait_ge(ms, 32)
                    dve.tensor_scalar(mask_col[:, :], col_u8[:, :], 1.0, LOW, ALU.subtract,
                                      ALU.mult).then_inc(masked, 1)
                    dve.tensor_scalar(mask_row[:, :], row_u8[:, :], 1.0, LOW, ALU.subtract,
                                      ALU.mult).then_inc(masked, 1)
                    dve.wait_ge(evac, 2)
                    dve.tensor_copy(ctx_rep[:, 0, :].rearrange("p (h m) -> p h m", m=M),
                                    ctxT[:, 0, :].unsqueeze(1).to_broadcast([P, HG, M])).then_inc(rep, 1)
                    dve.tensor_copy(ctx_rep[0:C1 + 1, 1, :].rearrange("p (h m) -> p h m", m=M),
                                    ctxT[0:C1 + 1, 1, :].unsqueeze(1).to_broadcast([C1 + 1, HG, M])
                                    ).then_inc(rep, 1)

                @block.gpsimd
                def _(pool):
                    pool.wait_ge(stated, 2)
                    pool.tensor_scalar(rs[:, 0:1], mv[:, 1:2], EPS, None, ALU.add).then_inc(added, 1)
                    pool.wait_ge(added, 1)
                    pool.tensor_tensor(rs[:, 1:2], rs[:, 0:1], neg_half[0:M, 0:1], ALU.pow).then_inc(powed, 1)

                @block.tensor
                def _(pe):
                    pe.wait_ge(cs, 16)
                    pe.transpose(bank(0, M), c_tok[:, 0:P], ident[0:M, 0:M])
                    pe.transpose(bank(1, M)[0:C1, :], c_tok[:, P:C], ident[0:M, 0:M]).then_inc(turned, 1)
                    pe.wait_ge(normed, 1)
                    pe.transpose(bank(2, M), c_nrm[:, 0:P], ident[0:M, 0:M])
                    pe.transpose(bank(3, M)[0:C1, :], c_nrm[:, P:C], ident[0:M, 0:M]).then_inc(turned, 1)

                @block.scalar
                def _(act):
                    act.wait_ge(turned, 1)
                    act.activation(ctxT[:, 0, :], bank(0, M), ACT.Copy).then_inc(evac, 1)
                    act.activation(ctxT[0:C1, 1, :], bank(1, M)[0:C1, :], ACT.Copy).then_inc(evac, 1)
                    act.wait_ge(turned, 2)
                    act.activation(cnT[:, 0, :], bank(2, M), ACT.Identity, bias=col("ln_x_b", 0),
                                   scale=col("ln_x_g", 0)).then_inc(evac, 1)
                    act.activation(cnT[0:C1, 1, :], bank(3, M)[0:C1, :], ACT.Identity,
                                   bias=col("ln_x_b", 1)[0:C1, :], scale=col("ln_x_g", 1)[0:C1, :]).then_inc(evac, 1)

        NK0 = T + 1
        KEYS0 = S + M

        def key_rows(j):
            return P if j < T else M

        def qkv0_stage(qT, kT, qTb, kTb, v_aug):
            with stage("qkv0", 11) as (block, (qk_done, v_done, squared, summed, floored, powed, normed, turned,
                                               evac, v_evac, cleared)), ExitStack() as tmp:
                sq = xn[:, 0:4, :].rearrange("p (i z) d -> p i (z d)", i=2)
                qk = xn[:, 4:8, :].rearrange("p (i z) d -> p i (z d)", i=2)
                ss = sb("ss", [P, NK0, 2 * H0], stack=tmp)
                fl = sb("fl", [P, NK0, 2 * H0], stack=tmp)
                ri = sb("ri", [P, NK0, 2 * H0], stack=tmp)
                v_pairs = v_aug[:, :, :, :].rearrange("p j (k i) (z d) -> p (j k) (i z) d", i=2, z=2)
                QB = 3

                def qk_bank(j):
                    return bank((0, 1, 6)[j % QB])

                @block.tensor
                def _(pe):
                    loaded(pe, "w0")

                    def turn_tile(j):
                        n = key_rows(j)
                        pe.wait_ge(normed, j + 1)
                        if j >= 2:
                            pe.wait_ge(evac, j - 1)
                        first = 0 if j < T else DK
                        for i in range(first, 2 * DK):
                            mm = pe.transpose(bank(4 + j % 2)[:, i * P:i * P + n], qk[0:n, j % 2, tok(i)],
                                              ident[0:n, 0:n])
                        mm.then_inc(turned, 1)
                    for j in range(NK0):
                        if j >= QB:
                            pe.wait_ge(normed, j - QB + 1)
                            pe.wait_ge(squared, j - QB + 1)
                        if j >= 2:
                            pe.wait_ge(v_evac, j - 1)
                        if j < T:
                            for k in range(DK):
                                mm = pe.matmul(qk_bank(j), xT[:, k, tok(j)], w0_qkv[:, k, 0:2 * D],
                                               start=(k == 0), stop=(k == DK - 1))
                            mm.then_inc(qk_done, 1)
                            for k in range(DK):
                                mm = pe.matmul(bank(2 + j % 2, D), xT[:, k, tok(j)], w0_qkv[:, k, 2 * D:3 * D],
                                               start=(k == 0), stop=(k == DK - 1))
                            mm.then_inc(v_done, 1)
                        else:
                            for k, r in enumerate((P, C1)):
                                mm = pe.matmul(qk_bank(j)[0:M, D:2 * D], cnT[0:r, k, :], w0_ckv[0:r, k, 0:D],
                                               start=(k == 0), stop=(k == 1))
                            mm.then_inc(qk_done, 1)
                            for k, r in enumerate((P, C1)):
                                mm = pe.matmul(bank(2 + j % 2)[0:M, 0:D], cnT[0:r, k, :], w0_ckv[0:r, k, D:2 * D],
                                               start=(k == 0), stop=(k == 1))
                            mm.then_inc(v_done, 1)
                        if j >= 2:
                            turn_tile(j - 2)
                    turn_tile(NK0 - 2)
                    turn_tile(NK0 - 1)

                @block.scalar
                def _(act):
                    def evacuate(j):
                        act.wait_ge(turned, j + 1)
                        n = key_rows(j)
                        both = bank(4 + j % 2).rearrange("p (i q) -> p i q", q=P)[:, :, 0:n]
                        if j < T:
                            act.activation(qT[:, :, tok(j)], both[:, 0:DK, :], ACT.Identity,
                                           scale=col("qn_g"), bias=0.0)
                        for i in range(2):
                            r = slice(DH0 * i, DH0 * (i + 1))
                            op = act.activation(kT[r, i::2, j * P:j * P + n], both[r, DK:2 * DK, :], ACT.Identity,
                                                scale=col("kn_g")[r, :], bias=0.0)
                        op.then_inc(evac, 1)
                    for j in range(NK0):
                        n = key_rows(j)
                        lo = 0 if j < T else D
                        act.wait_ge(qk_done, j + 1)
                        if j >= 2:
                            act.wait_ge(summed, j - 1)
                        act.activation(sq[0:n, j % 2, lo:], qk_bank(j)[0:n, lo:], ACT.Square).then_inc(squared, 1)
                        act.wait_ge(v_done, j + 1)
                        act.activation(v_pairs[0:n, j * DK:(j + 1) * DK, 0::3, :],
                                       bank(2 + j % 2, D)[0:n, :].rearrange("p (k i d) -> p k i d", i=2, d=DH0),
                                       ACT.Copy).then_inc(v_evac, 1)
                        if j >= 2:
                            evacuate(j - 2)
                    evacuate(NK0 - 2)
                    evacuate(NK0 - 1)

                @block.vector
                def _(dve):
                    def scale_tile(j):
                        n = key_rows(j)
                        h = 0 if j < T else H0
                        dve.wait_ge(powed, j + 1)
                        if j >= 2:
                            dve.wait_ge(turned, j - 1)
                        dve.tensor_tensor(qk[0:n, j % 2, h * DH0:].rearrange("p (h d) -> p h d", d=DH0),
                                          qk_bank(j)[0:n, h * DH0:].rearrange("p (h d) -> p h d", d=DH0),
                                          ri[0:n, j, h:].unsqueeze(2).to_broadcast([n, 2 * H0 - h, DH0]),
                                          ALU.mult).then_inc(normed, 1)

                    def bf_tile(j):
                        n = key_rows(j)
                        dve.wait_ge(evac, j + 1)
                        if j < T:
                            dve.tensor_copy(qTb[:, :, tok(j)], qT[:, :, tok(j)])
                        for i in range(2):
                            r = slice(DH0 * i, DH0 * (i + 1))
                            dve.tensor_copy(kTb[r, :, j * P:j * P + n], kT[r, i::2, j * P:j * P + n])
                    dve.memset(v_pairs[:, :, 1:3, :], 1.0)
                    for j in range(NK0):
                        n = key_rows(j)
                        h = 0 if j < T else H0
                        dve.wait_ge(squared, j + 1)
                        dve.tensor_reduce(ss[0:n, j, h:], sq[0:n, j % 2, h * DH0:].rearrange("p (h d) -> p h d", d=DH0),
                                          AX.X, ALU.add).then_inc(summed, 1)
                        if j:
                            scale_tile(j - 1)
                        if j >= 3:
                            bf_tile(j - 3)
                    scale_tile(NK0 - 1)
                    for j in range(NK0 - 3, NK0):
                        bf_tile(j)

                @block.gpsimd
                def _(pool):
                    for i in range(2):
                        pool.memset(kT[DH0 * (1 - i):DH0 * (2 - i), i::2, :], 0.0).then_inc(cleared, 1)
                    pool.wait_ge(cleared, 2)
                    for j in range(NK0):
                        n = key_rows(j)
                        h = 0 if j < T else H0
                        pool.wait_ge(summed, j + 1)
                        pool.tensor_scalar(fl[0:n, j, h:], ss[0:n, j, h:], 1.0 / DH0, 1e-16, ALU.mult,
                                           ALU.max).then_inc(floored, 1)
                        pool.wait_ge(floored, j + 1)
                        pool.tensor_tensor(ri[0:n, j, h:], fl[0:n, j, h:], neg_half[0:n, h:2 * H0],
                                           ALU.pow).then_inc(powed, 1)

        def attend0_stage(qT, kT, qTb, kTb, v_aug, oT):
            with stage("attend0", 9) as (block, (scored, maxed, turned, shifted, sdone, edone, pv, ok,
                                                 recd)), ExitStack() as tmp:
                mx = sb("mx", [P, 2, TB], stack=tmp)
                shift = sb("shift", [1, 2, BLK], BF16, stack=tmp)
                rc = sb("rc", [P, BLK], stack=tmp)
                UNITS = H0 * NB
                R = NK0 + 1

                def unit(u):
                    return divmod(u, NB)

                def ring(u, j):
                    return bank(3 + (u * R + j + 1) % 3)

                @block.tensor
                def _(pe):
                    def score_max(u, q):
                        h, c = unit(u)
                        t = c * TB + q
                        r, k = slice(DH0 * (h % 2), DH0 * (h % 2 + 1)), h // 2
                        if u * TB + q:
                            pe.wait_ge(maxed, u * TB + q)
                        for lo in range(0, KEYS0, 512):
                            w = min(512, KEYS0 - lo)
                            mm = pe.matmul(psum[:, lo:lo + w], qTb[r, k, tok(t)], kTb[r, k, lo:lo + w],
                                           start=True, stop=(w == 512))
                        mm = pe.matmul(psum[:, S:S + M], ones_bf[0:1, :], mask_row[0:1, :],
                                       start=False, stop=True)
                        mm.then_inc(scored, 1)

                    def bank_free(u, j):
                        turn_ = u * R + j + 1 - 3
                        if turn_ < 0:
                            return
                        v, i = divmod(turn_, R)
                        if i == 0:
                            pe.wait_ge(shifted, v + 1)
                        else:
                            pe.wait_ge(edone, v * NK0 + i)

                    def turn_max(u):
                        pe.wait_ge(maxed, TB * (u + 1))
                        bank_free(u, -1)
                        for q in range(TB):
                            mm = pe.transpose(ring(u, -1)[0:1, tok(q)], mx[:, u % 2, q:q + 1], ident[:, :])
                        mm.then_inc(turned, 1)

                    def scores(u, j):
                        h, c = unit(u)
                        w = key_rows(j)
                        if j == 0:
                            pe.wait_ge(shifted, u + 1)
                        bank_free(u, j)
                        pe.matmul(ring(u, j)[0:w, :], kT[:, h, j * P:j * P + w], qT[:, h // 2, blk(c)],
                                  start=True, stop=False)
                        pe.matmul(ring(u, j)[0:w, :], ones_bf[0:1, 0:w], shift[:, u % 2, :],
                                  start=False, stop=True).then_inc(sdone, 1)

                    def values(u, j):
                        h = unit(u)[0]
                        n = u * NK0 + j
                        w = key_rows(j)
                        pe.wait_ge(edone, n + 1)
                        if j == 0 and u >= 2:
                            pe.wait_ge(ok, u - 1)
                        pe.matmul(bank(6 + u % 2), v_aug[0:w, j, h, :], probs(n)[0:w, :],
                                  start=(j == 0), stop=(j == NK0 - 1)).then_inc(pv, 1)
                    for q in range(TB):
                        score_max(0, q)
                    turn_max(0)
                    for n in range(UNITS * NK0 + 2):
                        u, j = divmod(n, NK0)
                        if u < UNITS:
                            scores(u, j)
                        if n >= 2:
                            values(*divmod(n - 2, NK0))
                        if u + 1 < UNITS and j % 2 == 1:
                            score_max(u + 1, j // 2)
                        if u + 1 < UNITS and j == NK0 - 1:
                            turn_max(u + 1)

                @block.scalar
                def _(act):
                    for n in range(UNITS * NK0):
                        u, j = divmod(n, NK0)
                        w = key_rows(j)
                        act.wait_ge(sdone, n + 1)
                        if n >= NPT:
                            act.wait_ge(pv, n - NPT + 1)
                        act.activation(probs(n)[0:w, :], ring(u, j)[0:w, :], ACT.Exp,
                                       scale=float(DH0) ** -0.5,
                                       bias=(mask_col[:, 0:1] if j == T else 0.0)).then_inc(edone, 1)

                @block.vector
                def _(dve):
                    def find_shift(u):
                        for q in range(TB):
                            dve.wait_ge(scored, u * TB + q + 1)
                            dve.tensor_reduce(mx[:, u % 2, q:q + 1], psum[:, 0:KEYS0], AX.X,
                                              ALU.max).then_inc(maxed, 1)
                        dve.wait_ge(turned, u + 1)
                        dve.tensor_scalar(shift[:, u % 2, :], ring(u, -1)[0:1, :], -1.0, None,
                                          ALU.mult).then_inc(shifted, 1)

                    def outputs(u):
                        h, c = unit(u)
                        dve.wait_ge(pv, NK0 * (u + 1))
                        mine, sums = halves(h)
                        if u:
                            dve.wait_ge(ok, u)
                        dve.reciprocal(rc[mine, :], bank(6 + u % 2)[sums, :]).then_inc(recd, 1)
                        dve.wait_ge(recd, u + 1)
                        dve.tensor_tensor(oT[mine, h // 2, blk(c)], bank(6 + u % 2)[mine, :], rc[mine, :],
                                          ALU.mult).then_inc(ok, 1)
                    find_shift(0)
                    for u in range(UNITS):
                        if u + 1 < UNITS:
                            find_shift(u + 1)
                        outputs(u)

        def first_largest(chain, dve, value, onehot, best, order):
            def over(v):
                return v.unsqueeze(2).to_broadcast([P, T, E])
            chain(dve.tensor_reduce(best, value, AX.X, ALU.max))
            chain(dve.tensor_tensor(onehot, value, over(best), ALU.is_equal))
            chain(dve.tensor_tensor(onehot, onehot, rank[:, :, :], ALU.mult))
            chain(dve.tensor_reduce(order, onehot, AX.X, ALU.max))
            chain(dve.tensor_tensor(onehot, onehot, over(order), ALU.is_equal))

        def over(v):
            return v.unsqueeze(2).to_broadcast([P, T, E])

        def chained(dve, step):
            count = [0]

            def chain(op):
                count[0] += 1
                op.then_inc(step, 1)
                dve.wait_ge(step, count[0])
                return count[0]
            return chain

        def moe0_stage():
            with stage("moe0", 10) as (block, (logged, centred, exped, step, weighted, turned, wt_ready,
                                               mm_done, added, bias_done)), ExitStack() as tmp:
                lg = sb("lg", [P, T, E], stack=tmp)
                ex = sb("ex", [P, T, E], stack=tmp)
                onehot = sb("onehot", [P, T, E], stack=tmp)
                wt = sb("wt", [P, T, E], stack=tmp)
                s1 = sb("s1", [P, 5, T], stack=tmp)
                wT = sb("wT", [E, T, P], stack=tmp)
                PAIRS = E // 2
                NBK = 5

                @block.tensor
                def _(pe):
                    loaded(pe, "e0")
                    for t in range(T):
                        for k in range(DK):
                            mm = pe.matmul(bank(6)[:, E * t:E * (t + 1)], xT[:, k, tok(t)], r0[:, k, :],
                                           start=(k == 0), stop=(k == DK - 1))
                    mm.then_inc(logged, 1)
                    for t in range(T):
                        for p in range(PAIRS):
                            n = t * PAIRS + p
                            if n >= NBK:
                                pe.wait_ge(added, 2 * (n - NBK + 1))
                            for k in range(DK):
                                mm = pe.matmul(bank(n % NBK), xT[:, k, tok(t)], e0[:, k, 512 * p:512 * (p + 1)],
                                               start=(k == 0), stop=(k == DK - 1))
                            mm.then_inc(mm_done, 1)
                        if t == 0:
                            pe.wait_ge(weighted, 1)
                            for u in range(T):
                                mm = pe.transpose(bank(5 if u < TB else 7)[0:E, tok(u % TB)], wt[:, u, :],
                                                  ident[:, :])
                            mm.then_inc(turned, 1)
                    pe.wait_ge(wt_ready, 2)
                    for t in range(T):
                        if t >= 2:
                            pe.wait_ge(added, 2 * T * PAIRS + t - 1)
                        pe.matmul(bank(5 + t % 2, D), wT[:, t, :], e0_b[:, :], start=True,
                                  stop=True).then_inc(bias_done, 1)

                @block.scalar
                def _(act):
                    act.wait_ge(centred, 1)
                    act.activation(ex[:, :, :], lg[:, :, :], ACT.Exp).then_inc(exped, 1)
                    act.wait_ge(turned, 1)
                    act.activation(wT[:, 0:TB, :], bank(5)[0:E, :].rearrange("p (t q) -> p t q", q=P),
                                   ACT.Copy).then_inc(wt_ready, 1)
                    act.activation(wT[:, TB:T, :], bank(7)[0:E, :].rearrange("p (t q) -> p t q", q=P),
                                   ACT.Copy).then_inc(wt_ready, 1)

                @block.vector
                def _(dve):
                    chain = chained(dve, step)
                    total, inverse, best, order, gate = (s1[:, i, :] for i in range(5))
                    dve.wait_ge(logged, 1)
                    chain(dve.tensor_tensor(lg[:, :, :], bank(6, T * E).rearrange("p (t e) -> p t e", e=E),
                                            cols[:, COLS["rb0"]:COLS["rb0"] + E].unsqueeze(1).to_broadcast([P, T, E]),
                                            ALU.add))
                    chain(dve.tensor_reduce(total, lg[:, :, :], AX.X, ALU.max))
                    dve.tensor_tensor(lg[:, :, :], lg[:, :, :], over(total), ALU.subtract).then_inc(centred, 1)
                    dve.wait_ge(exped, 1)
                    chain(dve.tensor_reduce(total, ex[:, :, :], AX.X, ALU.add))
                    chain(dve.reciprocal(inverse, total))
                    first_largest(chain, dve, ex[:, :, :], onehot[:, :, :], best, order)
                    chain(dve.tensor_tensor(gate, inverse, best, ALU.mult))
                    chain(dve.tensor_scalar(gate, gate, tg[:, 4:5], None, ALU.mult))
                    dve.tensor_tensor(wt[:, :, :], onehot[:, :, :], over(gate), ALU.mult).then_inc(weighted, 1)
                    dve.wait_ge(weighted, 1)
                    for t in range(T):
                        for e in range(E):
                            n = t * E + e
                            dve.wait_ge(mm_done, n // 2 + 1)
                            if e:
                                dve.wait_ge(added, n)
                            dve.scalar_tensor_tensor(out=x[:, t, :], in0=bank(n // 2 % NBK)[:, e % 2 * D:(e % 2 + 1) * D],
                                                     scalar=wt[:, t, e:e + 1], in1=x[:, t, :],
                                                     op0=ALU.mult, op1=ALU.add).then_inc(added, 1)
                    dve.wait_ge(added, T * E)
                    for t in range(T):
                        dve.wait_ge(bias_done, t + 1)
                        dve.tensor_tensor(x[:, t, :], bank(5 + t % 2, D), x[:, t, :], ALU.add).then_inc(added, 1)

        def moe1_stage():
            with stage("moe1", 12) as (block, (logged, centred, exped, step, weighted, up_done, silued, gated_h,
                                               turned, evac, down, updated)), ExitStack() as tmp:
                lg = sb("lg", [P, T, E], stack=tmp)
                ex = sb("ex", [P, T, E], stack=tmp)
                one1 = sb("one1", [P, T, E], stack=tmp)
                one2 = sb("one2", [P, T, E], stack=tmp)
                wt = sb("wt", [P, T, E], stack=tmp)
                s1 = sb("s1", [P, 5, T], stack=tmp)
                sl = sb("sl", [P, 2, 2, P], stack=tmp)
                gh = sb("gh", [P, 2, 2, P], stack=tmp)
                gT = sb("gT", [P, 2, 2, P], stack=tmp)
                PAIRS = E // 2
                N = T * PAIRS

                @block.tensor
                def _(pe):
                    loaded(pe, "e1")
                    for t in range(T):
                        for k in range(DK):
                            mm = pe.matmul(bank(7)[:, E * t:E * (t + 1)], xT[:, k, tok(t)], r1[:, k, :],
                                           start=(k == 0), stop=(k == DK - 1))
                    mm.then_inc(logged, 1)

                    def up(n):
                        t, p = divmod(n, PAIRS)
                        if n >= 3:
                            pe.wait_ge(gated_h, n - 2)
                        for k in range(DK):
                            mm = pe.matmul(bank(n % 3), xT[:, k, tok(t)], e1_up[:, k, 512 * p:512 * (p + 1)],
                                           start=(k == 0), stop=(k == DK - 1))
                        mm.then_inc(up_done, 1)

                    def turn_pair(n):
                        pe.wait_ge(gated_h, n + 1)
                        if n >= 2:
                            pe.wait_ge(evac, n - 1)
                        for i in range(2):
                            mm = pe.transpose(bank(3 + n % 2)[:, tok(i)], gh[:, n % 2, i, :], ident[:, :])
                        mm.then_inc(turned, 1)

                    def down_pair(n):
                        t, p = divmod(n, PAIRS)
                        pe.wait_ge(evac, n + 1)
                        if p == 0 and t >= 2:
                            pe.wait_ge(updated, t - 1)
                        for i in range(2):
                            mm = pe.matmul(bank(5 + t % 2, D), gT[:, n % 2, i, :], e1_down[:, 2 * p + i, :],
                                           start=(p == 0 and i == 0), stop=(p == PAIRS - 1 and i == 1))
                        mm.then_inc(down, 1)
                    for n in range(N + 3):
                        if n < N:
                            up(n)
                        if 2 <= n < N + 2:
                            turn_pair(n - 2)
                        if n >= 3:
                            down_pair(n - 3)

                @block.scalar
                def _(act):
                    act.wait_ge(centred, 1)
                    act.activation(ex[:, :, :], lg[:, :, :], ACT.Exp).then_inc(exped, 1)
                    act.wait_ge(weighted, 1)

                    def evacuate(n):
                        act.wait_ge(turned, n + 1)
                        if n >= 2:
                            act.wait_ge(down, n - 1)
                        act.activation(gT[:, n % 2, :, :], bank(3 + n % 2, D).rearrange("p (i q) -> p i q", q=P),
                                       ACT.Copy).then_inc(evac, 1)
                    for n in range(N + 2):
                        if n < N:
                            t, p = divmod(n, PAIRS)
                            act.wait_ge(up_done, n + 1)
                            if n >= 2:
                                act.wait_ge(gated_h, n - 1)
                            for i in range(2):
                                e = 2 * p + i
                                act.activation(sl[:, n % 2, i, :], bank(n % 3)[:, i * D:i * D + P], ACT.Silu,
                                               scale=wt[:, t, e:e + 1]).then_inc(silued, 1)
                        if n >= 2:
                            evacuate(n - 2)

                @block.vector
                def _(dve):
                    chain = chained(dve, step)
                    total, inverse, best, order, gate = (s1[:, i, :] for i in range(5))
                    dve.wait_ge(logged, 1)
                    chain(dve.tensor_copy(lg[:, :, :], bank(7, T * E).rearrange("p (t e) -> p t e", e=E)))
                    chain(dve.tensor_reduce(total, lg[:, :, :], AX.X, ALU.max))
                    dve.tensor_tensor(lg[:, :, :], lg[:, :, :], over(total), ALU.subtract).then_inc(centred, 1)
                    dve.wait_ge(exped, 1)
                    chain(dve.tensor_reduce(total, ex[:, :, :], AX.X, ALU.add))
                    chain(dve.reciprocal(inverse, total))
                    first_largest(chain, dve, ex[:, :, :], one1[:, :, :], best, order)
                    chain(dve.scalar_tensor_tensor(out=lg[:, :, :], in0=one1[:, :, :], scalar=-4.0,
                                                   in1=ex[:, :, :], op0=ALU.mult, op1=ALU.add))
                    first_largest(chain, dve, lg[:, :, :], one2[:, :, :], best, order)
                    chain(dve.tensor_tensor(one1[:, :, :], one1[:, :, :], one2[:, :, :], ALU.add))
                    chain(dve.tensor_tensor(one1[:, :, :], one1[:, :, :], ex[:, :, :], ALU.mult))
                    dve.tensor_tensor(wt[:, :, :], one1[:, :, :], over(inverse), ALU.mult).then_inc(weighted, 1)
                    dve.wait_ge(weighted, 1)

                    def update(t):
                        dve.wait_ge(down, PAIRS * (t + 1))
                        dve.scalar_tensor_tensor(out=x[:, t, :], in0=bank(5 + t % 2, D), scalar=tg[:, 5:6],
                                                 in1=x[:, t, :], op0=ALU.mult, op1=ALU.add).then_inc(updated, 1)
                    for n in range(N):
                        t, p = divmod(n, PAIRS)
                        dve.wait_ge(silued, 2 * (n + 1))
                        if n >= 2:
                            dve.wait_ge(turned, n - 1)
                        for i in range(2):
                            e = 2 * p + i
                            op = dve.scalar_tensor_tensor(out=gh[:, n % 2, i, :],
                                                          in0=bank(n % 3)[:, i * D + P:(i + 1) * D],
                                                          scalar=wt[:, t, e:e + 1], in1=sl[:, n % 2, i, :],
                                                          op0=ALU.mult, op1=ALU.mult)
                        op.then_inc(gated_h, 1)
                        if n >= PAIRS + 2 and n % PAIRS == 2:
                            update(t - 1)
                    update(T - 1)

        VW = HG * (DH1 + 1)

        def small_prepare_stage(name, group, wq, wk, wv, bq, qT, qTb, kbd, kbdb, vbig):
            with stage(name, 7) as (block, (q_done, q_evac, k_done, k_evac, v_done, v_evac, ones_done)), \
                    ExitStack() as tmp:
                @block.tensor
                def _(pe):
                    loaded(pe, group)
                    for g in range(G):
                        for kc, r in enumerate((P, C1 + 1)):
                            mm = pe.matmul(bank(6 + g, M), wk[0:r, kc, tok(g)], ctxT[0:r, kc, :],
                                           start=(kc == 0), stop=(kc == 1))
                        mm.then_inc(k_done, 1)
                    for i in range(G * NB):
                        g, c = divmod(i, NB)
                        if i >= 2:
                            pe.wait_ge(q_evac, i - 1)
                        for k in range(DK):
                            mm = pe.matmul(bank(i % 2), wq[:, k, tok(g)], xT[:, k, blk(c)],
                                           start=(k == 0), stop=(k == DK - 1))
                        mm.then_inc(q_done, 1)
                    for ch, (lo, w) in enumerate(CH):
                        if ch >= 2:
                            pe.wait_ge(v_evac, ch - 1)
                        for kc, r in enumerate((P, C1 + 1)):
                            mm = pe.matmul(bank(2 + ch % 2)[0:w, 0:D], ctx_rep[0:r, kc, lo:lo + w], wv[0:r, kc, :],
                                           start=(kc == 0), stop=(kc == 1))
                        mm.then_inc(v_done, 1)

                @block.scalar
                def _(act):
                    for i in range(G * NB):
                        g, c = divmod(i, NB)
                        act.wait_ge(q_done, i + 1)
                        act.activation(qT[:, g, blk(c)], bank(i % 2), ACT.Identity,
                                       bias=col(bq, g)).then_inc(q_evac, 1)

                @block.vector
                def _(dve):
                    for g in range(G):
                        dve.wait_ge(k_done, g + 1)
                        dve.tensor_tensor(kbd[:, g, :].rearrange("p (h m) -> p h m", m=M),
                                          bank(6 + g, M).unsqueeze(1).to_broadcast([P, HG, M]),
                                          head_of_feature[:, :].unsqueeze(2).to_broadcast([P, HG, M]),
                                          ALU.mult).then_inc(k_evac, 1)
                    for ch, (lo, w) in enumerate(CH):
                        dve.wait_ge(v_done, ch + 1)
                        v = vbig[0:w, ch, :, :].rearrange("p g (h d) -> p g h d", d=DH1 + 1)
                        for g in range(G):
                            op = dve.tensor_tensor(v[:, g, :, 0:DH1],
                                                   bank(2 + ch % 2)[0:w, g * P:(g + 1) * P].rearrange(
                                                       "p (h d) -> p h d", d=DH1),
                                                   head_of_row[0:w, ch, :].unsqueeze(2).to_broadcast([w, HG, DH1]),
                                                   ALU.mult)
                        op.then_inc(v_evac, 1)
                    dve.wait_ge(k_evac, G)
                    for g in range(G):
                        dve.tensor_copy(kbdb[:, g, :], kbd[:, g, :])

                @block.gpsimd
                def _(pool):
                    for g in range(G):
                        pool.tensor_copy(vbig[:, :, g, DH1::DH1 + 1], head_of_row[:, :, :])
                    for i in range(G * NB):
                        g, c = divmod(i, NB)
                        pool.wait_ge(q_evac, i + 1)
                        pool.tensor_copy(qTb[:, g, blk(c)], qT[:, g, blk(c)])

        def small_shift_stage(name, qTb, kbdb, shift, clip):
            with stage(name, 5) as (block, (scored, maxed, capped, turned, shifted)), ExitStack() as tmp:
                mx = sb("mx", [P, T, H1], stack=tmp)
                HALF = GM // 2

                @block.tensor
                def _(pe):
                    for t in range(T):
                        for g in range(G):
                            n = G * t + g
                            if n >= 3:
                                pe.wait_ge(maxed, n - 2)
                            for i in range(2):
                                mm = pe.matmul(bank(2 * (n % 3) + i, HALF), qTb[:, g, tok(t)],
                                               kbdb[:, g, i * HALF:(i + 1) * HALF], start=True, stop=True)
                            mm.then_inc(scored, 1)
                        if t % TB == TB - 1:
                            c = t // TB
                            pe.wait_ge(capped if clip else maxed, c + 1 if clip else G * (t + 1))
                            for u in tiles_of(c):
                                mm = pe.transpose(bank(6 + c)[0:H1, tok(u % TB)], mx[:, u, :], ident[:, :])
                            mm.then_inc(turned, 1)

                @block.vector
                def _(dve):
                    for t in range(T):
                        for g in range(G):
                            n = G * t + g
                            dve.wait_ge(scored, n + 1)
                            r = psum[:, 1024 * (n % 3):1024 * (n % 3) + 1024].rearrange("p (i z) -> p i z", i=2)
                            dve.tensor_reduce(mx[:, t, HG * g:HG * (g + 1)].rearrange("p (i h) -> p i h", i=2),
                                              r[:, :, 0:HALF].rearrange("p i (h m) -> p i h m", m=M),
                                              AX.X, ALU.max).then_inc(maxed, 1)
                        if clip and t % TB == TB - 1:
                            bound = CLAMP * float(DH1) ** 0.5
                            now = mx[:, t - TB + 1:t + 1, :]
                            dve.wait_ge(maxed, G * (t + 1))
                            dve.tensor_scalar(now, now, bound, -bound, ALU.min, ALU.max).then_inc(capped, 1)

                @block.scalar
                def _(act):
                    for c in range(NB):
                        act.wait_ge(turned, c + 1)
                        act.activation(shift[:, blk(c)], bank(6 + c)[0:H1, :], ACT.Copy,
                                       scale=-1.0).then_inc(shifted, 1)

        def small_attend_stage(name, qT, kbd, vbig, shift, o_tok):
            with stage(name, 5) as (block, (sdone, edone, pv, recd, ok)), ExitStack() as tmp:
                NPT = 4
                pt = sb("pt", [P, NPT, BLK], stack=tmp)
                rc = sb("rc", [P, 2, TB, HG], stack=tmp)
                N = G * len(CH)

                def where(n):
                    c, i = divmod(n, N)
                    g, ch = divmod(i, len(CH))
                    return c, g, ch

                @block.tensor
                def _(pe):
                    def scores(n):
                        c, g, ch = where(n)
                        lo, w = CH[ch]
                        if n >= 4:
                            pe.wait_ge(edone, n - 3)
                        pe.matmul(bank(n % 4)[0:w, :], kbd[:, g, lo:lo + w], qT[:, g, blk(c)],
                                  start=True, stop=False)
                        pe.matmul(bank(n % 4)[0:w, :], pick_row[:, g, lo:lo + w], shift[:, blk(c)],
                                  start=False, stop=True).then_inc(sdone, 1)

                    def values(n):
                        c, g, ch = where(n)
                        lo, w = CH[ch]
                        u = c * G + g
                        pe.wait_ge(edone, n + 1)
                        if ch == 0 and u >= 2:
                            pe.wait_ge(ok, u - 1)
                        for q in range(TB):
                            mm = pe.matmul(bank(4 + 2 * (u % 2) + q // 2)[:, VW * (q % 2):VW * (q % 2 + 1)],
                                           pt[0:w, n % NPT, tok(q)], vbig[0:w, ch, g, :],
                                           start=(ch == 0 and q % 2 == 0), stop=(ch == len(CH) - 1),
                                           skip_group_check=True)
                        mm.then_inc(pv, 1)
                    for n in range(NB * N + 2):
                        if n < NB * N:
                            scores(n)
                        if n >= 2:
                            values(n - 2)

                @block.scalar
                def _(act):
                    for n in range(NB * N):
                        c, g, ch = where(n)
                        w = CH[ch][1]
                        act.wait_ge(sdone, n + 1)
                        if n >= NPT:
                            act.wait_ge(pv, n - NPT + 1)
                        act.activation(pt[0:w, n % NPT, :], bank(n % 4)[0:w, :], ACT.Exp,
                                       scale=float(DH1) ** -0.5).then_inc(edone, 1)

                @block.vector
                def _(dve):
                    for u in range(NB * G):
                        c, g = divmod(u, G)
                        dve.wait_ge(pv, len(CH) * (u + 1))
                        for i in range(2):
                            o = bank(4 + 2 * (u % 2) + i, 2 * VW).rearrange("p (q h d) -> p q h d", q=2, d=DH1 + 1)
                            r = rc[:, u % 2, 2 * i:2 * i + 2, :]
                            dve.reciprocal(r.unsqueeze(3), o[:, :, :, DH1:]).then_inc(recd, 1)
                            dve.wait_ge(recd, 2 * u + i + 1)
                            for q in range(2):
                                op = dve.tensor_tensor(
                                    o_tok[:, c * TB + 2 * i + q, g * P:(g + 1) * P].rearrange(
                                        "p (h d) -> p h d", d=DH1),
                                    o[:, q, :, 0:DH1], r[:, q, :].unsqueeze(2).to_broadcast([P, HG, DH1]), ALU.mult)
                        op.then_inc(ok, 1)

        def clipped_attend_stage(name, qT, kbd, vbig, shift, o_tok):
            with stage(name, 7) as (block, (sdone, clipped, shifted, edone, pv, recd, ok)), ExitStack() as tmp:
                NPT = 4
                sc = sb("sc", [P, NPT, BLK], stack=tmp)
                pt = sb("pt", [P, NPT, BLK], stack=tmp)
                rc = sb("rc", [P, 2, TB, HG], stack=tmp)
                N = G * len(CH)
                BOUND = CLAMP * float(DH1) ** 0.5

                def where(n):
                    c, i = divmod(n, N)
                    g, ch = divmod(i, len(CH))
                    return c, g, ch

                @block.tensor
                def _(pe):
                    def scores(n):
                        c, g, ch = where(n)
                        lo, w = CH[ch]
                        if n >= 2:
                            pe.wait_ge(shifted, n - 1)
                        pe.matmul(bank(n % 2)[0:w, :], kbd[:, g, lo:lo + w], qT[:, g, blk(c)],
                                  start=True, stop=True)
                        pe.matmul(bank(2 + n % 2)[0:w, :], pick_row[:, g, lo:lo + w], shift[:, blk(c)],
                                  start=True, stop=True).then_inc(sdone, 1)

                    def values(n):
                        c, g, ch = where(n)
                        lo, w = CH[ch]
                        u = c * G + g
                        pe.wait_ge(edone, n + 1)
                        if ch == 0 and u >= 2:
                            pe.wait_ge(ok, u - 1)
                        for q in range(TB):
                            mm = pe.matmul(bank(4 + 2 * (u % 2) + q // 2)[:, VW * (q % 2):VW * (q % 2 + 1)],
                                           pt[0:w, n % NPT, tok(q)], vbig[0:w, ch, g, :],
                                           start=(ch == 0 and q % 2 == 0), stop=(ch == len(CH) - 1),
                                           skip_group_check=True)
                        mm.then_inc(pv, 1)
                    for n in range(NB * N + 3):
                        if n < NB * N:
                            scores(n)
                        if n >= 3:
                            values(n - 3)

                @block.scalar
                def _(act):
                    for n in range(NB * N):
                        c, g, ch = where(n)
                        w = CH[ch][1]
                        act.wait_ge(shifted, n + 1)
                        if n >= NPT:
                            act.wait_ge(pv, n - NPT + 1)
                        act.activation(pt[0:w, n % NPT, :], sc[0:w, n % NPT, :], ACT.Exp,
                                       scale=float(DH1) ** -0.5).then_inc(edone, 1)

                @block.vector
                def _(dve):
                    def normalise(u):
                        c, g = divmod(u, G)
                        dve.wait_ge(pv, len(CH) * (u + 1))
                        for i in range(2):
                            o = bank(4 + 2 * (u % 2) + i, 2 * VW).rearrange("p (q h d) -> p q h d", q=2, d=DH1 + 1)
                            r = rc[:, u % 2, 2 * i:2 * i + 2, :]
                            dve.reciprocal(r.unsqueeze(3), o[:, :, :, DH1:]).then_inc(recd, 1)
                            dve.wait_ge(recd, 2 * u + i + 1)
                            for q in range(2):
                                op = dve.tensor_tensor(
                                    o_tok[:, c * TB + 2 * i + q, g * P:(g + 1) * P].rearrange(
                                        "p (h d) -> p h d", d=DH1),
                                    o[:, q, :, 0:DH1], r[:, q, :].unsqueeze(2).to_broadcast([P, HG, DH1]), ALU.mult)
                        op.then_inc(ok, 1)
                    total = NB * N

                    def subtract(n):
                        w = CH[where(n)[2]][1]
                        dve.wait_ge(clipped, n + 1)
                        dve.tensor_tensor(sc[0:w, n % NPT, :], sc[0:w, n % NPT, :], bank(2 + n % 2)[0:w, :],
                                          ALU.add).then_inc(shifted, 1)
                    for n in range(total):
                        w = CH[where(n)[2]][1]
                        dve.wait_ge(sdone, n + 1)
                        if n >= NPT:
                            dve.wait_ge(edone, n - NPT + 1)
                        dve.tensor_scalar(sc[0:w, n % NPT, :], bank(n % 2)[0:w, :], BOUND, -BOUND,
                                          ALU.min, ALU.max).then_inc(clipped, 1)
                        if n:
                            subtract(n - 1)
                        if n >= len(CH) + 3 and (n - 3) % len(CH) == 0:
                            normalise((n - 3) // len(CH) - 1)
                    subtract(total - 1)
                    normalise(NB * G - 1)

        KC2 = H2 * DH2 // P

        def kv2_stage(kT, kTb, v_aug):
            with stage("kv2", 5) as (block, (k_done, k_evac, v_done, v_evac, cleared)):
                @block.tensor
                def _(pe):
                    loaded(pe, "w2")
                    for j in range(KC2):
                        for kc, r in enumerate((P, C1)):
                            mm = pe.matmul(bank(j // 4)[:, (j % 4) * M:(j % 4 + 1) * M], w2_kv[0:r, kc, tok(j)],
                                           ctxT[0:r, kc, :], start=(kc == 0), stop=(kc == 1))
                    mm.then_inc(k_done, 1)
                    for i in range(2):
                        for kc, r in enumerate((P, C1)):
                            mm = pe.matmul(bank(2 + i)[0:M, :], ctxT[0:r, kc, :],
                                           w2_kv[0:r, kc, H2 * DH2 + 512 * i:H2 * DH2 + 512 * (i + 1)],
                                           start=(kc == 0), stop=(kc == 1))
                        mm.then_inc(v_done, 1)

                @block.scalar
                def _(act):
                    act.wait_ge(k_done, 1)
                    for i in range(2):
                        for p in range(2):
                            r = slice(DH2 * p, DH2 * (p + 1))
                            act.activation(kT[r, 8 * i + p:8 * i + 8:2, :],
                                           bank(i, 4 * M)[r, :].rearrange("p (j m) -> p j m", m=M),
                                           ACT.Copy).then_inc(k_evac, 1)

                @block.vector
                def _(dve):
                    for p in range(2):
                        dve.memset(kT[DH2 * (1 - p):DH2 * (2 - p), p::2, :], 0.0)
                    dve.wait_ge(cleared, 1)
                    for i in range(2):
                        dve.wait_ge(v_done, i + 1)
                        dve.tensor_copy(v_aug[0:M, 8 * i:8 * i + 8, 0:DH2],
                                        bank(2 + i)[0:M, :].rearrange("p (h d) -> p h d", d=DH2)).then_inc(v_evac, 1)

                @block.gpsimd
                def _(pool):
                    pool.memset(v_aug[:, :, :], 1.0).then_inc(cleared, 1)
                    pool.memset(xn[:, :, :], 0.0).then_inc(cleared, 1)
                    pool.wait_ge(cleared, 2)
                    pool.wait_ge(k_evac, 4)
                    for p in range(2):
                        r = slice(DH2 * p, DH2 * (p + 1))
                        pool.tensor_copy(kTb[r, :, :], kT[r, p::2, :]).then_inc(cleared, 1)
                    pool.wait_ge(cleared, 4)

        def attend2_stage(kT, kTb, v_aug):
            with stage("attend2", 17) as (block, (q_done, q_evac, q_bf, scored, maxed, turned, shifted, sdone,
                                                  edone, pv, recd, ok, o_turned, o_low, o_high, summed,
                                                  updated)), ExitStack() as tmp:
                qT = sb("qT2", [P, 3, BLK], stack=tmp)
                qTb = sb("qTb2", [P, 3, BLK], BF16, stack=tmp)
                o_tok = sb("o2", [P, TB, H2 * DH2], stack=tmp)
                oT = sb("oT2", [P, 2, KC2, P], stack=tmp)
                mx = sb("mx", [P, TB, 2], stack=tmp)
                shift = sb("shift", [2, BLK], BF16, stack=tmp)
                rc = sb("rc", [P, 2, TB], stack=tmp)
                UNITS = NB * KC2
                KH = KC2 // 2

                @block.tensor
                def _(pe):
                    def queries(u):
                        c, k = divmod(u, KC2)
                        if u:
                            pe.wait_ge(q_evac, u)
                        if u > KC2 and u % KC2 == 2:
                            pe.wait_ge(o_low, TB * (u // KC2))
                        for kc in range(DK):
                            mm = pe.matmul(bank(0), w2_q[:, kc, tok(k)], xT[:, kc, blk(c)],
                                           start=(kc == 0), stop=(kc == DK - 1))
                        mm.then_inc(q_done, 1)

                    def score_max(u):
                        k = u % KC2
                        pe.wait_ge(q_bf, u + 1)
                        for i in range(2):
                            r = halves(i)[0]
                            if u:
                                pe.wait_ge(maxed, 2 * (u - 1) + i + 1)
                            for t in range(TB):
                                mm = pe.matmul(bank(1 + i)[:, t * M:(t + 1) * M], qTb[r, u % 3, tok(t)],
                                               kTb[r, k, :], start=True, stop=True, skip_group_check=True)
                            mm.then_inc(scored, 1)

                    def turn_max(u):
                        pe.wait_ge(maxed, 2 * (u + 1))
                        if u:
                            pe.wait_ge(shifted, u)
                        if u > KC2 and u % KC2 == 1:
                            pe.wait_ge(o_high, TB * (u // KC2))
                        for t in range(TB):
                            mm = pe.transpose(bank(3)[0:2, tok(t)], mx[:, t, :], ident[:, :])
                        mm.then_inc(turned, 1)

                    def scores(u, i):
                        k = u % KC2
                        n = 2 * u + i
                        if i == 0:
                            pe.wait_ge(shifted, u + 1)
                        if n >= 2:
                            pe.wait_ge(edone, n - 1)
                        pe.matmul(bank(4 + i)[0:M, :], kT[:, 2 * k + i, :], qT[:, u % 3, :], start=True, stop=False)
                        pe.matmul(bank(4 + i)[0:M, :], pick2[:, i, :], shift[:, :], start=False,
                                  stop=True).then_inc(sdone, 1)

                    def values(u, i):
                        n = 2 * u + i
                        pe.wait_ge(edone, n + 1)
                        if n >= 2:
                            pe.wait_ge(ok, n - 1)
                        if u >= KC2 and u % KC2 == 0:
                            pe.wait_ge(updated, TB * (u // KC2))
                        for q in range(TB):
                            mm = pe.matmul(bank(6 + i)[:, q * (DH2 + 1):(q + 1) * (DH2 + 1)], probs(n)[:, tok(q)],
                                           v_aug[:, 2 * (u % KC2) + i, :], start=True, stop=True)
                        mm.then_inc(pv, 1)

                    def turn_tile(t):
                        if t:
                            pe.wait_ge(o_low, t)
                            pe.wait_ge(o_high, t)
                        for k in range(KC2):
                            mm = pe.transpose(bank(0 if k < KH else 3)[:, tok(k % KH)], o_tok[:, t % TB, tok(k)],
                                              ident[:, :])
                            if k % KH == KH - 1:
                                mm.then_inc(o_turned, 1)

                    def project(c):
                        pe.wait_ge(ok, 2 * KC2 * (c + 1))
                        pe.wait_ge(q_evac, min(UNITS, KC2 * (c + 1) + 2))
                        pe.wait_ge(shifted, min(UNITS, KC2 * (c + 1) + 1))
                        turn_tile(c * TB)
                        for t in tiles_of(c):
                            if t % TB + 1 < TB:
                                turn_tile(t + 1)
                            pe.wait_ge(o_low, t + 1)
                            pe.wait_ge(o_high, t + 1)
                            if t >= 2:
                                pe.wait_ge(updated, t - 1)
                            for k in range(KC2):
                                mm = pe.matmul(bank(6 + t % 2, D), oT[:, t % 2, k, :], w2_o[:, k, :],
                                               start=(k == 0), stop=(k == KC2 - 1))
                            mm.then_inc(summed, 1)
                    loaded(pe, "w2")
                    queries(0)
                    queries(1)
                    score_max(0)
                    turn_max(0)
                    for u in range(UNITS):
                        scores(u, 0)
                        if u + 1 < UNITS:
                            score_max(u + 1)
                        scores(u, 1)
                        if u and u % KC2 == 0:
                            project(u // KC2 - 1)
                        values(u, 0)
                        if u + 2 < UNITS:
                            queries(u + 2)
                        if u + 1 < UNITS:
                            turn_max(u + 1)
                        values(u, 1)
                    project(NB - 1)

                @block.scalar
                def _(act):
                    def queries(u):
                        act.wait_ge(q_done, u + 1)
                        if u >= 3:
                            act.wait_ge(sdone, 2 * (u - 2))
                            act.wait_ge(q_bf, u - 2)
                        act.activation(qT[:, u % 3, :], bank(0), ACT.Copy).then_inc(q_evac, 1)

                    def shift_rows(u):
                        act.wait_ge(turned, u + 1)
                        if u:
                            act.wait_ge(sdone, 2 * u)
                        act.activation(shift[:, :], bank(3)[0:2, :], ACT.Copy, scale=-1.0).then_inc(shifted, 1)
                    def low_half(c):
                        for t in tiles_of(c):
                            act.wait_ge(o_turned, 2 * t + 1)
                            if t >= 2:
                                act.wait_ge(summed, t - 1)
                            act.activation(oT[:, t % 2, 0:KH, :], bank(0).rearrange("p (k q) -> p k q", q=P),
                                           ACT.Copy).then_inc(o_low, 1)
                    queries(0)
                    queries(1)
                    shift_rows(0)
                    for u in range(UNITS):
                        for i in range(2):
                            n = 2 * u + i
                            act.wait_ge(sdone, n + 1)
                            if n >= NPT:
                                act.wait_ge(pv, n - NPT + 1)
                            act.activation(probs(n)[0:M, :], bank(4 + i)[0:M, :], ACT.Exp,
                                           scale=float(DH2) ** -0.5).then_inc(edone, 1)
                        if u and u % KC2 == 0:
                            low_half(u // KC2 - 1)
                        if u + 2 < UNITS:
                            queries(u + 2)
                        if u + 1 < UNITS:
                            shift_rows(u + 1)
                    low_half(NB - 1)

                @block.gpsimd
                def _(pool):
                    for u in range(UNITS):
                        pool.wait_ge(q_evac, u + 1)
                        if u >= 3:
                            pool.wait_ge(scored, 2 * (u - 2))
                        pool.tensor_copy(qTb[:, u % 3, :], qT[:, u % 3, :]).then_inc(q_bf, 1)

                @block.vector
                def _(dve):
                    def largest(u):
                        for i in range(2):
                            dve.wait_ge(scored, 2 * u + i + 1)
                            if u:
                                dve.wait_ge(turned, u)
                            dve.tensor_reduce(mx[:, :, i], bank(1 + i, TB * M).rearrange("p (t m) -> p t m", m=M),
                                              AX.X, ALU.max).then_inc(maxed, 1)

                    def outputs(u, i):
                        n = 2 * u + i
                        k = u % KC2
                        dve.wait_ge(pv, n + 1)
                        if n >= 2:
                            dve.wait_ge(ok, n - 1)
                        o = bank(6 + i, TB * (DH2 + 1)).rearrange("p (q d) -> p q d", d=DH2 + 1)
                        dve.reciprocal(rc[:, i, :].unsqueeze(2), o[:, :, DH2:]).then_inc(recd, 1)
                        dve.wait_ge(recd, n + 1)
                        dve.tensor_tensor(o_tok[:, :, (2 * k + i) * DH2:(2 * k + i + 1) * DH2], o[:, :, 0:DH2],
                                          rc[:, i, :].unsqueeze(2).to_broadcast([P, TB, DH2]),
                                          ALU.mult).then_inc(ok, 1)

                    def high_half(t):
                        dve.wait_ge(o_turned, 2 * t + 2)
                        if t >= 2:
                            dve.wait_ge(summed, t - 1)
                        dve.tensor_copy(oT[:, t % 2, KH:KC2, :], bank(3).rearrange("p (k q) -> p k q", q=P)
                                        ).then_inc(o_high, 1)

                    def update(c):
                        high_half(c * TB)
                        for t in tiles_of(c):
                            if t % TB + 1 < TB:
                                high_half(t + 1)
                            dve.wait_ge(summed, t + 1)
                            dve.scalar_tensor_tensor(out=x[:, t, :], in0=bank(6 + t % 2, D), scalar=tg[:, 2:3],
                                                     in1=x[:, t, :], op0=ALU.mult, op1=ALU.add).then_inc(updated, 1)
                    largest(0)
                    for u in range(UNITS):
                        if u + 1 < UNITS:
                            largest(u + 1)
                        if u and u % KC2 == 0:
                            update(u // KC2 - 1)
                        outputs(u, 0)
                        outputs(u, 1)
                    update(NB - 1)

        def lora_stage():
            with stage("lora", 4) as (block, (a_done, a_evac, summed, updated)), ExitStack() as tmp:
                lowT = sb("lowT", [16, NB, BLK], stack=tmp)

                @block.tensor
                def _(pe):
                    loaded(pe, "lora")
                    for c in range(NB):
                        for k in range(DK):
                            mm = pe.matmul(bank(c)[0:16, :], lora_a[:, k, :], xT[:, k, blk(c)],
                                           start=(k == 0), stop=(k == DK - 1))
                        mm.then_inc(a_done, 1)
                    for t in range(T):
                        if t >= 4:
                            pe.wait_ge(updated, t - 3)
                        for k in range(DK):
                            pe.matmul(bank(2 + t % 4, D), xT[:, k, tok(t)], wq8[:, k, :], start=(k == 0), stop=False)
                        pe.wait_ge(a_evac, t // TB + 1)
                        pe.matmul(bank(2 + t % 4, D), lowT[:, t // TB, tok(t % TB)], lora_b[:, :], start=False,
                                  stop=True).then_inc(summed, 1)

                @block.scalar
                def _(act):
                    for c in range(NB):
                        act.wait_ge(a_done, c + 1)
                        act.activation(lowT[:, c, :], bank(c)[0:16, :], ACT.Copy).then_inc(a_evac, 1)

                @block.vector
                def _(dve):
                    for t in range(T):
                        dve.wait_ge(summed, t + 1)
                        dve.scalar_tensor_tensor(out=x[:, t, :], in0=bank(2 + t % 4, D), scalar=tg[:, 6:7],
                                                 in1=x[:, t, :], op0=ALU.mult, op1=ALU.add).then_inc(updated, 1)

        def mlp3_stage(o_tok):
            with stage("mlp3", 6) as (block, (turned, evac, h_done, h_evac, summed, updated)), ExitStack() as tmp:
                oT = sb("oT", [P, DK, S], stack=tmp)
                hT = sb("hT", [P, 2 * DK, BLK], stack=tmp)
                HC = 2 * DK

                @block.tensor
                def _(pe):
                    loaded(pe, "w3")
                    for c in range(NB):
                        for k in range(DK):
                            for t in tiles_of(c):
                                mm = pe.transpose(bank(DK * c + k)[:, tok(t % TB)], o_tok[:, t, tok(k)], ident[:, :])
                            mm.then_inc(turned, 1)
                    for c in range(NB):
                        pe.wait_ge(evac, DK * (c + 1))
                        for m in range(HC):
                            n = c * HC + m
                            if n >= 2:
                                pe.wait_ge(h_evac, n - 1)
                            for k in range(DK):
                                mm = pe.matmul(bank(4 + n % 2), w3_1[:, k, tok(m)], oT[:, k, blk(c)],
                                               start=(k == 0), stop=(k == DK - 1))
                            mm.then_inc(h_done, 1)
                        pe.wait_ge(h_evac, HC * (c + 1))
                        for t in tiles_of(c):
                            if t >= 2:
                                pe.wait_ge(updated, t - 1)
                            for m in range(HC):
                                mm = pe.matmul(bank(6 + t % 2, D), hT[:, m, tok(t % TB)], w3_2[:, m, :],
                                               start=(m == 0), stop=(m == HC - 1))
                            mm.then_inc(summed, 1)

                @block.scalar
                def _(act):
                    for c in range(NB):
                        for k in range(DK):
                            act.wait_ge(turned, DK * c + k + 1)
                            act.activation(oT[:, k, blk(c)], bank(DK * c + k), ACT.Copy).then_inc(evac, 1)
                    for c in range(NB):
                        if c:
                            act.wait_ge(summed, TB * c)
                        for m in range(HC):
                            n = c * HC + m
                            act.wait_ge(h_done, n + 1)
                            act.activation(hT[:, m, :], bank(4 + n % 2), ACT.Relu, bias=col("b1_3", m)
                                           ).then_inc(h_evac, 1)

                @block.vector
                def _(dve):
                    for t in range(T):
                        dve.wait_ge(summed, t + 1)
                        dve.scalar_tensor_tensor(out=x[:, t, :], in0=bank(6 + t % 2, D), scalar=tg[:, 3:4],
                                                 in1=x[:, t, :], op0=ALU.mult, op1=ALU.add).then_inc(updated, 1)

        def dispatch_stage(b):
            with stage("dispatch", 9) as (block, (logged, centred, exped, step, chosen, counted, kept_x, placed,
                                                   saved)), ExitStack() as tmp:
                lg = sb("lg", [P, T, E], stack=tmp)
                ex = sb("ex", [P, T, E], stack=tmp)
                onehot = sb("onehot", [P, T, E], stack=tmp)
                before = sb("before", [P, T + 1, E], stack=tmp)
                cum = sb("cum", [P, T, E], stack=tmp)
                s1 = sb("s1", [P, 8, T], stack=tmp)
                to = sb("to", [P, T], U32, stack=tmp)

                @block.sync
                def _(sp):
                    sp.dma_start(residual.rearrange("(b t p) d -> b p t d", p=P, t=T)[bass.ds(b, 1)]
                                 .rearrange("o p t d -> p (o t) d"), x[:, :, :]).then_inc(saved, 16)
                    sp.wait_ge(saved, 16)

                @block.tensor
                def _(pe):
                    loaded(pe, "w3")
                    for t in range(T):
                        for k in range(DK):
                            mm = pe.matmul(bank(6)[:, E * t:E * (t + 1)], xT[:, k, tok(t)], r3[:, k, :],
                                           start=(k == 0), stop=(k == DK - 1))
                    mm.then_inc(logged, 1)
                    pe.wait_ge(chosen, 1)
                    flat = onehot[:, :, :].rearrange("p t e -> p (t e)")
                    pe.matmul(bank(0, T * E), upper[:, :], flat, start=True, stop=True)
                    pe.matmul(bank(1, T * E), ones_f[:, :], flat, start=True, stop=True).then_inc(counted, 1)

                @block.scalar
                def _(act):
                    act.wait_ge(centred, 1)
                    act.activation(ex[:, :, :], lg[:, :, :], ACT.Exp).then_inc(exped, 1)

                @block.vector
                def _(dve):
                    chain = chained(dve, step)
                    total, inverse, best, order, base, pos, kept, far = (s1[:, i, :] for i in range(8))
                    dve.wait_ge(logged, 1)
                    chain(dve.tensor_copy(lg[:, :, :], bank(6, T * E).rearrange("p (t e) -> p t e", e=E)))
                    chain(dve.tensor_reduce(total, lg[:, :, :], AX.X, ALU.max))
                    dve.tensor_tensor(lg[:, :, :], lg[:, :, :], over(total), ALU.subtract).then_inc(centred, 1)
                    dve.wait_ge(exped, 1)
                    chain(dve.tensor_reduce(total, ex[:, :, :], AX.X, ALU.add))
                    chain(dve.reciprocal(inverse, total))
                    first_largest(chain, dve, ex[:, :, :], onehot[:, :, :], best, order)
                    dve.tensor_copy(before[:, 0, :], taken[:, :]).then_inc(chosen, 1)
                    dve.wait_ge(chosen, 1)
                    dve.wait_ge(counted, 1)
                    for t in range(T):
                        chain(dve.tensor_tensor(before[:, t + 1, :], before[:, t, :], bank(1)[:, E * t:E * (t + 1)],
                                                ALU.add))
                    chain(dve.tensor_copy(taken[:, :], before[:, T, :]))
                    chain(dve.tensor_tensor(cum[:, :, :], before[:, 0:T, :],
                                            bank(0, T * E).rearrange("p (t e) -> p t e", e=E), ALU.add))
                    chain(dve.tensor_tensor(cum[:, :, :], cum[:, :, :], onehot[:, :, :], ALU.mult))
                    chain(dve.tensor_reduce(pos, cum[:, :, :], AX.X, ALU.add))
                    chain(dve.tensor_scalar(pos, pos, 1.0, None, ALU.subtract))
                    chain(dve.tensor_scalar(base, order, -float(CAP), float(E * CAP), ALU.mult, ALU.add))
                    chain(dve.tensor_scalar(kept, pos, float(CAP), None, ALU.is_lt))
                    chain(dve.tensor_scalar(far, kept, -FAR, FAR, ALU.mult, ALU.add))
                    chain(dve.tensor_tensor(far, far, base, ALU.add))
                    chain(dve.tensor_tensor(far, far, pos, ALU.add))
                    dve.tensor_copy(to[:, :], far).then_inc(placed, 1)
                    chain(dve.tensor_scalar(pos, pos, float(CAP - 1), None, ALU.min))
                    chain(dve.tensor_tensor(pos, pos, base, ALU.add))
                    dve.tensor_copy(slot[:, bass.ds(b * T, T)], pos).then_inc(kept_x, 1)
                    chain(dve.tensor_tensor(best, best, inverse, ALU.mult))
                    chain(dve.tensor_tensor(best, best, kept, ALU.mult))
                    chain(dve.tensor_scalar(best, best, tg[:, 7:8], None, ALU.mult))
                    dve.tensor_copy(prob[:, bass.ds(b * T, T)], best).then_inc(kept_x, 1)

                @block.gpsimd
                def _(pool):
                    pool.wait_ge(placed, 1)
                    for t in range(T):
                        pool.indirect_dma_start(out=slots_in, out_offset=bass.IndirectOffsetOnAxis(
                            ap=to[:, t:t + 1], axis=0), in_=xn[:, t, :], in_offset=None,
                            bounds_check=SLOTS - 1, oob_is_err=False).then_inc(sent, 16)
                    pool.wait_ge(sent, b * (16 * T) + 16 * T)

        def expert_stage(e, bufs, mine, nxt):
            w1, w2, b1, b2, tk = bufs[mine]
            with stage("expert", 8) as (block, (loading, turned, evac, up_done, gelued, down, biased, stored)), \
                    ExitStack() as tmp:
                tT = sb("tT", [P, DK, CAP], stack=tmp)
                hT = sb("hT", [P, FC, CAP], stack=tmp)
                eo = sb("eo", [P, CT, D], stack=tmp)
                HALF = CAP // 2
                HT = HALF // P

                @block.sync
                def _(sp):
                    if nxt is not None:
                        expert_loads(sp, nxt, bufs[1 - mine], loading)
                    for t in range(CT):
                        sp.wait_ge(biased, t + 1)
                        sp.dma_start(slots_out.rearrange("(e t p) d -> e t p d", e=E, p=P)[bass.ds(e, 1), t]
                                     .rearrange("o p d -> (o p) d"), eo[:, t, :]).then_inc(stored, 16)
                    sp.wait_ge(stored, 16 * CT)
                    if nxt is not None:
                        sp.wait_ge(loading, 16 * 5)

                @block.tensor
                def _(pe):
                    for half in range(2):
                        for k in range(DK):
                            for t in range(HT):
                                mm = pe.transpose(bank(2 * half + k)[:, tok(t)], tk[:, half * HT + t, tok(k)],
                                                  ident[:, :])
                            mm.then_inc(turned, 1)
                    for half in range(2):
                        pe.wait_ge(evac, DK * (half + 1))
                        for f in range(FC):
                            n = half * FC + f
                            if n >= 2:
                                pe.wait_ge(gelued, n - 1)
                            for k in range(DK):
                                mm = pe.matmul(bank(4 + n % 2, HALF), w1[:, k, tok(f)],
                                               tT[:, k, half * HALF:(half + 1) * HALF],
                                               start=(k == 0), stop=(k == DK - 1))
                            mm.then_inc(up_done, 1)
                    for t in range(CT):
                        pe.wait_ge(gelued, FC * (t // HT + 1))
                        if t >= 2:
                            pe.wait_ge(biased, t - 1)
                        for f in range(FC):
                            mm = pe.matmul(bank(6 + t % 2, D), hT[:, f, tok(t)], w2[:, f, :],
                                           start=(f == 0), stop=(f == FC - 1))
                        mm.then_inc(down, 1)

                @block.scalar
                def _(act):
                    for n in range(2 * FC):
                        half, f = divmod(n, FC)
                        act.wait_ge(up_done, n + 1)
                        act.activation(hT[:, f, half * HALF:(half + 1) * HALF], bank(4 + n % 2, HALF), ACT.Gelu,
                                       bias=b1[:, f:f + 1]).then_inc(gelued, 1)

                @block.vector
                def _(dve):
                    for i in range(2 * DK):
                        half, k = divmod(i, DK)
                        dve.wait_ge(turned, i + 1)
                        dve.tensor_copy(tT[:, k, half * HALF:(half + 1) * HALF], bank(i, HALF)).then_inc(evac, 1)
                    for t in range(CT):
                        dve.wait_ge(down, t + 1)
                        dve.tensor_tensor(eo[:, t, :], bank(6 + t % 2, D), b2[:, :], ALU.add).then_inc(biased, 1)

        def expert_loads(sp, e, buf, loading):
            w1, w2, b1, b2, tk = buf
            def of(ap):
                return ap[bass.ds(e, 1)] if not isinstance(e, int) else ap[e:e + 1]
            sp.dma_start(tk[:, :, :], of(slots_in.rearrange("(e t p) d -> e p t d", e=E, p=P))
                         .rearrange("o p t d -> p (o t) d")).then_inc(loading, 16)
            sp.dma_start(w1[:, :, :], of(a["L3_ffn_w1"]).rearrange("o (k p) f -> p (o k) f", p=P)).then_inc(loading, 16)
            sp.dma_start(b1[:, :], of(a["b1_cols"]).rearrange("o p f -> (o p) f")).then_inc(loading, 16)
            sp.dma_start(w2[:, :, :], of(a["L3_ffn_w2"]).rearrange("o (f p) d -> p (o f) d", p=P)).then_inc(loading, 16)
            sp.dma_start(b2[:, :], of(a["L3_ffn_b2"]).to_broadcast([P, D])).then_inc(loading, 16)

        def combine_stage(b):
            with stage("combine", 4) as (block, (xs, indexed, summed, stored)), ExitStack() as tmp:
                got = sb("got", [P, T, D], stack=tmp)
                idx = sb("idx", [P, T], U32, stack=tmp)
                pr = sb("pr", [P, T], stack=tmp)
                of_batch = "(b t p) d -> b p t d"

                @block.sync
                def _(sp):
                    sp.dma_start(x[:, :, :], residual.rearrange(of_batch, p=P, t=T)[bass.ds(b, 1)]
                                 .rearrange("o p t d -> p (o t) d")).then_inc(xs, 16)
                    sp.wait_ge(summed, T)
                    sp.dma_start(out.rearrange(of_batch, p=P, t=T)[bass.ds(b, 1)]
                                 .rearrange("o p t d -> p (o t) d"), x[:, :, :]).then_inc(stored, 16)
                    sp.wait_ge(stored, 16)

                @block.vector
                def _(dve):
                    dve.tensor_copy(idx[:, :], slot[:, bass.ds(b * T, T)]).then_inc(indexed, 1)
                    dve.tensor_copy(pr[:, :], prob[:, bass.ds(b * T, T)]).then_inc(indexed, 1)
                    dve.wait_ge(indexed, 2)
                    dve.wait_ge(xs, 16)
                    for t in range(T):
                        dve.wait_ge(fetched[t], b * 16 + 16)
                        dve.scalar_tensor_tensor(out=x[:, t, :], in0=got[:, t, :], scalar=pr[:, t:t + 1],
                                                 in1=x[:, t, :], op0=ALU.mult, op1=ALU.add).then_inc(summed, 1)

                @block.gpsimd
                def _(pool):
                    pool.wait_ge(indexed, 1)
                    for t in range(T):
                        pool.indirect_dma_start(out=got[:, t, :], out_offset=None, in_=slots_out,
                                                in_offset=bass.IndirectOffsetOnAxis(ap=idx[:, t:t + 1], axis=0),
                                                bounds_check=SLOTS - 1, oob_is_err=True).then_inc(fetched[t], 16)

        def small_buffers(stack):
            return (sb("qT1", [P, G, S], stack=stack), sb("qTb1", [P, G, S], BF16, stack=stack),
                    sb("kbd", [P, G, GM], stack=stack), sb("kbdb", [P, G, GM], BF16, stack=stack),
                    sb("vbig", [P, len(CH), G, VW], stack=stack), sb("shift1", [H1, S], BF16, stack=stack))

        with nc.Fori(0, B) as b:
            at_start = turn[0]
            load_stage(b)
            norm_stage("norm0", bias_row="bo0", double=True)
            with ExitStack() as tmp:
                qT = sb("qT0", [P, DK, S], stack=tmp)
                kT = sb("kT0", [P, H0, KEYS0 + 3], stack=tmp)
                qTb = sb("qTb0", [P, DK, S], BF16, stack=tmp)
                kTb = sb("kTb0", [P, DK, KEYS0 + 3], BF16, stack=tmp)
                v_aug = sb("v0", [P, NK0, H0, 2 * DH0], stack=tmp)
                qkv0_stage(qT, kT, qTb, kTb, v_aug)
                attend0_stage(qT, kT, qTb, kTb, v_aug, xT)
            project_T_stage("project0", xT, w0_o, "w0", DK, 0)
            if upto > 1:
                norm_stage("norm1")
                moe0_stage()
            if upto > 2:
                norm_stage("norm2", bias_row="bo1")
                with ExitStack() as tmp:
                    small = small_buffers(tmp)
                    small_prepare_stage("prepare1", "w1", w1_q, w1_k, w1_v, "bq1", *small[:5])
                    small_shift_stage("shift1", small[1], small[3], small[5], True)
                    clipped_attend_stage("attend1", small[0], small[2], small[4], small[5], xn)
                project_stage("project1", xn, w1_o, "w1", DK, 1)
            if upto > 3:
                norm_stage("norm3")
                moe1_stage()
            if upto > 4:
                norm_stage("norm4", bias_row="bproj")
                with ExitStack() as tmp:
                    kT = sb("kT2", [P, H2, M], stack=tmp)
                    kTb = sb("kTb2", [P, KC2, M], BF16, stack=tmp)
                    v_aug = sb("v2", [P, H2, DH2 + 1], stack=tmp)
                    kv2_stage(kT, kTb, v_aug)
                    attend2_stage(kT, kTb, v_aug)
            if upto > 5:
                norm_stage("norm5", bias_row="bias2")
                lora_stage()
            if upto > 6:
                norm_stage("norm6", bias_row="b2_3")
                with ExitStack() as tmp:
                    small = small_buffers(tmp)
                    small_prepare_stage("prepare3", "w3", w3_q, w3_k, w3_v, "bq3", *small[:5])
                    small_shift_stage("shift3", small[1], small[3], small[5], False)
                    small_attend_stage("attend3", small[0], small[2], small[4], small[5], xn)
                mlp3_stage(xn)
            if upto > 7:
                norm_stage("norm7")
                dispatch_stage(b)
            else:
                with stage("dump", 1) as (block, (dumped,)):
                    @block.sync
                    def _(sp):
                        sp.dma_start(out.rearrange("(b t p) d -> b p t d", p=P, t=T)[bass.ds(b, 1)]
                                     .rearrange("o p t d -> p (o t) d"), x[:, :, :]).then_inc(dumped, 16)
                        sp.wait_ge(dumped, 16)
                        for group in loads:
                            loaded(sp, group)
            if turn[0] != at_start:
                with stage("even", 0):
                    pass
        if upto > 7:
            arena.close()
            with ExitStack() as tmp:
                bufs = [(sb(f"ew1_{i}", [P, DK, F3], stack=tmp), sb(f"ew2_{i}", [P, FC, D], stack=tmp),
                         sb(f"eb1_{i}", [P, FC], stack=tmp), sb(f"eb2_{i}", [P, D], stack=tmp),
                         sb(f"etk_{i}", [P, CT, D], stack=tmp)) for i in range(2)]
                with stage("first_expert", 1) as (block, (loading,)):
                    @block.sync
                    def _(sp):
                        expert_loads(sp, 0, bufs[0], loading)
                        sp.wait_ge(loading, 16 * 5)
                with nc.Fori(0, E // 2 - 1) as i:
                    expert_stage(i * 2, bufs, 0, i * 2 + 1)
                    expert_stage(i * 2 + 1, bufs, 1, i * 2 + 2)
                expert_stage(E - 2, bufs, 0, E - 1)
                expert_stage(E - 1, bufs, 1, None)
                with nc.Fori(0, B) as b:
                    combine_stage(b)
                    with stage("even2", 0):
                        pass


def kernel(**inputs):
    import numpy as np
    import concourse.bacc as bacc
    from concourse.bass_utils import run_bass_kernel_spmd

    arrays = layout(inputs)
    nc = bacc.Bacc("TRN2", target_bir_lowering=False, num_devices=1)
    args = {n: nc.dram_tensor("in_" + n, v.shape, mybir.dt.from_np(v.dtype), kind="ExternalInput").ap()
            for n, v in arrays.items()}
    out = nc.dram_tensor("out", [B * S, D], F32, kind="ExternalOutput").ap()
    flamingo_kernel(nc, args, out)
    r = run_bass_kernel_spmd(nc, [{"in_" + n: v for n, v in arrays.items()}], core_ids=[0])
    return r.results[0]["out"].reshape(B, S, D)


def layout(inputs):
    import numpy as np

    v = {n: np.asarray(i) for n, i in inputs.items()}
    out = {n: v[n] for n in (
        "x", "ctx_768", "L0_ffn_router_w", "L0_ffn_expert_w", "L0_ffn_expert_b", "L1_xattn_Wq", "L1_xattn_Wo",
        "L1_ffn_gate_w", "L1_ffn_w1", "L1_ffn_w2", "L1_ffn_w3", "L2_xattn_Wq", "L2_xattn_Wkv", "L2_xattn_Wproj",
        "L2_ffn_kernel", "L2_ffn_a", "L2_ffn_b", "L3_xattn_Wq", "L3_xattn_W1", "L3_xattn_W2", "L3_ffn_w1",
        "L3_ffn_w2", "L3_ffn_b2")}
    out["mask"] = v["mask_BxS2_bk0"]
    out["w0_qkv"] = np.concatenate([v["L0_xattn_Wq"], v["L0_xattn_Wlkv"]]).T
    out["w0_ckv"] = v["L0_xattn_Wkv"].T
    out["w0_o"] = v["L0_xattn_Wo"].T
    for i in (1, 3):
        for w in "kv":
            out[f"w{i}_{w}"] = np.concatenate([v[f"L{i}_xattn_W{w}"], v[f"L{i}_xattn_b{w}"][None]])
    out["r3"] = v["L3_ffn_router_w"].T
    out["b1_cols"] = v["L3_ffn_b1"].reshape(E, FC, P).transpose(0, 2, 1)

    def columns(vector):
        return np.pad(vector, (0, -len(vector) % P)).reshape(-1, P).T

    def same(vector):
        return np.broadcast_to(vector, (P, len(vector)))

    out["cols"] = np.concatenate([
        same(v["g_xattn"]), same(v["g_ffn"]), same(v["L0_ffn_router_b"]), columns(v["L0_xattn_ln_x_g"]),
        columns(v["L0_xattn_ln_x_b"]), columns(v["L0_xattn_ln_l_g"]), columns(v["L0_xattn_ln_l_b"]),
        columns(np.tile(v["L0_xattn_qn_g"], 2)), columns(np.tile(v["L0_xattn_kn_g"], 2)),
        columns(v["L1_xattn_bq"]), columns(v["L3_xattn_bq"]), columns(v["L3_xattn_b1"])], axis=1)
    out["rows"] = np.concatenate([same(v[n]) for n in (
        "L0_xattn_bo", "L1_xattn_bo", "L2_xattn_bproj", "L2_ffn_bias", "L3_xattn_b2")], axis=1)
    return {n: np.ascontiguousarray(i) for n, i in out.items()}
```

```python
from contextlib import ExitStack, contextmanager

import concourse.bass as bass
from concourse import mybir

F32 = mybir.dt.float32
F32R = mybir.dt.float32r
BF16 = mybir.dt.bfloat16
U8 = mybir.dt.uint8
U32 = mybir.dt.uint32
ALU = mybir.AluOpType
ACT = mybir.ActivationFunctionType
AX = mybir.AxisListType

P = 128
B, S, D = 4, 1024, 256
T = S // P
DK = D // P
BLK = 512
NB = S // BLK
TB = BLK // P
M = 77
C = 192
C1 = C - P
E = 8
H0, DH0 = 4, 64
H1, DH1 = 16, 16
H2, DH2 = 16, 64
G = DK
HG = H1 // G
GM = HG * M
CH = [(c * P, min(P, GM - c * P)) for c in range((GM + P - 1) // P)]
F3 = 1024
CAP = 768
CT = CAP // P
FC = F3 // P
SLOTS = E * CAP
FAR = 1.0e6
EPS = 1e-5
LOW = 1.0e30


COLS, at = {}, 0
for name, n in (("gates", 8), ("rb0", E), ("ln_x_g", 2), ("ln_x_b", 2), ("ln_l_g", 2), ("ln_l_b", 2), ("qn_g", 1),
                ("kn_g", 1), ("bq1", 2), ("bq3", 2), ("b1_3", 4)):
    COLS[name] = at
    at += n
GATED = (("bo0", 0), ("bo1", 1), ("bproj", 2), ("bias2", 6), ("b2_3", 3))
ROWS = {name: i for i, (name, _) in enumerate(GATED)}
CLAMP = 10000.0


def flamingo_kernel(nc, a, out):
    ctx = ExitStack()
    with ctx:
        named = []

        def sb(name, shape, dt=F32, stack=ctx):
            named.append(name)
            name = name if stack is ctx else f"{name}_{len(named)}"
            return stack.enter_context(nc.sbuf_tensor(name, shape, dt))

        def sem(name):
            return ctx.enter_context(nc.semaphore(name))

        psum = ctx.enter_context(nc.psum_tensor("psum", [P, 8 * 512], F32))

        def bank(i, n=512):
            return psum[:, 512 * i:512 * i + n]

        residual = nc.dram_tensor("residual", [B * S, D], F32, kind="Internal").ap()
        slots_in = nc.dram_tensor("slots_in", [SLOTS, D], F32, kind="Internal").ap()
        slots_out = nc.dram_tensor("slots_out", [SLOTS, D], F32, kind="Internal").ap()

        NSEM = 40
        sem_banks = [[sem(f"stage_{i}_{j}") for j in range(NSEM)] for i in range(2)]
        turn = [1]

        @contextmanager
        def stage(name, count):
            turn[0] ^= 1
            old = sem_banks[1 - turn[0]]
            named.append(name)
            with nc.Block(f"{name}_{len(named)}") as block:
                @block.sync
                def _(sp):
                    sp.sem_clear(range(old[0].num, old[-1].num + 1))
                yield block, sem_banks[turn[0]][:count]

        sent = sem("rows_sent")
        BEFORE = 16
        fetched = [sem(f"row_fetched_{t}") for t in range(2 * T)]

        loads = {}

        ident = sb("ident", [P, P])
        ones_bf = sb("ones_bf", [1, P], BF16)
        ones_f = sb("ones_f", [P, P])
        upper = sb("upper", [P, P])
        cols = sb("cols", list(a["cols"].shape))
        rows = sb("rows", list(a["rows"].shape))
        tg = sb("tg", [P, 8])
        neg_half = sb("neg_half", [P, 16])
        rank = sb("rank", [P, T, E])
        head_of_feature = sb("head_of_feature", [P, HG])
        head_of_row = sb("head_of_row", [P, len(CH), HG])
        pick_row = sb("pick_row", [H1, G, GM], BF16)
        pick2 = sb("pick2", [2, 2, M], BF16)
        mask_col = sb("mask_col", [M, 1])
        mask_row = sb("mask_row", [1, M], BF16)
        slot = sb("slot", [P, B * T], U32)
        prob = sb("prob", [P, B * T])
        zeros = sb("zeros", [P, P])
        st0 = sb("st0", [P, T, 6])
        mv0 = sb("mv0", [P, T, 2])
        taken = sb("taken", [P, E])

        x = sb("x", [P, T, D])
        xn = sb("xn", [P, T, D])
        xT = sb("xT", [P, DK, S])
        ctxT = sb("ctxT", [P, 2, M])
        cnT = sb("cnT", [P, 2, M])
        ctx_rep = sb("ctx_rep", [P, 2, GM])


        arena = ExitStack()
        ctx.enter_context(arena)

        def wsb(name, shape):
            return arena.enter_context(nc.sbuf_tensor(name, shape, F32))

        w0_qkv = wsb("w0_qkv", [P, DK, 3 * D])
        w0_ckv = wsb("w0_ckv", [P, 2, 2 * D])
        w0_o = wsb("w0_o", [P, DK, D])
        r0 = wsb("r0", [P, DK, E])
        e0_b = wsb("e0_b", [E, D])
        moe_w = wsb("moe_w", [P, DK, E * D])
        w1_q = wsb("w1_q", [P, DK, D])
        w1_k = wsb("w1_k", [P, 2, D])
        w1_v = wsb("w1_v", [P, 2, D])
        w1_o = wsb("w1_o", [P, DK, D])
        r1 = wsb("r1", [P, DK, E])
        e1_down = wsb("e1_down", [P, E, D])
        w2_q = wsb("w2_q", [P, DK, H2 * DH2])
        w2_kv = moe_w
        w2_o = wsb("w2_o", [P, H2 * DH2 // P, D])
        wq8 = wsb("wq8", [P, DK, D])
        lora_a = wsb("lora_a", [P, DK, 16])
        lora_b = wsb("lora_b", [16, D])
        w3_q = wsb("w3_q", [P, DK, D])
        w3_k = wsb("w3_k", [P, 2, D])
        w3_v = wsb("w3_v", [P, 2, D])
        w3_1 = wsb("w3_1", [P, DK, 2 * D])
        w3_2 = wsb("w3_2", [P, 2 * DK, D])
        r3 = wsb("r3", [P, DK, E])

        def col(name, k=0):
            return cols[:, COLS[name] + k:COLS[name] + k + 1]

        def row(name):
            return rows[:, ROWS[name] * D:(ROWS[name] + 1) * D]

        def load(eng, group, *pairs):
            loads[group] = (sem("load_" + group), 16 * len(pairs))
            for dst, src in pairs:
                eng.dma_start(dst, src).then_inc(loads[group][0], 16)

        def loaded(eng, group):
            eng.wait_ge(*loads[group])

        def chunked(dst, src):
            n = src.shape[0]
            if n % P == 0:
                return [(dst[:, :, :], src.rearrange("(k p) n -> p k n", p=P))]
            return [(dst[:, 0, :], src[0:P, :]), (dst[0:n - P, 1, :], src[P:n, :])]

        def tiles_of(c):
            return range(c * TB, (c + 1) * TB)

        def tok(t):
            return slice(t * P, (t + 1) * P)

        def blk(c):
            return slice(c * BLK, (c + 1) * BLK)

        def moe0_weights():
            return [(moe_w[:, k, :].rearrange("p (e n) -> p e n", e=E),
                     a["L0_ffn_expert_w"][:, tok(k), :].rearrange("e p n -> p e n")) for k in range(DK)]

        def moe1_weights():
            return [(moe_w[:, k, :].rearrange("p (e i n) -> p e i n", e=E, i=2)[:, :, i, :],
                     a[w][:, tok(k), :].rearrange("e p n -> p e n"))
                    for k in range(DK) for i, w in enumerate(("L1_ffn_w1", "L1_ffn_w3"))]

        def reload(sp, arrived, pairs):
            for dst, src in pairs:
                sp.dma_start(dst, src).then_inc(arrived, 16)
            sp.wait_ge(arrived, 16 * len(pairs))

        CONTEXT_SEMS = 10

        class Context:
            def __init__(self, sems, stack, base):
                (self.cs, self.ms, self.stated, self.added, self.powed, self.normed, self.masked, self.turned,
                 self.evac, self.rep) = sems
                self.base = base
                self.tok = sb("c_tok", [M, C], stack=stack)
                self.nrm = sb("c_nrm", [M, C], stack=stack)
                self.st = sb("cst", [M, 6], stack=stack)
                self.mv = sb("cmv", [M, 2], stack=stack)
                self.rs = sb("crs", [M, 2], stack=stack)
                self.col_u8 = sb("col_u8", [M, 1], U8, stack=stack)
                self.row_u8 = sb("row_u8", [1, M], U8, stack=stack)

            def sync(self, sp, b):
                sp.dma_start(self.tok[:, :], a["ctx_768"][bass.ds(b, 1), :, :].rearrange("o m c -> (o m) c")
                             ).then_inc(self.cs, 16)
                mask = a["mask"][bass.ds(b, 1), :]
                sp.dma_start(self.col_u8[:, :], mask.rearrange("o m -> m o")).then_inc(self.ms, 16)
                sp.dma_start(self.row_u8[:, :], mask).then_inc(self.ms, 16)

            def vector_norm(self, dve):
                dve.wait_ge(self.cs, 16)
                dve.bn_stats(self.st[:, :], self.tok[:, :]).then_inc(self.stated, 1)
                dve.wait_ge(self.stated, 1)
                dve.bn_aggr(self.mv[:, :], self.st[:, :]).then_inc(self.stated, 1)
                dve.wait_ge(self.powed, 1)
                dve.tensor_scalar(self.nrm[:, :], self.tok[:, :], self.mv[:, 0:1], self.rs[:, 1:2], ALU.subtract,
                                  ALU.mult).then_inc(self.normed, 1)
                dve.wait_ge(self.ms, 32)
                dve.tensor_scalar(mask_col[:, :], self.col_u8[:, :], 1.0, LOW, ALU.subtract,
                                  ALU.mult).then_inc(self.masked, 1)
                dve.tensor_scalar(mask_row[:, :], self.row_u8[:, :], 1.0, LOW, ALU.subtract,
                                  ALU.mult).then_inc(self.masked, 1)

            def vector_tokens(self, dve, xs, stated):
                dve.wait_ge(xs, 16)
                for t in range(T):
                    dve.bn_stats(st0[:, t, :], x[:, t, :]).then_inc(stated, 1)
                for t in range(T):
                    dve.wait_ge(stated, t + 1)
                    dve.bn_aggr(mv0[:, t, :], st0[:, t, :])

            def vector_repeat(self, dve):
                dve.wait_ge(self.evac, 2)
                dve.tensor_copy(ctx_rep[:, 0, :].rearrange("p (h m) -> p h m", m=M),
                                ctxT[:, 0, :].unsqueeze(1).to_broadcast([P, HG, M])).then_inc(self.rep, 1)
                dve.tensor_copy(ctx_rep[0:C1 + 1, 1, :].rearrange("p (h m) -> p h m", m=M),
                                ctxT[0:C1 + 1, 1, :].unsqueeze(1).to_broadcast([C1 + 1, HG, M])
                                ).then_inc(self.rep, 1)

            def gpsimd(self, pool):
                pool.wait_ge(self.stated, 2)
                pool.tensor_scalar(self.rs[:, 0:1], self.mv[:, 1:2], EPS, None, ALU.add).then_inc(self.added, 1)
                pool.wait_ge(self.added, 1)
                pool.tensor_tensor(self.rs[:, 1:2], self.rs[:, 0:1], neg_half[0:M, 0:1],
                                   ALU.pow).then_inc(self.powed, 1)

            def tensor(self, pe):
                n = self.base
                pe.wait_ge(self.cs, 16)
                pe.transpose(bank(n, M), self.tok[:, 0:P], ident[0:M, 0:M])
                pe.transpose(bank(n + 1, M)[0:C1, :], self.tok[:, P:C], ident[0:M, 0:M]).then_inc(self.turned, 1)
                pe.wait_ge(self.normed, 1)
                pe.transpose(bank(n + 2, M), self.nrm[:, 0:P], ident[0:M, 0:M])
                pe.transpose(bank(n + 3, M)[0:C1, :], self.nrm[:, P:C], ident[0:M, 0:M]).then_inc(self.turned, 1)

            def scalar(self, act):
                n = self.base
                act.wait_ge(self.turned, 1)
                act.activation(ctxT[:, 0, :], bank(n, M), ACT.Copy).then_inc(self.evac, 1)
                act.activation(ctxT[0:C1, 1, :], bank(n + 1, M)[0:C1, :], ACT.Copy).then_inc(self.evac, 1)
                act.wait_ge(self.turned, 2)
                act.activation(cnT[:, 0, :], bank(n + 2, M), ACT.Identity, bias=col("ln_x_b", 0),
                               scale=col("ln_x_g", 0)).then_inc(self.evac, 1)
                act.activation(cnT[0:C1, 1, :], bank(n + 3, M)[0:C1, :], ACT.Identity,
                               bias=col("ln_x_b", 1)[0:C1, :], scale=col("ln_x_g", 1)[0:C1, :]).then_inc(self.evac, 1)

        with stage("prepare", 11 + CONTEXT_SEMS) as (block, (
                zeroed, selected, tanhed, maxed, absmax, scaled, rounded, gates, cleared, xs, measured,
                *sems)):
            quant_tmp = ExitStack()
            kern = sb("kern", [P, DK, D], stack=quant_tmp)
            kscale = sb("kscale", [P, 4], stack=quant_tmp)
            context = Context(sems, quant_tmp, 0)

            @block.sync
            def _(sp):
                load(sp, "cols", (cols[:, :], a["cols"]))
                sp.dma_start(x[:, :, :], a["x"][0].rearrange("(t p) d -> p t d", p=P)).then_inc(xs, 16)
                context.sync(sp, 0)
                load(sp, "w0", *chunked(w0_qkv, a["w0_qkv"]), *chunked(w0_ckv, a["w0_ckv"]),
                     *chunked(w0_o, a["w0_o"]))
                load(sp, "rows", (rows[:, :], a["rows"]))
                load(sp, "kern", *chunked(kern, a["L2_ffn_kernel"]))
                load(sp, "e0", *chunked(r0, a["L0_ffn_router_w"]), *moe0_weights())
                load(sp, "w1", *chunked(w1_q, a["L1_xattn_Wq"]), *chunked(w1_k, a["w1_k"]),
                     *chunked(w1_v, a["w1_v"]), *chunked(w1_o, a["L1_xattn_Wo"]))
                load(sp, "e1", *chunked(r1, a["L1_ffn_gate_w"]),
                     (e1_down[:, :, :], a["L1_ffn_w2"].rearrange("e p n -> p e n")))
                load(sp, "w2", *chunked(w2_q, a["L2_xattn_Wq"]),
                     *chunked(w2_o, a["L2_xattn_Wproj"]))
                load(sp, "lora", *chunked(lora_a, a["L2_ffn_a"]), (lora_b[:, :], a["L2_ffn_b"]))
                load(sp, "w3", *chunked(w3_q, a["L3_xattn_Wq"]), *chunked(w3_k, a["w3_k"]),
                     *chunked(w3_v, a["w3_v"]), *chunked(w3_1, a["L3_xattn_W1"]),
                     *chunked(w3_2, a["L3_xattn_W2"]), *chunked(r3, a["r3"]))
                sp.wait_ge(cleared, 1)
                zrows = slots_in.rearrange("(n p r) d -> n p (r d)", p=P, r=T)
                load(sp, "zero", *[(zrows[n].rearrange("p (r z) -> p r z", z=P),
                                    zeros[:, :].unsqueeze(1).to_broadcast([P, T * D // P, P]))
                                   for n in range(SLOTS // (P * T))])
                sp.wait_ge(xs, 16)

            @block.tensor
            def _(pe):
                pe.wait_ge(selected, 8)
                context.tensor(pe)

            @block.gpsimd
            def _(pool):
                pool.dma_start(e0_b[:, :], a["L0_ffn_expert_b"]).then_inc(sent, BEFORE)
                n = [0]

                def fill(ap, value):
                    pool.memset(ap, value).then_inc(zeroed, 1)
                    n[0] += 1
                fill(ident[:, :], 0.0)
                fill(neg_half[:, :], -0.5)
                fill(upper[:, :], 1.0)
                fill(head_of_feature[:, :], 1.0)
                fill(head_of_row[:, :, :], 1.0)
                fill(pick_row[:, :, :], 0.0)
                fill(pick2[:, :, :], 0.0)
                fill(ones_bf[:, :], 1.0)
                fill(ones_f[:, :], 1.0)
                fill(taken[:, :], 0.0)
                fill(ctxT[:, :, :], 1.0)
                for e in range(E):
                    fill(rank[:, :, e:e + 1], float(E - e))
                pool.wait_ge(zeroed, n[0])

                def choose(ap, op, value, base, pattern, mult):
                    pool.affine_select(out=ap, in_=ap, compare_op=op, fill=value, base=base, pattern=pattern,
                                       channel_multiplier=mult).then_inc(selected, 1)
                choose(ident[:, :], ALU.not_equal, 1.0, 0, [[-1, P]], 1)
                choose(upper[:, :], ALU.is_ge, 0.0, 0, [[1, P]], -1)
                choose(head_of_feature[:, :], ALU.is_ge, 0.0, 0, [[-DH1, HG]], 1)
                choose(head_of_row[:, :, :], ALU.is_ge, 0.0, 0, [[P, len(CH)], [-M, HG]], 1)
                choose(pick_row[:, :, :].rearrange("p g (h m) -> p g h m", m=M), ALU.not_equal, 1.0, 0,
                       [[-HG, G], [-1, HG], [0, M]], 1)
                choose(pick2[:, :, :], ALU.not_equal, 1.0, 0, [[-1, 2], [0, M]], 1)
                pool.wait_ge(selected, 6)
                choose(head_of_feature[:, :], ALU.is_ge, 0.0, DH1 - 1, [[DH1, HG]], -1)
                choose(head_of_row[:, :, :], ALU.is_ge, 0.0, M - 1, [[-P, len(CH)], [M, HG]], -1)
                pool.wait_ge(selected, 8)
                context.gpsimd(pool)
                pool.wait_ge(maxed, 1)
                pool.partition_all_reduce(kscale[:, 1:2], kscale[:, 0:1], P,
                                          bass.bass_isa.ReduceOp.max).then_inc(absmax, 1)

            @block.scalar
            def _(act):
                loaded(act, "cols")
                act.activation(tg[:, :], cols[:, COLS["gates"]:COLS["gates"] + 8], ACT.Tanh).then_inc(tanhed, 1)
                context.scalar(act)

            @block.vector
            def _(dve):
                dve.memset(zeros[:, :], 0.0).then_inc(cleared, 1)
                dve.wait_ge(zeroed, 2)
                context.vector_norm(dve)
                context.vector_repeat(dve)
                context.vector_tokens(dve, xs, measured)
                loaded(dve, "rows")
                dve.wait_ge(tanhed, 1)
                for name, g in GATED:
                    dve.tensor_scalar(row(name), row(name), tg[:, g:g + 1], None, ALU.mult).then_inc(gates, 1)
                loaded(dve, "kern")
                dve.tensor_reduce(kscale[:, 0:1], kern[:, :, :], AX.XY, ALU.max,
                                  apply_absolute_value=True).then_inc(maxed, 1)
                dve.wait_ge(absmax, 1)
                dve.tensor_scalar(kscale[:, 2:3], kscale[:, 1:2], 1.0 / 7.0, None, ALU.mult).then_inc(scaled, 1)
                dve.wait_ge(scaled, 1)
                dve.reciprocal(kscale[:, 3:4], kscale[:, 2:3]).then_inc(scaled, 1)
                dve.wait_ge(scaled, 2)
                dve.tensor_scalar(wq8[:, :, :], kern[:, :, :], kscale[:, 3:4], None, ALU.mult).then_inc(scaled, 1)
                dve.wait_ge(scaled, 3)
                magic = 1.5 * 2.0 ** 23
                dve.tensor_scalar(wq8[:, :, :], wq8[:, :, :], magic, None, ALU.add).then_inc(rounded, 1)
                dve.wait_ge(rounded, 1)
                dve.tensor_scalar(wq8[:, :, :], wq8[:, :, :], magic, None, ALU.subtract).then_inc(rounded, 1)
                dve.wait_ge(rounded, 2)
                dve.tensor_scalar(wq8[:, :, :], wq8[:, :, :], -8.0, 7.0, ALU.max, ALU.min).then_inc(rounded, 1)
                dve.wait_ge(rounded, 3)
                dve.tensor_scalar(wq8[:, :, :], wq8[:, :, :], kscale[:, 2:3], None, ALU.mult).then_inc(rounded, 1)
            quant_tmp.close()

        def exact3(pe, out_, ah, al, bh, bl, first, last):
            pe.matmul(out_, ah, bh, start=first, stop=False)
            pe.matmul(out_, ah, bl, start=False, stop=False)
            return pe.matmul(out_, al, bh, start=False, stop=last)

        NORM_SEMS = 8

        class Norm:
            GROUPS = (range(0, 4), range(4, 6), range(6, 8))

            def __init__(self, sems, stack):
                (self.stated, self.varied, self.added, self.powed, self.normed, self.turned, self.evac,
                 self.evac_dve) = sems
                self.st = sb("st", [P, T, 6], stack=stack)
                self.mv = sb("mv", [P, T, 2], stack=stack)
                self.rs = sb("rs", [P, 2, T], stack=stack)

            def vector(self, dve, t):
                dve.bn_stats(self.st[:, t, :], x[:, t, :]).then_inc(self.stated, 1)
                if t:
                    self.aggregate(dve, t - 1)
                for g, ts in enumerate(self.GROUPS):
                    if t == ts[-1] + 1:
                        self.normalise(dve, g)
                if t == T - 1:
                    self.aggregate(dve, t)
                    self.normalise(dve, len(self.GROUPS) - 1)
                    dve.wait_ge(self.turned, DK * T)
                    dve.tensor_copy(xT[:, DK - 1, blk(NB - 1)], bank(DK * NB - 1)).then_inc(self.evac_dve, 1)

            def aggregate(self, dve, t):
                dve.wait_ge(self.stated, t + 1)
                dve.bn_aggr(self.mv[:, t, :], self.st[:, t, :]).then_inc(self.varied, 1)

            def normalise(self, dve, g):
                dve.wait_ge(self.powed, g + 1)
                for t in self.GROUPS[g]:
                    dve.tensor_scalar(xn[:, t, :], x[:, t, :], self.mv[:, t, 0:1], self.rs[:, 1, t:t + 1],
                                      ALU.subtract, ALU.mult).then_inc(self.normed, 1)

            def gpsimd(self, pool):
                for c, tiles in enumerate(self.GROUPS):
                    ts = slice(tiles[0], tiles[-1] + 1)
                    pool.wait_ge(self.varied, tiles[-1] + 1)
                    pool.tensor_scalar(self.rs[:, 0, ts], self.mv[:, ts, 1], EPS, None, ALU.add).then_inc(self.added, 1)
                    pool.wait_ge(self.added, c + 1)
                    pool.tensor_tensor(self.rs[:, 1, ts], self.rs[:, 0, ts], neg_half[:, ts],
                                       ALU.pow).then_inc(self.powed, 1)

            def tensor(self, pe):
                for c in range(NB):
                    for t in tiles_of(c):
                        pe.wait_ge(self.normed, t + 1)
                        for k in range(DK):
                            pe.transpose(bank(DK * c + k)[:, tok(t % TB)], xn[:, t, tok(k)],
                                         ident[:, :]).then_inc(self.turned, 1)

            def scalar(self, act):
                for c in range(NB):
                    act.wait_ge(self.turned, DK * TB * (c + 1))
                    for k in range(DK if c + 1 < NB else DK - 1):
                        act.activation(xT[:, k, blk(c)], bank(DK * c + k), ACT.Copy).then_inc(self.evac, 1)

        def add_bias(pool, name, biased):
            for t in range(T):
                pool.tensor_tensor(x[:, t, :], x[:, t, :], row(name), ALU.add).then_inc(biased, 1)

        def clear_other_half(eng, k, i):
            return eng.memset(k[64 * (1 - i):64 * (2 - i), i::2, :].bitcast(F32), 0.0)

        def first_norm_stage(b, kT):
            with stage("norm0", 9) as (block, (added, powed, scaled, normed, ready, normed_act, turned, evac,
                                               cleared)), \
                    ExitStack() as tmp:
                rs = sb("rs", [P, 6, T], stack=tmp)
                v0, r, v1, r1, both, offset = (rs[:, i, :] for i in range(6))
                mean, var = mv0[:, :, 0], mv0[:, :, 1]

                @block.gpsimd
                def _(pool):
                    pool.tensor_scalar(v0, var, EPS, None, ALU.add).then_inc(added, 1)
                    pool.wait_ge(added, 1)
                    pool.tensor_tensor(r, v0, neg_half[:, 0:T], ALU.pow).then_inc(powed, 1)
                    pool.wait_ge(scaled, 3)
                    pool.tensor_tensor(r1, v1, neg_half[:, 0:T], ALU.pow).then_inc(powed, 1)
                    pool.wait_ge(powed, 2)
                    for i in range(2):
                        clear_other_half(pool, kT[1], i).then_inc(cleared, 1)
                        pool.wait_ge(cleared, i + 1)

                @block.vector
                def _(dve):
                    dve.wait_ge(powed, 1)
                    dve.tensor_tensor(v1, r, r, ALU.mult).then_inc(scaled, 1)
                    dve.wait_ge(scaled, 1)
                    dve.tensor_tensor(v1, v1, var, ALU.mult).then_inc(scaled, 1)
                    dve.wait_ge(scaled, 2)
                    dve.tensor_scalar(v1, v1, EPS, None, ALU.add).then_inc(scaled, 1)
                    dve.wait_ge(powed, 2)
                    dve.tensor_tensor(both, r, r1, ALU.mult).then_inc(scaled, 1)
                    dve.wait_ge(scaled, 4)
                    dve.scalar_tensor_tensor(out=offset, in0=mean, scalar=-1.0, in1=both, op0=ALU.mult,
                                             op1=ALU.mult).then_inc(ready, 1)
                    dve.wait_ge(sent, b * (16 * T) + BEFORE)
                    for t in range(0, T, 2):
                        dve.tensor_scalar(xn[:, t, :], x[:, t, :], mv0[:, t, 0:1], both[:, t:t + 1],
                                          ALU.subtract, ALU.mult).then_inc(normed, 1)
                    for i in range(2):
                        clear_other_half(dve, kT[0], i)

                @block.tensor
                def _(pe):
                    for t in range(T):
                        pe.wait_ge(normed_act if t % 2 else normed, t // 2 + 1)
                        for k in range(DK):
                            pe.transpose(bank(DK * (t // TB) + k)[:, tok(t % TB)], xn[:, t, tok(k)],
                                         ident[:, :]).then_inc(turned, 1)

                @block.scalar
                def _(act):
                    act.wait_ge(ready, 1)
                    act.wait_ge(sent, b * (16 * T) + BEFORE)
                    for t in range(1, T, 2):
                        act.activation(xn[:, t, :], x[:, t, :], ACT.Identity, scale=both[:, t:t + 1],
                                       bias=offset[:, t:t + 1]).then_inc(normed_act, 1)
                    for c in range(NB):
                        act.wait_ge(turned, DK * TB * (c + 1))
                        for k in range(DK):
                            act.activation(xT[:, k, blk(c)], bank(DK * c + k), ACT.Identity,
                                           bias=col("ln_l_b", k), scale=col("ln_l_g", k)).then_inc(evac, 1)

        def project_stage(name, o_tok, w, group, chunks, gate):
            with stage(name, 4 + NORM_SEMS) as (block, (turned, evac, summed, updated, *sems)), \
                    ExitStack() as tmp:
                oT = sb("oT", [P, 2, chunks, P], stack=tmp)
                norm = Norm(sems, tmp)
                per = (chunks + 3) // 4

                @block.tensor
                def _(pe):
                    loaded(pe, group)

                    def turn_tile(t):
                        if t >= 2:
                            pe.wait_ge(evac, per * (t - 1))
                        for k in range(chunks):
                            pe.transpose(bank(per * (t % 2) + k // 4)[:, tok(k % 4)], o_tok[:, t, tok(k)],
                                         ident[:, :]).then_inc(turned, 1)
                    turn_tile(0)
                    for t in range(T):
                        if t + 1 < T:
                            turn_tile(t + 1)
                        pe.wait_ge(evac, per * (t + 1))
                        if t >= 4:
                            pe.wait_ge(updated, t - 3)
                        for k in range(chunks):
                            mm = pe.matmul(bank(4 + t % 4, D), oT[:, t % 2, k, :], w[:, k, :],
                                           start=(k == 0), stop=(k == chunks - 1))
                        mm.then_inc(summed, 1)
                    norm.tensor(pe)

                @block.scalar
                def _(act):
                    for t in range(T):
                        act.wait_ge(turned, chunks * (t + 1))
                        if t >= 2:
                            act.wait_ge(summed, t - 1)
                        for i in range(per):
                            n = min(4, chunks - 4 * i)
                            act.activation(oT[:, t % 2, 4 * i:4 * i + n, :],
                                           bank(per * (t % 2) + i, n * P).rearrange("p (k q) -> p k q", q=P),
                                           ACT.Copy).then_inc(evac, 1)
                    norm.scalar(act)

                @block.vector
                def _(dve):
                    for t in range(T):
                        dve.wait_ge(summed, t + 1)
                        dve.scalar_tensor_tensor(out=x[:, t, :], in0=bank(4 + t % 4, D), scalar=tg[:, gate:gate + 1],
                                                 in1=x[:, t, :], op0=ALU.mult, op1=ALU.add).then_inc(updated, 1)
                        if t:
                            dve.wait_ge(updated, t)
                            norm.vector(dve, t - 1)
                    dve.wait_ge(updated, T)
                    norm.vector(dve, T - 1)

                @block.gpsimd
                def _(pool):
                    norm.gpsimd(pool)

        def halves(h):
            return (slice(64 * (h % 2), 64 * (h % 2) + 64), slice(64 - 64 * (h % 2), 128 - 64 * (h % 2)))

        NPT = 4

        def probs(n):
            return xn[:, 2 * (n % NPT):2 * (n % NPT) + 2, :].rearrange("p t d -> p (t d)")

        NK0 = T + 1
        KEYS0 = S + M

        def key_rows(j):
            return P if j < T else M

        def qkv0_stage(qT, kT, qTb, kTb, v_aug):
            with stage("qkv0", 11) as (block, (qk_done, v_done, squared, summed, floored, powed, normed, turned,
                                               evac, low, v_evac)), ExitStack() as tmp:
                sq = xn[:, 0:4, :].rearrange("p (i z) d -> p i (z d)", i=2)
                qk = xn[:, 4:8, :].rearrange("p (i z) d -> p i (z d)", i=2)
                ss = sb("ss", [P, NK0, 2 * H0], stack=tmp)
                fl = sb("fl", [P, NK0, 2 * H0], stack=tmp)
                ri = sb("ri", [P, NK0, 2 * H0], stack=tmp)
                v_pairs = v_aug[:, :, :, :].rearrange("p j k (z d) -> p (j k) z d", z=3)
                (qT_h, qT_l), (kT_h, kT_l) = qT, kT
                QB = 3

                def qk_bank(j):
                    return bank((0, 1, 6)[j % QB])

                @block.tensor
                def _(pe):
                    loaded(pe, "w0")

                    def turn_tile(j):
                        n = key_rows(j)
                        pe.wait_ge(normed, j + 1)
                        if j >= 2:
                            pe.wait_ge(evac, j - 1)
                            pe.wait_ge(low, j - 1)
                        first = 0 if j < T else DK
                        for i in range(first, 2 * DK):
                            mm = pe.transpose(bank(4 + j % 2)[:, i * P:i * P + n], qk[0:n, j % 2, tok(i)],
                                              ident[0:n, 0:n])
                        mm.then_inc(turned, 1)
                    for j in range(NK0):
                        if j >= QB:
                            pe.wait_ge(normed, j - QB + 1)
                            pe.wait_ge(squared, j - QB + 1)
                        if j >= 2:
                            pe.wait_ge(v_evac, j - 1)
                        if j < T:
                            for k in range(DK):
                                mm = pe.matmul(qk_bank(j), xT[:, k, tok(j)], w0_qkv[:, k, 0:2 * D],
                                               start=(k == 0), stop=(k == DK - 1))
                            mm.then_inc(qk_done, 1)
                            for k in range(DK):
                                mm = pe.matmul(bank(2 + j % 2, D), xT[:, k, tok(j)], w0_qkv[:, k, 2 * D:3 * D],
                                               start=(k == 0), stop=(k == DK - 1))
                            mm.then_inc(v_done, 1)
                        else:
                            for k, r in enumerate((P, C1)):
                                mm = pe.matmul(qk_bank(j)[0:M, D:2 * D], cnT[0:r, k, :], w0_ckv[0:r, k, 0:D],
                                               start=(k == 0), stop=(k == 1))
                            mm.then_inc(qk_done, 1)
                            for k, r in enumerate((P, C1)):
                                mm = pe.matmul(bank(2 + j % 2)[0:M, 0:D], cnT[0:r, k, :], w0_ckv[0:r, k, D:2 * D],
                                               start=(k == 0), stop=(k == 1))
                            mm.then_inc(v_done, 1)
                        if j >= 2:
                            turn_tile(j - 2)
                    turn_tile(NK0 - 2)
                    turn_tile(NK0 - 1)

                @block.scalar
                def _(act):
                    def evacuate(j):
                        act.wait_ge(turned, j + 1)
                        n = key_rows(j)
                        both = bank(4 + j % 2).rearrange("p (i q) -> p i q", q=P)[:, :, 0:n]
                        if j < T:
                            act.activation(qT_h[:, :, tok(j)], both[:, 0:DK, :], ACT.Identity,
                                           scale=col("qn_g"), bias=0.0)
                            act.activation(qTb[:, :, tok(j)], both[:, 0:DK, :], ACT.Identity,
                                           scale=col("qn_g"), bias=0.0)
                        for i in range(2):
                            r = slice(DH0 * i, DH0 * (i + 1))
                            op = act.activation(kT_h[r, i::2, j * P:j * P + n], both[r, DK:2 * DK, :], ACT.Identity,
                                                scale=col("kn_g")[r, :], bias=0.0)
                        op.then_inc(evac, 1)
                    for j in range(NK0):
                        n = key_rows(j)
                        lo = 0 if j < T else D
                        act.wait_ge(qk_done, j + 1)
                        if j >= 2:
                            act.wait_ge(summed, j - 1)
                        act.activation(sq[0:n, j % 2, lo:], qk_bank(j)[0:n, lo:], ACT.Square).then_inc(squared, 1)
                        act.wait_ge(v_done, j + 1)
                        act.activation(v_pairs[0:n, j * DK:(j + 1) * DK, 0::2, :],
                                       bank(2 + j % 2, D)[0:n, :].rearrange("p (k i d) -> p k i d", i=2, d=DH0),
                                       ACT.Copy).then_inc(v_evac, 1)
                        if j >= 2:
                            evacuate(j - 2)
                    evacuate(NK0 - 2)
                    evacuate(NK0 - 1)

                @block.vector
                def _(dve):
                    def scale_tile(j):
                        n = key_rows(j)
                        h = 0 if j < T else H0
                        dve.wait_ge(powed, j + 1)
                        if j >= 2:
                            dve.wait_ge(turned, j - 1)
                        dve.tensor_tensor(qk[0:n, j % 2, h * DH0:].rearrange("p (h d) -> p h d", d=DH0),
                                          qk_bank(j)[0:n, h * DH0:].rearrange("p (h d) -> p h d", d=DH0),
                                          ri[0:n, j, h:].unsqueeze(2).to_broadcast([n, 2 * H0 - h, DH0]),
                                          ALU.mult).then_inc(normed, 1)

                    def low_tile(j):
                        n = key_rows(j)
                        ks = slice(j * P, j * P + n)
                        dve.wait_ge(evac, j + 1)
                        both = bank(4 + j % 2).rearrange("p (i q) -> p i q", q=P)[:, :, 0:n]
                        if j < T:
                            dve.scalar_tensor_tensor(out=qT_l[:, :, tok(j)], in0=both[:, 0:DK, :], scalar=col("qn_g"),
                                                     in1=qT_h[:, :, tok(j)].bitcast(F32), op0=ALU.mult,
                                                     op1=ALU.subtract)
                        for i in range(2):
                            r = slice(DH0 * i, DH0 * (i + 1))
                            op = dve.scalar_tensor_tensor(out=kT_l[r, i::2, ks], in0=both[r, DK:2 * DK, :],
                                                          scalar=col("kn_g")[r, :],
                                                          in1=kT_h[r, i::2, ks].bitcast(F32), op0=ALU.mult,
                                                          op1=ALU.subtract)
                        op.then_inc(low, 1)
                        for i in range(2):
                            r = slice(DH0 * i, DH0 * (i + 1))
                            dve.tensor_copy(kTb[r, :, ks], kT_h[r, i::2, ks].bitcast(F32))
                    dve.memset(v_pairs[:, :, 1, :], 1.0)
                    for j in range(NK0):
                        n = key_rows(j)
                        h = 0 if j < T else H0
                        dve.wait_ge(squared, j + 1)
                        dve.tensor_reduce(ss[0:n, j, h:], sq[0:n, j % 2, h * DH0:].rearrange("p (h d) -> p h d", d=DH0),
                                          AX.X, ALU.add).then_inc(summed, 1)
                        if j:
                            scale_tile(j - 1)
                        if j >= 3:
                            low_tile(j - 3)
                    scale_tile(NK0 - 1)
                    for j in range(NK0 - 3, NK0):
                        low_tile(j)

                @block.gpsimd
                def _(pool):
                    for j in range(NK0):
                        n = key_rows(j)
                        h = 0 if j < T else H0
                        pool.wait_ge(summed, j + 1)
                        pool.tensor_scalar(fl[0:n, j, h:], ss[0:n, j, h:], 1.0 / DH0, 1e-16, ALU.mult,
                                           ALU.max).then_inc(floored, 1)
                        pool.wait_ge(floored, j + 1)
                        pool.tensor_tensor(ri[0:n, j, h:], fl[0:n, j, h:], neg_half[0:n, h:2 * H0],
                                           ALU.pow).then_inc(powed, 1)

        def attend0_stage(qT, kT, qTb, kTb, v_aug, oT):
            with stage("attend0", 12 + NORM_SEMS) as (block, (
                    scored, maxed, turned, shifted, sdone, edone, pv, ok, recd, summed, updated, biased, *sems)), \
                    ExitStack() as tmp:
                norm = Norm(sems, tmp)
                mx = sb("mx", [P, 2, TB], stack=tmp)
                shift = sb("shift", [1, 2, BLK], BF16, stack=tmp)
                rc = sb("rc", [P, BLK], stack=tmp)
                UNITS = H0 * NB
                MAX_AT = (1, 4, 5, 6)
                R = NK0 + 1

                def region(u, q):
                    return 3 * 512 if u == 0 and q % 2 else 0

                def unit(u):
                    return divmod(u, NB)

                def ring(u, j):
                    return bank(3 + (u * R + j + 1) % 3)

                @block.tensor
                def _(pe):
                    def score_max(u, q):
                        h, c = unit(u)
                        t = c * TB + q
                        r, k = slice(DH0 * (h % 2), DH0 * (h % 2 + 1)), h // 2
                        if u == 0 and q >= 2:
                            pe.wait_ge(maxed, q - 1)
                        elif u:
                            pe.wait_ge(maxed, u * TB + q)
                        o = region(u, q)
                        for lo in range(0, KEYS0, 512):
                            w = min(512, KEYS0 - lo)
                            mm = pe.matmul(psum[:, o + lo:o + lo + w], qTb[r, k, tok(t)], kTb[r, k, lo:lo + w],
                                           start=True, stop=(w == 512))
                        mm = pe.matmul(psum[:, o + S:o + S + M], ones_bf[0:1, :], mask_row[0:1, :],
                                       start=False, stop=True)
                        mm.then_inc(scored, 1)

                    def bank_free(u, j):
                        turn_ = u * R + j + 1 - 3
                        if turn_ < 0:
                            return
                        v, i = divmod(turn_, R)
                        if i == 0:
                            pe.wait_ge(shifted, v + 1)
                        else:
                            pe.wait_ge(edone, v * NK0 + i)

                    def turn_max(u):
                        pe.wait_ge(maxed, TB * (u + 1))
                        bank_free(u, -1)
                        for q in range(TB):
                            mm = pe.transpose(ring(u, -1)[0:1, tok(q)], mx[:, u % 2, q:q + 1], ident[:, :])
                        mm.then_inc(turned, 1)

                    def scores(u, j):
                        h, c = unit(u)
                        w = key_rows(j)
                        if j == 0:
                            pe.wait_ge(shifted, u + 1)
                        bank_free(u, j)
                        ks = slice(j * P, j * P + w)
                        exact3(pe, ring(u, j)[0:w, :], kT[0][:, h, ks], kT[1][:, h, ks], qT[0][:, h // 2, blk(c)],
                               qT[1][:, h // 2, blk(c)], True, False)
                        pe.matmul(ring(u, j)[0:w, :], ones_bf[0:1, 0:w], shift[:, u % 2, :],
                                  start=False, stop=True).then_inc(sdone, 1)

                    def values(u, j):
                        h = unit(u)[0]
                        n = u * NK0 + j
                        w = key_rows(j)
                        pe.wait_ge(edone, n + 1)
                        if j == 0 and u >= 2:
                            pe.wait_ge(ok, u - 1)
                        mine = slice(DH0 * (h % 2), DH0 * (h % 2) + 2 * DH0)
                        pe.matmul(bank(6 + u % 2), v_aug[0:w, j, h // 2, mine], probs(n)[0:w, :],
                                  start=(j == 0), stop=(j == NK0 - 1)).then_inc(pv, 1)
                    def project(t):
                        if t in (0, TB):
                            pe.wait_ge(ok, UNITS - NB + t // TB + 1)
                        if t == TB + 2:
                            pe.wait_ge(ok, UNITS + 1)
                        if t >= 3:
                            pe.wait_ge(updated, t - 2)
                        for k in range(DK):
                            mm = pe.matmul(bank(t % 3, D), oT[:, k, tok(t)], w0_o[:, k, :],
                                           start=(k == 0), stop=(k == DK - 1))
                        mm.then_inc(summed, 1)
                    for q in range(TB):
                        score_max(0, q)
                    turn_max(0)
                    for n in range(UNITS * NK0 + 2):
                        u, j = divmod(n, NK0)
                        if u < UNITS:
                            scores(u, j)
                        if n >= 2:
                            values(*divmod(n - 2, NK0))
                        if u + 1 < UNITS and j in MAX_AT:
                            score_max(u + 1, MAX_AT.index(j))
                        if u + 1 < UNITS and j == NK0 - 2:
                            turn_max(u + 1)
                        if u == UNITS - 1 and j >= NK0 - TB:
                            project(j - (NK0 - TB))
                    for t in tiles_of(1):
                        project(t)
                    pe.wait_ge(updated, T)
                    norm.tensor(pe)

                @block.scalar
                def _(act):
                    for n in range(UNITS * NK0):
                        u, j = divmod(n, NK0)
                        w = key_rows(j)
                        act.wait_ge(sdone, n + 1)
                        if n >= NPT:
                            act.wait_ge(pv, n - NPT + 1)
                        act.activation(probs(n)[0:w, :], ring(u, j)[0:w, :], ACT.Exp,
                                       scale=float(DH0) ** -0.5,
                                       bias=(mask_col[:, 0:1] if j == T else 0.0)).then_inc(edone, 1)
                    norm.scalar(act)

                @block.gpsimd
                def _(pool):
                    add_bias(pool, "bo0", biased)
                    norm.gpsimd(pool)

                @block.vector
                def _(dve):
                    def find_shift(u):
                        for q in range(TB):
                            dve.wait_ge(scored, u * TB + q + 1)
                            o = region(u, q)
                            dve.tensor_reduce(mx[:, u % 2, q:q + 1], psum[:, o:o + KEYS0], AX.X,
                                              ALU.max).then_inc(maxed, 1)
                        dve.wait_ge(turned, u + 1)
                        dve.tensor_scalar(shift[:, u % 2, :], ring(u, -1)[0:1, :], -1.0, None,
                                          ALU.mult).then_inc(shifted, 1)

                    def outputs(u):
                        h, c = unit(u)
                        dve.wait_ge(pv, NK0 * (u + 1))
                        mine, sums = halves(h)
                        if u:
                            dve.wait_ge(ok, u)
                        parts = 2 if u == UNITS - 1 else 1
                        for i in range(parts):
                            r = slice(i * BLK // parts, (i + 1) * BLK // parts)
                            dve.reciprocal(rc[mine, r], bank(6 + u % 2)[sums, r]).then_inc(recd, 1)
                            dve.wait_ge(recd, u + i + 1)
                            dve.tensor_tensor(oT[mine, h // 2, c * BLK + r.start:c * BLK + r.stop],
                                              bank(6 + u % 2)[mine, r], rc[mine, r], ALU.mult).then_inc(ok, 1)

                    def update(t):
                        dve.wait_ge(summed, t + 1)
                        dve.scalar_tensor_tensor(out=x[:, t, :], in0=bank(t % 3, D), scalar=tg[:, 0:1],
                                                 in1=x[:, t, :], op0=ALU.mult, op1=ALU.add).then_inc(updated, 1)
                        if t:
                            dve.wait_ge(updated, t)
                            norm.vector(dve, t - 1)
                    find_shift(0)
                    for u in range(UNITS):
                        if u + 1 < UNITS:
                            find_shift(u + 1)
                        else:
                            dve.wait_ge(biased, T)
                            for t in tiles_of(0):
                                update(t)
                        outputs(u)
                    for t in tiles_of(1):
                        update(t)
                    dve.wait_ge(updated, T)
                    norm.vector(dve, T - 1)

        class Split:
            SEMS = 2

            def __init__(self, sems, stack):
                self.high, self.low = sems
                self.w = [sb(f"moe_{j}", [P, DK, E * D], F32R, stack=stack) for j in "hl"]
                self.x = [sb(f"xT_{j}", [P, DK, S], F32R, stack=stack) for j in "hl"]
                pair = [slice(2 * D * p, 2 * D * (p + 1)) for p in range(E // 2)]
                self.pieces = ([(xT[:, :, blk(0)], *(v[:, :, blk(0)] for v in self.x))] +
                               [(moe_w[:, :, r], *(v[:, :, r] for v in self.w)) for r in pair] +
                               [(xT[:, :, blk(1)], *(v[:, :, blk(1)] for v in self.x))])

            def scalar(self, act):
                for whole, high, low in self.pieces:
                    act.activation(high, whole, ACT.Copy).then_inc(self.high, 1)

            def vector(self, dve):
                for n, (whole, high, low) in enumerate(self.pieces):
                    dve.wait_ge(self.high, n + 1)
                    dve.tensor_tensor(low, whole, high.bitcast(F32), ALU.subtract).then_inc(self.low, 1)

            def product(self, pe, out_, t, p):
                if t == 0:
                    pe.wait_ge(self.low, p + 2)
                if t == TB and p == 0:
                    pe.wait_ge(self.low, len(self.pieces))
                (xh, xl), (wh, wl) = self.x, self.w
                r = slice(2 * D * p, 2 * D * (p + 1))
                for k in range(DK):
                    mm = exact3(pe, out_, xh[:, k, tok(t)], xl[:, k, tok(t)], wh[:, k, r], wl[:, k, r],
                                k == 0, k == DK - 1)
                return mm

        def first_largest(chain, dve, value, onehot, best, order):
            def over(v):
                return v.unsqueeze(2).to_broadcast([P, T, E])
            chain(dve.tensor_reduce(best, value, AX.X, ALU.max))
            chain(dve.tensor_tensor(onehot, value, over(best), ALU.is_equal))
            chain(dve.tensor_tensor(onehot, onehot, rank[:, :, :], ALU.mult))
            chain(dve.tensor_reduce(order, onehot, AX.X, ALU.max))
            chain(dve.tensor_tensor(onehot, onehot, over(order), ALU.is_equal))

        def over(v):
            return v.unsqueeze(2).to_broadcast([P, T, E])

        def chained(dve, step):
            count = [0]

            def chain(op):
                count[0] += 1
                op.then_inc(step, 1)
                dve.wait_ge(step, count[0])
                return count[0]
            return chain

        def moe0_stage():
            with stage("moe0", 11 + NORM_SEMS + Split.SEMS) as (block, (
                    logged, centred, exped, step, weighted, turned, wt_ready, mm_done, added, bias_done, updated,
                    *sems)), ExitStack() as tmp:
                norm = Norm(sems[:NORM_SEMS], tmp)
                split = Split(sems[NORM_SEMS:], tmp)
                lg = sb("lg", [P, T, E], stack=tmp)
                ex = sb("ex", [P, T, E], stack=tmp)
                onehot = sb("onehot", [P, T, E], stack=tmp)
                wt = sb("wt", [P, T, E], stack=tmp)
                s1 = sb("s1", [P, 5, T], stack=tmp)
                wT = sb("wT", [E, T, P], stack=tmp)
                PAIRS = E // 2
                NBK = 5

                def where(n):
                    two, rest = divmod(n, 2 * PAIRS)
                    p, i = divmod(rest, 2)
                    return 2 * two + i, p, i

                def in_x(n, j):
                    t, p, i = where(n)
                    return (t // 2) * 2 * E + 2 * (2 * p + j) + i

                @block.tensor
                def _(pe):
                    loaded(pe, "e0")
                    for t in range(T):
                        for k in range(DK):
                            mm = pe.matmul(bank(6)[:, E * t:E * (t + 1)], xT[:, k, tok(t)], r0[:, k, :],
                                           start=(k == 0), stop=(k == DK - 1))
                    mm.then_inc(logged, 1)

                    def turn_weights():
                        pe.wait_ge(weighted, 1)
                        for u in range(T):
                            mm = pe.transpose(bank(5 if u < TB else 7)[0:E, tok(u % TB)], wt[:, u, :], ident[:, :])
                        mm.then_inc(turned, 1)

                    def bias(t):
                        if t == 0:
                            pe.wait_ge(wt_ready, 2)
                        if t >= 2:
                            pe.wait_ge(updated, t - 1)
                        pe.matmul(bank(5 + t % 2, D), wT[:, t, :], e0_b[:, :], start=True,
                                  stop=True).then_inc(bias_done, 1)
                    for n in range(T * PAIRS):
                        t, p, i = where(n)
                        if n >= NBK:
                            pe.wait_ge(added, in_x(n - NBK, 1) + 1)
                        split.product(pe, bank(n % NBK), t, p).then_inc(mm_done, 1)
                        if n == NBK - 1:
                            turn_weights()
                        if t >= 2 and p == 0 and i == 1:
                            bias(t - 3)
                            bias(t - 2)
                    bias(T - 2)
                    bias(T - 1)
                    pe.wait_ge(updated, T)
                    norm.tensor(pe)

                @block.scalar
                def _(act):
                    loaded(act, "e0")
                    split.scalar(act)
                    act.wait_ge(centred, 1)
                    act.activation(ex[:, :, :], lg[:, :, :], ACT.Exp).then_inc(exped, 1)
                    act.wait_ge(turned, 1)
                    act.activation(wT[:, 0:TB, :], bank(5)[0:E, :].rearrange("p (t q) -> p t q", q=P),
                                   ACT.Copy).then_inc(wt_ready, 1)
                    act.activation(wT[:, TB:T, :], bank(7)[0:E, :].rearrange("p (t q) -> p t q", q=P),
                                   ACT.Copy).then_inc(wt_ready, 1)
                    norm.scalar(act)

                @block.gpsimd
                def _(pool):
                    norm.gpsimd(pool)

                @block.vector
                def _(dve):
                    chain = chained(dve, step)
                    total, inverse, best, order, gate = (s1[:, i, :] for i in range(5))
                    split.vector(dve)
                    dve.wait_ge(logged, 1)
                    chain(dve.tensor_tensor(lg[:, :, :], bank(6, T * E).rearrange("p (t e) -> p t e", e=E),
                                            cols[:, COLS["rb0"]:COLS["rb0"] + E].unsqueeze(1).to_broadcast([P, T, E]),
                                            ALU.add))
                    chain(dve.tensor_reduce(total, lg[:, :, :], AX.X, ALU.max))
                    dve.tensor_tensor(lg[:, :, :], lg[:, :, :], over(total), ALU.subtract).then_inc(centred, 1)
                    dve.wait_ge(exped, 1)
                    chain(dve.tensor_reduce(total, ex[:, :, :], AX.X, ALU.add))
                    chain(dve.reciprocal(inverse, total))
                    first_largest(chain, dve, ex[:, :, :], onehot[:, :, :], best, order)
                    chain(dve.tensor_tensor(gate, inverse, best, ALU.mult))
                    chain(dve.tensor_scalar(gate, gate, tg[:, 4:5], None, ALU.mult))
                    dve.tensor_tensor(wt[:, :, :], onehot[:, :, :], over(gate), ALU.mult).then_inc(weighted, 1)
                    dve.wait_ge(weighted, 1)
                    for m in range(T * E):
                        two, rest = divmod(m, 2 * E)
                        e, i = divmod(rest, 2)
                        t = 2 * two + i
                        n = two * 2 * PAIRS + e // 2 * 2 + i
                        dve.wait_ge(mm_done, n + 1)
                        if e:
                            dve.wait_ge(added, m - 1)
                        dve.scalar_tensor_tensor(out=x[:, t, :], in0=bank(n % NBK)[:, e % 2 * D:(e % 2 + 1) * D],
                                                 scalar=wt[:, t, e:e + 1], in1=x[:, t, :],
                                                 op0=ALU.mult, op1=ALU.add).then_inc(added, 1)
                        if e < E - 1 or i == 0:
                            continue
                        for u in (t - 1, t):
                            dve.wait_ge(bias_done, u + 1)
                            dve.wait_ge(added, m + u - t + 1)
                            dve.tensor_tensor(x[:, u, :], bank(5 + u % 2, D), x[:, u, :], ALU.add).then_inc(updated, 1)
                        for u in (t - 1, t):
                            dve.wait_ge(updated, u + 1)
                            norm.vector(dve, u)

        def moe1_stage():
            with stage("moe1", 16 + NORM_SEMS + Split.SEMS) as (block, (
                    logged, centred, exped, step, weighted, up_done, silued, gated_h, turned, evac, down, updated,
                    arrived, down_high, down_low, g_low, *sems)), ExitStack() as tmp:
                norm = Norm(sems[:NORM_SEMS], tmp)
                split = Split(sems[NORM_SEMS:], tmp)
                lg = sb("lg", [P, T, E], stack=tmp)
                ex = sb("ex", [P, T, E], stack=tmp)
                one1 = sb("one1", [P, T, E], stack=tmp)
                one2 = sb("one2", [P, T, E], stack=tmp)
                wt = sb("wt", [P, T, E], stack=tmp)
                s1 = sb("s1", [P, 5, T], stack=tmp)
                sl = sb("sl", [P, 2, 2, P], stack=tmp)
                gh = sb("gh", [P, 2, 2, P], stack=tmp)
                gT_h, gT_l = (sb(f"gT_{j}", [P, 2, 2, P], F32R, stack=tmp) for j in "hl")
                down_h, down_l = (sb(f"down_{j}", [P, E, D], F32R, stack=tmp) for j in "hl")
                PAIRS = E // 2
                N = T * PAIRS

                @block.sync
                def _(sp):
                    sp.wait_ge(split.low, len(split.pieces))
                    reload(sp, arrived, chunked(w2_kv, a["L2_xattn_Wkv"]))

                @block.tensor
                def _(pe):
                    loaded(pe, "e1")
                    for t in range(T):
                        for k in range(DK):
                            mm = pe.matmul(bank(7)[:, E * t:E * (t + 1)], xT[:, k, tok(t)], r1[:, k, :],
                                           start=(k == 0), stop=(k == DK - 1))
                    mm.then_inc(logged, 1)

                    def up(n):
                        t, p = divmod(n, PAIRS)
                        if n >= 3:
                            pe.wait_ge(gated_h, n - 2)
                        split.product(pe, bank(n % 3), t, p).then_inc(up_done, 1)

                    def turn_pair(n):
                        pe.wait_ge(gated_h, n + 1)
                        if n >= 2:
                            pe.wait_ge(g_low, n - 1)
                        for i in range(2):
                            mm = pe.transpose(bank(3 + n % 2)[:, tok(i)], gh[:, n % 2, i, :], ident[:, :])
                        mm.then_inc(turned, 1)

                    def down_pair(n):
                        t, p = divmod(n, PAIRS)
                        pe.wait_ge(g_low, n + 1)
                        if n == 0:
                            pe.wait_ge(down_low, 1)
                        if p == 0 and t >= 2:
                            pe.wait_ge(updated, t - 1)
                        for i in range(2):
                            e = 2 * p + i
                            mm = exact3(pe, bank(5 + t % 2, D), gT_h[:, n % 2, i, :], gT_l[:, n % 2, i, :],
                                        down_h[:, e, :], down_l[:, e, :], e == 0, e == E - 1)
                        mm.then_inc(down, 1)
                    for n in range(N + 3):
                        if n < N:
                            up(n)
                        if 2 <= n < N + 2:
                            turn_pair(n - 2)
                        if n >= 3:
                            down_pair(n - 3)
                    norm.tensor(pe)

                @block.scalar
                def _(act):
                    split.scalar(act)
                    act.wait_ge(centred, 1)
                    act.activation(ex[:, :, :], lg[:, :, :], ACT.Exp).then_inc(exped, 1)
                    loaded(act, "e1")
                    act.activation(down_h[:, :, :], e1_down[:, :, :], ACT.Copy).then_inc(down_high, 1)
                    act.wait_ge(weighted, 1)

                    def evacuate(n):
                        act.wait_ge(turned, n + 1)
                        if n >= 2:
                            act.wait_ge(down, n - 1)
                        act.activation(gT_h[:, n % 2, :, :], bank(3 + n % 2, D).rearrange("p (i q) -> p i q", q=P),
                                       ACT.Copy).then_inc(evac, 1)
                    for n in range(N + 2):
                        if n < N:
                            t, p = divmod(n, PAIRS)
                            act.wait_ge(up_done, n + 1)
                            if n >= 2:
                                act.wait_ge(gated_h, n - 1)
                            for i in range(2):
                                e = 2 * p + i
                                act.activation(sl[:, n % 2, i, :], bank(n % 3)[:, i * D:i * D + P], ACT.Silu,
                                               scale=wt[:, t, e:e + 1]).then_inc(silued, 1)
                        if n >= 2:
                            evacuate(n - 2)
                    norm.scalar(act)

                @block.gpsimd
                def _(pool):
                    norm.gpsimd(pool)

                @block.vector
                def _(dve):
                    chain = chained(dve, step)
                    total, inverse, best, order, gate = (s1[:, i, :] for i in range(5))
                    split.vector(dve)
                    dve.wait_ge(logged, 1)
                    chain(dve.tensor_copy(lg[:, :, :], bank(7, T * E).rearrange("p (t e) -> p t e", e=E)))
                    chain(dve.tensor_reduce(total, lg[:, :, :], AX.X, ALU.max))
                    dve.tensor_tensor(lg[:, :, :], lg[:, :, :], over(total), ALU.subtract).then_inc(centred, 1)
                    dve.wait_ge(exped, 1)
                    chain(dve.tensor_reduce(total, ex[:, :, :], AX.X, ALU.add))
                    chain(dve.reciprocal(inverse, total))
                    first_largest(chain, dve, ex[:, :, :], one1[:, :, :], best, order)
                    chain(dve.scalar_tensor_tensor(out=lg[:, :, :], in0=one1[:, :, :], scalar=-4.0,
                                                   in1=ex[:, :, :], op0=ALU.mult, op1=ALU.add))
                    first_largest(chain, dve, lg[:, :, :], one2[:, :, :], best, order)
                    chain(dve.tensor_tensor(one1[:, :, :], one1[:, :, :], one2[:, :, :], ALU.add))
                    chain(dve.tensor_tensor(one1[:, :, :], one1[:, :, :], ex[:, :, :], ALU.mult))
                    dve.tensor_tensor(wt[:, :, :], one1[:, :, :], over(inverse), ALU.mult).then_inc(weighted, 1)
                    dve.wait_ge(weighted, 1)

                    def low_part(n):
                        dve.wait_ge(evac, n + 1)
                        if n >= 2:
                            dve.wait_ge(down, n - 1)
                        dve.tensor_tensor(gT_l[:, n % 2, :, :], bank(3 + n % 2, D).rearrange("p (i q) -> p i q", q=P),
                                          gT_h[:, n % 2, :, :].bitcast(F32), ALU.subtract).then_inc(g_low, 1)

                    def update(t):
                        dve.wait_ge(down, PAIRS * (t + 1))
                        dve.scalar_tensor_tensor(out=x[:, t, :], in0=bank(5 + t % 2, D), scalar=tg[:, 5:6],
                                                 in1=x[:, t, :], op0=ALU.mult, op1=ALU.add).then_inc(updated, 1)
                        dve.wait_ge(updated, t + 1)
                        norm.vector(dve, t)
                    for n in range(N):
                        t, p = divmod(n, PAIRS)
                        dve.wait_ge(silued, 2 * (n + 1))
                        if n >= 2:
                            dve.wait_ge(turned, n - 1)
                        for i in range(2):
                            e = 2 * p + i
                            op = dve.scalar_tensor_tensor(out=gh[:, n % 2, i, :],
                                                          in0=bank(n % 3)[:, i * D + P:(i + 1) * D],
                                                          scalar=wt[:, t, e:e + 1], in1=sl[:, n % 2, i, :],
                                                          op0=ALU.mult, op1=ALU.mult)
                        op.then_inc(gated_h, 1)
                        if n == 0:
                            dve.wait_ge(down_high, 1)
                            dve.tensor_tensor(down_l[:, :, :], e1_down[:, :, :], down_h[:, :, :].bitcast(F32),
                                              ALU.subtract).then_inc(down_low, 1)
                        if n >= 2:
                            low_part(n - 2)
                        if n >= PAIRS + 2 and n % PAIRS == 2:
                            update(t - 1)
                    low_part(N - 2)
                    low_part(N - 1)
                    update(T - 1)

        VW = HG * (DH1 + 1)

        def small_prepare_stage(name, group, bias_row, clip, wq, wk, wv, bq, qT, qTb, kbd, kbdb, vbig, shift):
            with stage(name, 15) as (block, (q_done, q_evac, q_bf, k_done, k_evac, k_bf, v_done, v_evac, biased,
                                             scored, maxed, capped, turned, shifted, arrived)), ExitStack() as tmp:
                mx = sb("mx", [P, T, H1], stack=tmp)
                HALF = GM // 2

                @block.sync
                def _(sp):
                    if clip:
                        reload(sp, arrived, moe1_weights())
                VALUES_AT = {2 * ch + 1: ch for ch in range(1, len(CH))}

                @block.tensor
                def _(pe):
                    def queries(i):
                        c, g = divmod(i, G)
                        if i >= 2:
                            pe.wait_ge(q_evac, i - 1)
                        for k in range(DK):
                            mm = pe.matmul(bank(i % 2), wq[:, k, tok(g)], xT[:, k, blk(c)],
                                           start=(k == 0), stop=(k == DK - 1))
                        mm.then_inc(q_done, 1)

                    def values(ch):
                        lo, w = CH[ch]
                        if ch >= 2:
                            pe.wait_ge(v_evac, ch - 1)
                        for kc, r in enumerate((P, C1 + 1)):
                            mm = pe.matmul(bank(2 + ch % 2)[0:w, 0:D], ctx_rep[0:r, kc, lo:lo + w], wv[0:r, kc, :],
                                           start=(kc == 0), stop=(kc == 1))
                        mm.then_inc(v_done, 1)

                    def score_max(n):
                        t, g = divmod(n, G)
                        pe.wait_ge(q_bf, G * (t // TB) + g + 1)
                        if n < G:
                            pe.wait_ge(k_bf, g + 1)
                        if n == 1:
                            pe.wait_ge(k_evac, G)
                        if n >= 2:
                            pe.wait_ge(maxed, n - 1)
                        for i in range(2):
                            mm = pe.matmul(bank(4 + 2 * (n % 2) + i, HALF), qTb[:, g, tok(t)],
                                           kbdb[:, g, i * HALF:(i + 1) * HALF], start=True, stop=True)
                        mm.then_inc(scored, 1)

                    def turn_max(c):
                        if clip:
                            pe.wait_ge(capped, c + 1)
                        else:
                            pe.wait_ge(maxed, G * TB * (c + 1))
                        pe.wait_ge(q_evac, G * NB)
                        for u in tiles_of(c):
                            mm = pe.transpose(bank(c)[0:H1, tok(u % TB)], mx[:, u, :], ident[:, :])
                        mm.then_inc(turned, 1)
                    loaded(pe, group)
                    for g in range(G):
                        for kc, r in enumerate((P, C1 + 1)):
                            mm = pe.matmul(bank(6 + g, M), wk[0:r, kc, tok(g)], ctxT[0:r, kc, :],
                                           start=(kc == 0), stop=(kc == 1))
                        mm.then_inc(k_done, 1)
                    for i in range(G):
                        queries(i)
                    values(0)
                    for n in range(G * T):
                        score_max(n)
                        if n < G:
                            queries(G + n)
                        if n in VALUES_AT:
                            values(VALUES_AT[n])
                        if n == G * TB + 2:
                            turn_max(0)
                    turn_max(1)

                @block.scalar
                def _(act):
                    for i in range(G * NB):
                        c, g = divmod(i, G)
                        act.wait_ge(q_done, i + 1)
                        act.activation(qTb[:, g, blk(c)], bank(i % 2), ACT.Identity,
                                       bias=col(bq, g)).then_inc(q_bf, 1)
                        act.activation(qT[:, g, blk(c)], bank(i % 2), ACT.Identity,
                                       bias=col(bq, g)).then_inc(q_evac, 1)
                    for c in range(NB):
                        act.wait_ge(turned, c + 1)
                        act.activation(shift[:, blk(c)], bank(c)[0:H1, :], ACT.Copy,
                                       scale=-1.0).then_inc(shifted, 1)

                @block.vector
                def _(dve):
                    def values(ch):
                        lo, w = CH[ch]
                        dve.wait_ge(v_done, ch + 1)
                        v = vbig[0:w, ch, :, :].rearrange("p g (h d) -> p g h d", d=DH1 + 1)
                        for g in range(G):
                            op = dve.tensor_tensor(v[:, g, :, 0:DH1],
                                                   bank(2 + ch % 2)[0:w, g * P:(g + 1) * P].rearrange(
                                                       "p (h d) -> p h d", d=DH1),
                                                   head_of_row[0:w, ch, :].unsqueeze(2).to_broadcast([w, HG, DH1]),
                                                   ALU.mult)
                        op.then_inc(v_evac, 1)

                    def largest(n):
                        t, g = divmod(n, G)
                        dve.wait_ge(scored, n + 1)
                        r = psum[:, 2048 + 1024 * (n % 2):3072 + 1024 * (n % 2)].rearrange("p (i z) -> p i z", i=2)
                        dve.tensor_reduce(mx[:, t, HG * g:HG * (g + 1)].rearrange("p (i h) -> p i h", i=2),
                                          r[:, :, 0:HALF].rearrange("p i (h m) -> p i h m", m=M),
                                          AX.X, ALU.max).then_inc(maxed, 1)
                        if clip and t % TB == TB - 1 and g == G - 1:
                            bound = CLAMP * float(DH1) ** 0.5
                            now = mx[:, t - TB + 1:t + 1, :]
                            dve.wait_ge(maxed, G * (t + 1))
                            dve.tensor_scalar(now, now, bound, -bound, ALU.min, ALU.max).then_inc(capped, 1)
                    for g in range(G):
                        dve.wait_ge(k_done, g + 1)
                        dve.tensor_tensor(kbd[:, g, :].rearrange("p (h m) -> p h m", m=M),
                                          bank(6 + g, M).unsqueeze(1).to_broadcast([P, HG, M]),
                                          head_of_feature[:, :].unsqueeze(2).to_broadcast([P, HG, M]),
                                          ALU.mult).then_inc(k_evac, 1)
                    for g in range(G):
                        dve.wait_ge(k_evac, g + 1)
                        dve.tensor_copy(kbdb[:, g, :], kbd[:, g, :]).then_inc(k_bf, 1)
                    values(0)
                    for n in range(G * T):
                        largest(n)
                        if n in VALUES_AT:
                            values(VALUES_AT[n])

                @block.gpsimd
                def _(pool):
                    for g in range(G):
                        pool.tensor_copy(vbig[:, :, g, DH1::DH1 + 1], head_of_row[:, :, :])
                    add_bias(pool, bias_row, biased)

        def small_attend_stage(name, qT, kbd, vbig, shift, o_tok):
            with stage(name, 5) as (block, (sdone, edone, pv, recd, ok)), ExitStack() as tmp:
                NPT = 4
                pt = sb("pt", [P, NPT, BLK], stack=tmp)
                rc = sb("rc", [P, 2, TB, HG], stack=tmp)
                N = G * len(CH)

                def where(n):
                    c, i = divmod(n, N)
                    g, ch = divmod(i, len(CH))
                    return c, g, ch

                @block.tensor
                def _(pe):
                    def scores(n):
                        c, g, ch = where(n)
                        lo, w = CH[ch]
                        if n >= 4:
                            pe.wait_ge(edone, n - 3)
                        pe.matmul(bank(n % 4)[0:w, :], kbd[:, g, lo:lo + w], qT[:, g, blk(c)],
                                  start=True, stop=False)
                        pe.matmul(bank(n % 4)[0:w, :], pick_row[:, g, lo:lo + w], shift[:, blk(c)],
                                  start=False, stop=True).then_inc(sdone, 1)

                    def values(n):
                        c, g, ch = where(n)
                        lo, w = CH[ch]
                        u = c * G + g
                        pe.wait_ge(edone, n + 1)
                        if ch == 0 and u >= 2:
                            pe.wait_ge(ok, u - 1)
                        for q in range(TB):
                            mm = pe.matmul(bank(4 + 2 * (u % 2) + q // 2)[:, VW * (q % 2):VW * (q % 2 + 1)],
                                           pt[0:w, n % NPT, tok(q)], vbig[0:w, ch, g, :],
                                           start=(ch == 0 and q % 2 == 0), stop=(ch == len(CH) - 1),
                                           skip_group_check=True)
                        mm.then_inc(pv, 1)
                    for n in range(NB * N + 2):
                        if n < NB * N:
                            scores(n)
                        if n >= 2:
                            values(n - 2)

                @block.scalar
                def _(act):
                    for n in range(NB * N):
                        c, g, ch = where(n)
                        w = CH[ch][1]
                        act.wait_ge(sdone, n + 1)
                        if n >= NPT:
                            act.wait_ge(pv, n - NPT + 1)
                        act.activation(pt[0:w, n % NPT, :], bank(n % 4)[0:w, :], ACT.Exp,
                                       scale=float(DH1) ** -0.5).then_inc(edone, 1)

                @block.vector
                def _(dve):
                    for u in range(NB * G):
                        c, g = divmod(u, G)
                        dve.wait_ge(pv, len(CH) * (u + 1))
                        for i in range(2):
                            o = bank(4 + 2 * (u % 2) + i, 2 * VW).rearrange("p (q h d) -> p q h d", q=2, d=DH1 + 1)
                            r = rc[:, u % 2, 2 * i:2 * i + 2, :]
                            dve.reciprocal(r.unsqueeze(3), o[:, :, :, DH1:]).then_inc(recd, 1)
                            dve.wait_ge(recd, 2 * u + i + 1)
                            for q in range(2):
                                op = dve.tensor_tensor(
                                    o_tok[:, c * TB + 2 * i + q, g * P:(g + 1) * P].rearrange(
                                        "p (h d) -> p h d", d=DH1),
                                    o[:, q, :, 0:DH1], r[:, q, :].unsqueeze(2).to_broadcast([P, HG, DH1]), ALU.mult)
                        op.then_inc(ok, 1)

        def clipped_attend_stage(name, qT, kbd, vbig, shift, o_tok):
            with stage(name, 7) as (block, (sdone, clipped, shifted, edone, pv, recd, ok)), ExitStack() as tmp:
                NPT = 4
                sc = sb("sc", [P, NPT, BLK], stack=tmp)
                pt = sb("pt", [P, NPT, BLK], stack=tmp)
                rc = sb("rc", [P, 2, TB, HG], stack=tmp)
                N = G * len(CH)
                BOUND = CLAMP * float(DH1) ** 0.5

                def where(n):
                    c, i = divmod(n, N)
                    g, ch = divmod(i, len(CH))
                    return c, g, ch

                @block.tensor
                def _(pe):
                    def scores(n):
                        c, g, ch = where(n)
                        lo, w = CH[ch]
                        if n >= 2:
                            pe.wait_ge(shifted, n - 1)
                        pe.matmul(bank(n % 2)[0:w, :], kbd[:, g, lo:lo + w], qT[:, g, blk(c)],
                                  start=True, stop=True)
                        pe.matmul(bank(2 + n % 2)[0:w, :], pick_row[:, g, lo:lo + w], shift[:, blk(c)],
                                  start=True, stop=True).then_inc(sdone, 1)

                    def values(n):
                        c, g, ch = where(n)
                        lo, w = CH[ch]
                        u = c * G + g
                        pe.wait_ge(edone, n + 1)
                        if ch == 0 and u >= 2:
                            pe.wait_ge(ok, u - 1)
                        for q in range(TB):
                            mm = pe.matmul(bank(4 + 2 * (u % 2) + q // 2)[:, VW * (q % 2):VW * (q % 2 + 1)],
                                           pt[0:w, n % NPT, tok(q)], vbig[0:w, ch, g, :],
                                           start=(ch == 0 and q % 2 == 0), stop=(ch == len(CH) - 1),
                                           skip_group_check=True)
                        mm.then_inc(pv, 1)
                    for n in range(NB * N + 3):
                        if n < NB * N:
                            scores(n)
                        if n >= 3:
                            values(n - 3)

                @block.scalar
                def _(act):
                    for n in range(NB * N):
                        c, g, ch = where(n)
                        w = CH[ch][1]
                        act.wait_ge(shifted, n + 1)
                        if n >= NPT:
                            act.wait_ge(pv, n - NPT + 1)
                        act.activation(pt[0:w, n % NPT, :], sc[0:w, n % NPT, :], ACT.Exp,
                                       scale=float(DH1) ** -0.5).then_inc(edone, 1)

                @block.vector
                def _(dve):
                    def normalise(u):
                        c, g = divmod(u, G)
                        dve.wait_ge(pv, len(CH) * (u + 1))
                        for i in range(2):
                            o = bank(4 + 2 * (u % 2) + i, 2 * VW).rearrange("p (q h d) -> p q h d", q=2, d=DH1 + 1)
                            r = rc[:, u % 2, 2 * i:2 * i + 2, :]
                            dve.reciprocal(r.unsqueeze(3), o[:, :, :, DH1:]).then_inc(recd, 1)
                            dve.wait_ge(recd, 2 * u + i + 1)
                            for q in range(2):
                                op = dve.tensor_tensor(
                                    o_tok[:, c * TB + 2 * i + q, g * P:(g + 1) * P].rearrange(
                                        "p (h d) -> p h d", d=DH1),
                                    o[:, q, :, 0:DH1], r[:, q, :].unsqueeze(2).to_broadcast([P, HG, DH1]), ALU.mult)
                        op.then_inc(ok, 1)
                    for n in range(NB * N):
                        w = CH[where(n)[2]][1]
                        dve.wait_ge(sdone, n + 1)
                        if n >= NPT:
                            dve.wait_ge(edone, n - NPT + 1)
                        dve.tensor_scalar(sc[0:w, n % NPT, :], bank(n % 2)[0:w, :], BOUND, -BOUND,
                                          ALU.min, ALU.max).then_inc(clipped, 1)
                        dve.wait_ge(clipped, n + 1)
                        dve.tensor_tensor(sc[0:w, n % NPT, :], sc[0:w, n % NPT, :], bank(2 + n % 2)[0:w, :],
                                          ALU.add).then_inc(shifted, 1)
                        if n >= len(CH) + 3 and (n - 3) % len(CH) == 0:
                            normalise((n - 3) // len(CH) - 1)
                    normalise(NB * G - 1)

        KC2 = H2 * DH2 // P

        def attend2_stage(kT, kTb, v_aug):
            with stage("attend2", 31 + NORM_SEMS) as (block, (
                    q_done, q_evac, q_bf, scored, maxed, turned, shifted, sdone, edone, pv, recd, ok, o_turned,
                    o_high, o_rest, summed, updated, arrived, k_done, k_evac, k_bf, v_done, v_evac, k_cleared,
                    v_cleared, xn_cleared, biased,
                    q_low, k_low, w_high, w_low, *sems)), ExitStack() as tmp:
                norm = Norm(sems, tmp)
                qT_h, qT_l = (sb(f"qT2_{j}", [P, 3, BLK], F32R, stack=tmp) for j in "hl")
                qTb = sb("qTb2", [P, 3, BLK], BF16, stack=tmp)
                o_tok = sb("o2", [P, TB, H2 * DH2], stack=tmp)
                oT_h, oT_l = (sb(f"oT2_{j}", [P, 2, KC2, P], F32R, stack=tmp) for j in "hl")
                wo_h, wo_l = (sb(f"w2_o_{j}", [P, KC2, D], F32R, stack=tmp) for j in "hl")
                kT_h, kT_l = kT
                mx = sb("mx", [P, TB, 2], stack=tmp)
                shift = sb("shift", [2, BLK], BF16, stack=tmp)
                rc = sb("rc", [P, 2, TB], stack=tmp)
                UNITS = NB * KC2
                KH = KC2 // 2

                @block.sync
                def _(sp):
                    sp.wait_ge(v_done, 2)
                    reload(sp, arrived, moe0_weights())

                @block.tensor
                def _(pe):
                    def queries(u):
                        c, k = divmod(u, KC2)
                        if u:
                            pe.wait_ge(q_low, u)
                        if u > KC2 and u % KC2 == 2:
                            pe.wait_ge(o_rest, 2 * TB * (u // KC2))
                        for kc in range(DK):
                            mm = pe.matmul(bank(0), w2_q[:, kc, tok(k)], xT[:, kc, blk(c)],
                                           start=(kc == 0), stop=(kc == DK - 1))
                        mm.then_inc(q_done, 1)

                    def score_max(u):
                        k = u % KC2
                        pe.wait_ge(q_bf, u + 1)
                        for i in range(2):
                            r = halves(i)[0]
                            if u:
                                pe.wait_ge(maxed, 2 * (u - 1) + i + 1)
                            for t in range(TB):
                                mm = pe.matmul(bank(1 + i)[:, t * M:(t + 1) * M], qTb[r, u % 3, tok(t)],
                                               kTb[r, k, :], start=True, stop=True, skip_group_check=True)
                            mm.then_inc(scored, 1)

                    def turn_max(u):
                        pe.wait_ge(maxed, 2 * (u + 1))
                        if u:
                            pe.wait_ge(shifted, u)
                        if u > KC2 and u % KC2 == 1:
                            pe.wait_ge(o_rest, 2 * TB * (u // KC2))
                        for t in range(TB):
                            mm = pe.transpose(bank(3)[0:2, tok(t)], mx[:, t, :], ident[:, :])
                        mm.then_inc(turned, 1)

                    def scores(u, i):
                        k = u % KC2
                        n = 2 * u + i
                        if i == 0:
                            pe.wait_ge(shifted, u + 1)
                        if n >= 2:
                            pe.wait_ge(edone, n - 1)
                        if i == 0:
                            pe.wait_ge(q_low, u + 1)
                        exact3(pe, bank(4 + i)[0:M, :], kT_h[:, 2 * k + i, :], kT_l[:, 2 * k + i, :],
                               qT_h[:, u % 3, :], qT_l[:, u % 3, :], True, False)
                        pe.matmul(bank(4 + i)[0:M, :], pick2[:, i, :], shift[:, :], start=False,
                                  stop=True).then_inc(sdone, 1)

                    def values(u, i):
                        n = 2 * u + i
                        pe.wait_ge(edone, n + 1)
                        if n >= 2:
                            pe.wait_ge(ok, n - 1)
                        if u >= KC2 and u % KC2 == 0:
                            pe.wait_ge(updated, TB * (u // KC2))
                        if n == 0:
                            pe.wait_ge(v_evac, 2)
                            pe.wait_ge(xn_cleared, 1)
                        for q in range(TB):
                            mm = pe.matmul(bank(6 + i)[:, q * (DH2 + 1):(q + 1) * (DH2 + 1)], probs(n)[:, tok(q)],
                                           v_aug[:, 2 * (u % KC2) + i, :], start=True, stop=True)
                        mm.then_inc(pv, 1)

                    def turn_tile(t):
                        if t:
                            pe.wait_ge(o_rest, 2 * t)
                        for k in range(KC2):
                            mm = pe.transpose(bank(0 if k < KH else 3)[:, tok(k % KH)], o_tok[:, t % TB, tok(k)],
                                              ident[:, :])
                            if k % KH == KH - 1:
                                mm.then_inc(o_turned, 1)

                    def project(c):
                        pe.wait_ge(ok, 2 * KC2 * (c + 1))
                        pe.wait_ge(q_low, min(UNITS, KC2 * (c + 1) + 2))
                        pe.wait_ge(shifted, min(UNITS, KC2 * (c + 1) + 1))
                        turn_tile(c * TB)
                        for t in tiles_of(c):
                            if t % TB + 1 < TB:
                                turn_tile(t + 1)
                            pe.wait_ge(o_rest, 2 * t + 2)
                            if t == 0:
                                pe.wait_ge(w_low, 1)
                            if t >= 2:
                                pe.wait_ge(updated, t - 1)
                            for k in range(KC2):
                                mm = exact3(pe, bank(6 + t % 2, D), oT_h[:, t % 2, k, :], oT_l[:, t % 2, k, :],
                                            wo_h[:, k, :], wo_l[:, k, :], k == 0, k == KC2 - 1)
                            mm.then_inc(summed, 1)
                    loaded(pe, "w2")
                    for j in range(KC2):
                        for kc, r in enumerate((P, C1)):
                            mm = pe.matmul(bank(4 + j // 4)[:, (j % 4) * M:(j % 4 + 1) * M], w2_kv[0:r, kc, tok(j)],
                                           ctxT[0:r, kc, :], start=(kc == 0), stop=(kc == 1))
                        if j % 4 == 3:
                            mm.then_inc(k_done, 1)
                    queries(0)
                    for i in range(2):
                        for kc, r in enumerate((P, C1)):
                            mm = pe.matmul(bank(6 + i)[0:M, :], ctxT[0:r, kc, :],
                                           w2_kv[0:r, kc, H2 * DH2 + 512 * i:H2 * DH2 + 512 * (i + 1)],
                                           start=(kc == 0), stop=(kc == 1))
                        mm.then_inc(v_done, 1)
                    queries(1)
                    pe.wait_ge(k_bf, 2)
                    pe.wait_ge(k_low, 4)
                    score_max(0)
                    turn_max(0)
                    for u in range(UNITS):
                        scores(u, 0)
                        if u + 1 < UNITS:
                            score_max(u + 1)
                        scores(u, 1)
                        if u and u % KC2 == 0:
                            project(u // KC2 - 1)
                        values(u, 0)
                        if u + 2 < UNITS:
                            queries(u + 2)
                        if u + 1 < UNITS:
                            turn_max(u + 1)
                        values(u, 1)
                    project(NB - 1)
                    norm.tensor(pe)

                @block.scalar
                def _(act):
                    def queries(u):
                        act.wait_ge(q_done, u + 1)
                        if u >= 3:
                            act.wait_ge(sdone, 2 * (u - 2))
                        act.activation(qT_h[:, u % 3, :], bank(0), ACT.Copy).then_inc(q_evac, 1)

                    def queries_bf(u):
                        if u >= 3:
                            act.wait_ge(scored, 2 * (u - 2))
                        act.activation(qTb[:, u % 3, :], bank(0), ACT.Copy).then_inc(q_bf, 1)

                    def shift_rows(u):
                        act.wait_ge(turned, u + 1)
                        if u:
                            act.wait_ge(sdone, 2 * u)
                        act.activation(shift[:, :], bank(3)[0:2, :], ACT.Copy, scale=-1.0).then_inc(shifted, 1)
                    def high_parts(c):
                        for t in tiles_of(c):
                            for i in range(2):
                                act.wait_ge(o_turned, 2 * t + i + 1)
                                if t >= 2:
                                    act.wait_ge(summed, t - 1)
                                act.activation(oT_h[:, t % 2, KH * i:KH * (i + 1), :],
                                               bank(3 * i).rearrange("p (k q) -> p k q", q=P),
                                               ACT.Copy).then_inc(o_high, 1)
                    for i in range(2):
                        act.wait_ge(k_done, i + 1)
                        if i == 0:
                            act.wait_ge(k_cleared, 2)
                        for p in range(2):
                            r = slice(DH2 * p, DH2 * (p + 1))
                            act.activation(kT_h[r, 8 * i + p:8 * i + 8:2, :],
                                           bank(4 + i, 4 * M)[r, :].rearrange("p (j m) -> p j m", m=M),
                                           ACT.Copy).then_inc(k_evac, 1)
                        if i == 0:
                            queries(0)
                            queries_bf(0)
                    queries(1)
                    queries_bf(1)
                    shift_rows(0)
                    for u in range(UNITS):
                        for i in range(2):
                            n = 2 * u + i
                            act.wait_ge(sdone, n + 1)
                            if n >= NPT:
                                act.wait_ge(pv, n - NPT + 1)
                            elif n == 0:
                                act.wait_ge(xn_cleared, 1)
                            act.activation(probs(n)[0:M, :], bank(4 + i)[0:M, :], ACT.Exp,
                                           scale=float(DH2) ** -0.5).then_inc(edone, 1)
                        if u and u % KC2 == 0:
                            high_parts(u // KC2 - 1)
                        if u == 1:
                            act.activation(wo_h[:, :, :], w2_o[:, :, :], ACT.Copy).then_inc(w_high, 1)
                        if u + 2 < UNITS:
                            queries(u + 2)
                        if u + 1 < UNITS:
                            shift_rows(u + 1)
                        if u + 2 < UNITS:
                            queries_bf(u + 2)
                    high_parts(NB - 1)
                    norm.scalar(act)

                @block.gpsimd
                def _(pool):
                    pool.memset(xn[:, :, :], 0.0).then_inc(xn_cleared, 1)
                    add_bias(pool, "bproj", biased)
                    norm.gpsimd(pool)

                @block.vector
                def _(dve):
                    def largest(u):
                        for i in range(2):
                            dve.wait_ge(scored, 2 * u + i + 1)
                            if u:
                                dve.wait_ge(turned, u)
                            dve.tensor_reduce(mx[:, :, i], bank(1 + i, TB * M).rearrange("p (t m) -> p t m", m=M),
                                              AX.X, ALU.max).then_inc(maxed, 1)

                    def outputs(u, i):
                        n = 2 * u + i
                        k = u % KC2
                        dve.wait_ge(pv, n + 1)
                        if n >= 2:
                            dve.wait_ge(ok, n - 1)
                        o = bank(6 + i, TB * (DH2 + 1)).rearrange("p (q d) -> p q d", d=DH2 + 1)
                        dve.reciprocal(rc[:, i, :].unsqueeze(2), o[:, :, DH2:]).then_inc(recd, 1)
                        dve.wait_ge(recd, n + 1)
                        dve.tensor_tensor(o_tok[:, :, (2 * k + i) * DH2:(2 * k + i + 1) * DH2], o[:, :, 0:DH2],
                                          rc[:, i, :].unsqueeze(2).to_broadcast([P, TB, DH2]),
                                          ALU.mult).then_inc(ok, 1)

                    def low_parts(t):
                        for i in range(2):
                            ks = slice(KH * i, KH * (i + 1))
                            dve.wait_ge(o_high, 2 * t + i + 1)
                            dve.tensor_tensor(oT_l[:, t % 2, ks, :], bank(3 * i).rearrange("p (k q) -> p k q", q=P),
                                              oT_h[:, t % 2, ks, :].bitcast(F32), ALU.subtract).then_inc(o_rest, 1)

                    def queries_low(u):
                        dve.wait_ge(q_bf, u + 1)
                        dve.tensor_tensor(qT_l[:, u % 3, :], bank(0), qT_h[:, u % 3, :].bitcast(F32),
                                          ALU.subtract).then_inc(q_low, 1)

                    def update(c):
                        dve.wait_ge(biased, T)
                        low_parts(c * TB)
                        for t in tiles_of(c):
                            if t % TB + 1 < TB:
                                low_parts(t + 1)
                            dve.wait_ge(summed, t + 1)
                            dve.scalar_tensor_tensor(out=x[:, t, :], in0=bank(6 + t % 2, D), scalar=tg[:, 2:3],
                                                     in1=x[:, t, :], op0=ALU.mult, op1=ALU.add).then_inc(updated, 1)
                            dve.wait_ge(updated, t + 1)
                            norm.vector(dve, t)
                    for part in kT:
                        dve.memset(part[:, :, :].bitcast(F32), 0.0).then_inc(k_cleared, 1)
                    dve.memset(v_aug[:, :, :], 1.0).then_inc(v_cleared, 1)
                    dve.wait_ge(k_cleared, 2)
                    for i in range(2):
                        dve.wait_ge(k_evac, 2 * i + 2)
                        for p in range(2):
                            r = slice(DH2 * p, DH2 * (p + 1))
                            hs = slice(8 * i + p, 8 * i + 8, 2)
                            dve.tensor_tensor(kT_l[r, hs, :],
                                              bank(4 + i, 4 * M)[r, :].rearrange("p (j m) -> p j m", m=M),
                                              kT_h[r, hs, :].bitcast(F32), ALU.subtract).then_inc(k_low, 1)
                    for p in range(2):
                        r = slice(DH2 * p, DH2 * (p + 1))
                        dve.tensor_copy(kTb[r, :, :], kT_h[r, p::2, :].bitcast(F32)).then_inc(k_bf, 1)
                    queries_low(0)
                    dve.wait_ge(v_cleared, 1)
                    for i in range(2):
                        dve.wait_ge(v_done, i + 1)
                        dve.tensor_copy(v_aug[0:M, 8 * i:8 * i + 8, 0:DH2],
                                        bank(6 + i)[0:M, :].rearrange("p (h d) -> p h d", d=DH2)).then_inc(v_evac, 1)
                    queries_low(1)
                    largest(0)
                    for u in range(UNITS):
                        if u + 1 < UNITS:
                            largest(u + 1)
                        if u == 1:
                            dve.wait_ge(w_high, 1)
                            dve.tensor_tensor(wo_l[:, :, :], w2_o[:, :, :], wo_h[:, :, :].bitcast(F32),
                                              ALU.subtract).then_inc(w_low, 1)
                        if u and u % KC2 == 0:
                            update(u // KC2 - 1)
                        outputs(u, 0)
                        outputs(u, 1)
                        if u + 2 < UNITS:
                            queries_low(u + 2)
                    update(NB - 1)

        def lora_stage():
            with stage("lora", 5 + NORM_SEMS) as (block, (a_done, a_evac, summed, updated, biased, *sems)), \
                    ExitStack() as tmp:
                norm = Norm(sems, tmp)
                lowT = sb("lowT", [16, NB, BLK], stack=tmp)

                @block.tensor
                def _(pe):
                    loaded(pe, "lora")
                    for c in range(NB):
                        for k in range(DK):
                            mm = pe.matmul(bank(c)[0:16, :], lora_a[:, k, :], xT[:, k, blk(c)],
                                           start=(k == 0), stop=(k == DK - 1))
                        mm.then_inc(a_done, 1)
                    for t in range(T):
                        if t >= 4:
                            pe.wait_ge(updated, t - 3)
                        for k in range(DK):
                            pe.matmul(bank(2 + t % 4, D), xT[:, k, tok(t)], wq8[:, k, :], start=(k == 0), stop=False)
                        pe.wait_ge(a_evac, t // TB + 1)
                        pe.matmul(bank(2 + t % 4, D), lowT[:, t // TB, tok(t % TB)], lora_b[:, :], start=False,
                                  stop=True).then_inc(summed, 1)
                    norm.tensor(pe)

                @block.scalar
                def _(act):
                    for c in range(NB):
                        act.wait_ge(a_done, c + 1)
                        act.activation(lowT[:, c, :], bank(c)[0:16, :], ACT.Copy).then_inc(a_evac, 1)
                    norm.scalar(act)

                @block.gpsimd
                def _(pool):
                    add_bias(pool, "bias2", biased)
                    norm.gpsimd(pool)

                @block.vector
                def _(dve):
                    for t in range(T):
                        dve.wait_ge(summed, t + 1)
                        dve.wait_ge(biased, t + 1)
                        dve.scalar_tensor_tensor(out=x[:, t, :], in0=bank(2 + t % 4, D), scalar=tg[:, 6:7],
                                                 in1=x[:, t, :], op0=ALU.mult, op1=ALU.add).then_inc(updated, 1)
                        if t:
                            dve.wait_ge(updated, t)
                            norm.vector(dve, t - 1)
                    dve.wait_ge(updated, T)
                    norm.vector(dve, T - 1)

        def mlp3_stage(o_tok):
            with stage("mlp3", 6 + NORM_SEMS) as (block, (turned, evac, h_done, h_evac, summed, updated, *sems)), \
                    ExitStack() as tmp:
                norm = Norm(sems, tmp)
                oT = sb("oT", [P, DK, S], stack=tmp)
                hT = sb("hT", [P, 2 * DK, BLK], stack=tmp)
                HC = 2 * DK

                @block.tensor
                def _(pe):
                    loaded(pe, "w3")
                    for c in range(NB):
                        for k in range(DK):
                            for t in tiles_of(c):
                                mm = pe.transpose(bank(DK * c + k)[:, tok(t % TB)], o_tok[:, t, tok(k)], ident[:, :])
                            mm.then_inc(turned, 1)
                    for c in range(NB):
                        pe.wait_ge(evac, DK * (c + 1))
                        for m in range(HC):
                            n = c * HC + m
                            if n >= 2:
                                pe.wait_ge(h_evac, n - 1)
                            for k in range(DK):
                                mm = pe.matmul(bank(4 + n % 2), w3_1[:, k, tok(m)], oT[:, k, blk(c)],
                                               start=(k == 0), stop=(k == DK - 1))
                            mm.then_inc(h_done, 1)
                        pe.wait_ge(h_evac, HC * (c + 1))
                        for t in tiles_of(c):
                            if t >= 2:
                                pe.wait_ge(updated, t - 1)
                            for m in range(HC):
                                mm = pe.matmul(bank(6 + t % 2, D), hT[:, m, tok(t % TB)], w3_2[:, m, :],
                                               start=(m == 0), stop=(m == HC - 1))
                            mm.then_inc(summed, 1)
                    norm.tensor(pe)

                @block.scalar
                def _(act):
                    for c in range(NB):
                        for k in range(DK):
                            act.wait_ge(turned, DK * c + k + 1)
                            act.activation(oT[:, k, blk(c)], bank(DK * c + k), ACT.Copy).then_inc(evac, 1)
                    for c in range(NB):
                        if c:
                            act.wait_ge(summed, TB * c)
                        for m in range(HC):
                            n = c * HC + m
                            act.wait_ge(h_done, n + 1)
                            act.activation(hT[:, m, :], bank(4 + n % 2), ACT.Relu, bias=col("b1_3", m)
                                           ).then_inc(h_evac, 1)
                    norm.scalar(act)

                @block.gpsimd
                def _(pool):
                    norm.gpsimd(pool)

                @block.vector
                def _(dve):
                    for t in range(T):
                        dve.wait_ge(summed, t + 1)
                        dve.scalar_tensor_tensor(out=x[:, t, :], in0=bank(6 + t % 2, D), scalar=tg[:, 3:4],
                                                 in1=x[:, t, :], op0=ALU.mult, op1=ALU.add).then_inc(updated, 1)
                        dve.wait_ge(updated, t + 1)
                        norm.vector(dve, t)

        def dispatch_stage(b):
            with stage("dispatch", 11 + CONTEXT_SEMS) as (block, (
                    logged, centred, exped, step, chosen, counted, kept_x, placed, saved, xs,
                    measured, *sems)), \
                    ExitStack() as tmp:
                following = (b + 1) % B
                context = Context(sems, tmp, 2)
                lg = sb("lg", [P, T, E], stack=tmp)
                ex = sb("ex", [P, T, E], stack=tmp)
                onehot = sb("onehot", [P, T, E], stack=tmp)
                before = sb("before", [P, T + 1, E], stack=tmp)
                cum = sb("cum", [P, T, E], stack=tmp)
                s1 = sb("s1", [P, 8, T], stack=tmp)
                to = sb("to", [P, T], U32, stack=tmp)

                @block.sync
                def _(sp):
                    sp.dma_start(residual.rearrange("(b t p) d -> b p t d", p=P, t=T)[bass.ds(b, 1)]
                                 .rearrange("o p t d -> p (o t) d"), x[:, :, :]).then_inc(saved, 16)
                    context.sync(sp, following)
                    sp.wait_ge(saved, 16)
                    sp.dma_start(x[:, :, :], a["x"][bass.ds(following, 1), :, :]
                                 .rearrange("o (t p) d -> p (o t) d", p=P)).then_inc(xs, 16)
                    sp.wait_ge(xs, 16)

                @block.tensor
                def _(pe):
                    loaded(pe, "w3")
                    for t in range(T):
                        for k in range(DK):
                            mm = pe.matmul(bank(6)[:, E * t:E * (t + 1)], xT[:, k, tok(t)], r3[:, k, :],
                                           start=(k == 0), stop=(k == DK - 1))
                    mm.then_inc(logged, 1)
                    context.tensor(pe)
                    pe.wait_ge(chosen, 1)
                    flat = onehot[:, :, :].rearrange("p t e -> p (t e)")
                    pe.matmul(bank(0, T * E), upper[:, :], flat, start=True, stop=True)
                    pe.matmul(bank(1, T * E), ones_f[:, :], flat, start=True, stop=True).then_inc(counted, 1)

                @block.scalar
                def _(act):
                    act.wait_ge(centred, 1)
                    act.activation(ex[:, :, :], lg[:, :, :], ACT.Exp).then_inc(exped, 1)
                    context.scalar(act)

                @block.vector
                def _(dve):
                    chain = chained(dve, step)
                    total, inverse, best, order, base, pos, kept, far = (s1[:, i, :] for i in range(8))
                    context.vector_norm(dve)
                    dve.wait_ge(logged, 1)
                    chain(dve.tensor_copy(lg[:, :, :], bank(6, T * E).rearrange("p (t e) -> p t e", e=E)))
                    chain(dve.tensor_reduce(total, lg[:, :, :], AX.X, ALU.max))
                    dve.tensor_tensor(lg[:, :, :], lg[:, :, :], over(total), ALU.subtract).then_inc(centred, 1)
                    dve.wait_ge(exped, 1)
                    chain(dve.tensor_reduce(total, ex[:, :, :], AX.X, ALU.add))
                    chain(dve.reciprocal(inverse, total))
                    first_largest(chain, dve, ex[:, :, :], onehot[:, :, :], best, order)
                    dve.tensor_copy(before[:, 0, :], taken[:, :]).then_inc(chosen, 1)
                    dve.wait_ge(chosen, 1)
                    dve.wait_ge(counted, 1)
                    for t in range(T):
                        chain(dve.tensor_tensor(before[:, t + 1, :], before[:, t, :], bank(1)[:, E * t:E * (t + 1)],
                                                ALU.add))
                    chain(dve.tensor_copy(taken[:, :], before[:, T, :]))
                    chain(dve.tensor_tensor(cum[:, :, :], before[:, 0:T, :],
                                            bank(0, T * E).rearrange("p (t e) -> p t e", e=E), ALU.add))
                    chain(dve.tensor_tensor(cum[:, :, :], cum[:, :, :], onehot[:, :, :], ALU.mult))
                    chain(dve.tensor_reduce(pos, cum[:, :, :], AX.X, ALU.add))
                    chain(dve.tensor_scalar(pos, pos, 1.0, None, ALU.subtract))
                    chain(dve.tensor_scalar(base, order, -float(CAP), float(E * CAP), ALU.mult, ALU.add))
                    chain(dve.tensor_scalar(kept, pos, float(CAP), None, ALU.is_lt))
                    chain(dve.tensor_scalar(far, kept, -FAR, FAR, ALU.mult, ALU.add))
                    chain(dve.tensor_tensor(far, far, base, ALU.add))
                    chain(dve.tensor_tensor(far, far, pos, ALU.add))
                    dve.tensor_copy(to[:, :], far).then_inc(placed, 1)
                    context.vector_repeat(dve)
                    chain(dve.tensor_scalar(pos, pos, float(CAP - 1), None, ALU.min))
                    chain(dve.tensor_tensor(pos, pos, base, ALU.add))
                    dve.tensor_copy(slot[:, bass.ds(b * T, T)], pos).then_inc(kept_x, 1)
                    chain(dve.tensor_tensor(best, best, inverse, ALU.mult))
                    chain(dve.tensor_tensor(best, best, kept, ALU.mult))
                    chain(dve.tensor_scalar(best, best, tg[:, 7:8], None, ALU.mult))
                    dve.tensor_copy(prob[:, bass.ds(b * T, T)], best).then_inc(kept_x, 1)
                    context.vector_tokens(dve, xs, measured)

                @block.gpsimd
                def _(pool):
                    context.gpsimd(pool)
                    loaded(pool, "zero")
                    pool.wait_ge(placed, 1)
                    for t in range(T):
                        pool.indirect_dma_start(out=slots_in, out_offset=bass.IndirectOffsetOnAxis(
                            ap=to[:, t:t + 1], axis=0), in_=xn[:, t, :], in_offset=None,
                            bounds_check=SLOTS - 1, oob_is_err=False).then_inc(sent, 16)

        class Experts:
            def __init__(self, stack):
                self.w1 = sb("ew1", [P, DK, F3], stack=stack)
                self.w2 = sb("ew2", [P, FC, D], stack=stack)
                self.tokens = x
                self.w1s = [[sb(f"ew1_{i}{j}", [P, DK, F3], F32R, stack=stack) for j in "hl"] for i in range(2)]
                self.w2s = [[sb(f"ew2_{i}{j}", [P, FC, D], F32R, stack=stack) for j in "hl"] for i in range(2)]
                self.tT = [[sb(f"etT_{i}{j}", [P, DK, CAP], F32R, stack=stack) for j in "hl"] for i in range(2)]
                self.hT = [sb(f"ehT_{j}", [P, FC, CAP], F32R, stack=stack) for j in "hl"]
                self.b1 = [sb(f"eb1_{i}", [P, FC], stack=stack) for i in range(2)]
                self.b2 = [sb(f"eb2_{i}", [P, D], stack=stack) for i in range(2)]

        class NextExpert:
            SEMS = 8
            HALF = CAP // 2
            HT = HALF // P

            def __init__(self, sems, ex, i):
                (self.w_in, self.t_in, self.b_in, self.w_high, self.w_low, self.turned, self.t_high,
                 self.t_low) = sems
                self.ex, self.i = ex, i

            def sync(self, sp, e):
                ex, i = self.ex, self.i

                def of(ap):
                    return ap[bass.ds(e, 1)]
                sp.dma_start(ex.w1[:, :, :], of(a["L3_ffn_w1"]).rearrange("o (k p) f -> p (o k) f", p=P)
                             ).then_inc(self.w_in, 16)
                sp.dma_start(ex.w2[:, :, :], of(a["L3_ffn_w2"]).rearrange("o (f p) d -> p (o f) d", p=P)
                             ).then_inc(self.w_in, 16)
                sp.dma_start(ex.tokens[:, 0:CT, :], of(slots_in.rearrange("(e t p) d -> e p t d", e=E, p=P))
                             .rearrange("o p t d -> p (o t) d")).then_inc(self.t_in, 16)
                sp.dma_start(ex.b1[i][:, :], of(a["b1_cols"]).rearrange("o p f -> (o p) f")).then_inc(self.b_in, 16)
                sp.dma_start(ex.b2[i][:, :], of(a["L3_ffn_b2"]).to_broadcast([P, D])).then_inc(self.b_in, 16)

            def arrived(self, sp):
                sp.wait_ge(self.w_in, 32)
                sp.wait_ge(self.t_in, 16)
                sp.wait_ge(self.b_in, 32)

            def pieces(self):
                ex, i = self.ex, self.i
                h = FC // 2
                return ([(ex.w1[:, k, :], ex.w1s[i][0][:, k, :], ex.w1s[i][1][:, k, :]) for k in range(DK)] +
                        [tuple(w[:, h * j:h * (j + 1), :] for w in (ex.w2, *ex.w2s[i])) for j in range(2)])

            def scalar(self, act):
                act.wait_ge(self.w_in, 32)
                for whole, high, low in self.pieces():
                    act.activation(high, whole, ACT.Copy).then_inc(self.w_high, 1)

            def tensor(self, pe):
                pe.wait_ge(self.t_in, 16)
                for half in range(2):
                    for k in range(DK):
                        for t in range(self.HT):
                            mm = pe.transpose(bank(2 * half + k)[:, tok(t)],
                                              self.ex.tokens[:, half * self.HT + t, tok(k)], ident[:, :])
                        mm.then_inc(self.turned, 1)

            def vector_tokens(self, dve):
                high, low = self.ex.tT[self.i]
                for n in range(2 * DK):
                    half, k = divmod(n, DK)
                    r = slice(half * self.HALF, (half + 1) * self.HALF)
                    dve.wait_ge(self.turned, n + 1)
                    dve.tensor_copy(high[:, k, r], bank(n, self.HALF)).then_inc(self.t_high, 1)
                    dve.wait_ge(self.t_high, n + 1)
                    dve.tensor_tensor(low[:, k, r], bank(n, self.HALF), high[:, k, r].bitcast(F32),
                                      ALU.subtract).then_inc(self.t_low, 1)

            def vector_weights(self, dve):
                for n, (whole, high, low) in enumerate(self.pieces()):
                    dve.wait_ge(self.w_high, n + 1)
                    dve.tensor_tensor(low, whole, high.bitcast(F32), ALU.subtract).then_inc(self.w_low, 1)

        def first_expert_stage(ex):
            with stage("first_expert", NextExpert.SEMS) as (block, sems):
                nxt = NextExpert(sems, ex, 0)

                @block.sync
                def _(sp):
                    sp.wait_ge(sent, B * 16 * T + BEFORE)
                    nxt.sync(sp, 0)
                    nxt.arrived(sp)

                @block.tensor
                def _(pe):
                    nxt.tensor(pe)

                @block.scalar
                def _(act):
                    nxt.scalar(act)

                @block.vector
                def _(dve):
                    nxt.vector_weights(dve)
                    nxt.vector_tokens(dve)

        def expert_stage(e, ex, mine, following):
            (w1h, w1l), (w2h, w2l), (tTh, tTl), (hTh, hTl) = ex.w1s[mine], ex.w2s[mine], ex.tT[mine], ex.hT
            with stage("expert", 7 + NextExpert.SEMS) as (block, (up_done, gelued, high, low, down, biased, stored,
                                                                  *sems)), ExitStack() as tmp:
                g = sb("g", [P, 2, CAP // 2], stack=tmp)
                eo = xn
                HALF = CAP // 2
                HT = HALF // P
                nxt = NextExpert(sems, ex, 1 - mine)

                @block.sync
                def _(sp):
                    if following is not None:
                        nxt.sync(sp, following)
                    for t in range(CT):
                        sp.wait_ge(biased, t + 1)
                        sp.dma_start(slots_out.rearrange("(e t p) d -> e t p d", e=E, p=P)[bass.ds(e, 1), t]
                                     .rearrange("o p d -> (o p) d"), eo[:, t, :]).then_inc(stored, 16)
                    sp.wait_ge(stored, 16 * CT)
                    if following is not None:
                        nxt.arrived(sp)

                @block.tensor
                def _(pe):
                    for n in range(2 * FC):
                        half, f = divmod(n, FC)
                        r = slice(half * HALF, (half + 1) * HALF)
                        if n >= 2:
                            pe.wait_ge(gelued, n - 1)
                        for k in range(DK):
                            mm = exact3(pe, bank(4 + n % 2, HALF), w1h[:, k, tok(f)], w1l[:, k, tok(f)],
                                        tTh[:, k, r], tTl[:, k, r], k == 0, k == DK - 1)
                        mm.then_inc(up_done, 1)
                    if following is not None:
                        nxt.tensor(pe)
                    for t in range(CT):
                        pe.wait_ge(low, FC * (t // HT + 1))
                        if t >= 2:
                            pe.wait_ge(biased, t - 1)
                        for f in range(FC):
                            mm = exact3(pe, bank(6 + t % 2, D), hTh[:, f, tok(t)], hTl[:, f, tok(t)], w2h[:, f, :],
                                        w2l[:, f, :], f == 0, f == FC - 1)
                        mm.then_inc(down, 1)

                @block.scalar
                def _(act):
                    for n in range(2 * FC):
                        half, f = divmod(n, FC)
                        act.wait_ge(up_done, n + 1)
                        if n >= 2:
                            act.wait_ge(low, n - 1)
                        act.activation(g[:, n % 2, :], bank(4 + n % 2, HALF), ACT.Gelu,
                                       bias=ex.b1[mine][:, f:f + 1]).then_inc(gelued, 1)
                        act.wait_ge(gelued, n + 1)
                        act.activation(hTh[:, f, half * HALF:(half + 1) * HALF], g[:, n % 2, :],
                                       ACT.Copy).then_inc(high, 1)
                    if following is not None:
                        nxt.scalar(act)

                @block.vector
                def _(dve):
                    for n in range(2 * FC):
                        half, f = divmod(n, FC)
                        r = slice(half * HALF, (half + 1) * HALF)
                        dve.wait_ge(high, n + 1)
                        dve.tensor_tensor(hTl[:, f, r], g[:, n % 2, :], hTh[:, f, r].bitcast(F32),
                                          ALU.subtract).then_inc(low, 1)

                    def add_bias2(t):
                        dve.wait_ge(down, t + 1)
                        dve.tensor_tensor(eo[:, t, :], bank(6 + t % 2, D), ex.b2[mine][:, :],
                                          ALU.add).then_inc(biased, 1)
                    if following is not None:
                        nxt.vector_tokens(dve)
                    add_bias2(0)
                    if following is not None:
                        nxt.vector_weights(dve)
                    for t in range(1, CT):
                        add_bias2(t)

        def combine_stage(i, buffers):
            x2, got = buffers
            with stage("combine", 4) as (block, (xs, indexed, summed, stored)), ExitStack() as tmp:
                idx = sb("idx", [P, 2 * T], U32, stack=tmp)
                pr = sb("pr", [P, 2 * T], stack=tmp)
                of_pair = "(i b t p) d -> i b p t d"

                @block.sync
                def _(sp):
                    for b in range(2):
                        sp.dma_start(x2[:, b, :, :], residual.rearrange(of_pair, p=P, t=T, b=2)[bass.ds(i, 1), b]
                                     .rearrange("o p t d -> p (o t) d")).then_inc(xs, 16)
                    for b in range(2):
                        for h in range(NB):
                            sp.wait_ge(summed, (b * NB + h + 1) * TB)
                            sp.dma_start(out.rearrange(of_pair, p=P, t=T, b=2)[bass.ds(i, 1), b, :, h * TB:(h + 1) * TB]
                                         .rearrange("o p t d -> p (o t) d"), x2[:, b, h * TB:(h + 1) * TB, :]
                                         ).then_inc(stored, 16)
                    sp.wait_ge(stored, 16 * 2 * NB)

                @block.vector
                def _(dve):
                    dve.tensor_copy(idx[:, :], slot[:, bass.ds(i * (2 * T), 2 * T)]).then_inc(indexed, 1)
                    dve.tensor_copy(pr[:, :], prob[:, bass.ds(i * (2 * T), 2 * T)]).then_inc(indexed, 1)
                    dve.wait_ge(indexed, 2)
                    dve.wait_ge(xs, 32)
                    for n in range(2 * T):
                        b, t = divmod(n, T)
                        dve.wait_ge(fetched[n], i * 16 + 16)
                        dve.scalar_tensor_tensor(out=x2[:, b, t, :], in0=got[:, n, :], scalar=pr[:, n:n + 1],
                                                 in1=x2[:, b, t, :], op0=ALU.mult, op1=ALU.add).then_inc(summed, 1)

                @block.gpsimd
                def _(pool):
                    pool.wait_ge(indexed, 1)
                    for n in range(2 * T):
                        pool.indirect_dma_start(out=got[:, n, :], out_offset=None, in_=slots_out,
                                                in_offset=bass.IndirectOffsetOnAxis(ap=idx[:, n:n + 1], axis=0),
                                                bounds_check=SLOTS - 1, oob_is_err=True).then_inc(fetched[n], 16)

        def small_buffers(stack):
            return (sb("qT1", [P, G, S], stack=stack), sb("qTb1", [P, G, S], BF16, stack=stack),
                    sb("kbd", [P, G, GM], stack=stack), sb("kbdb", [P, G, GM], BF16, stack=stack),
                    sb("vbig", [P, len(CH), G, VW], stack=stack), sb("shift1", [H1, S], BF16, stack=stack))

        with nc.Fori(0, B) as b:
            at_start = turn[0]
            with ExitStack() as tmp:
                qT = [sb(f"qT0_{j}", [P, DK, S], F32R, stack=tmp) for j in "hl"]
                kT = [sb(f"kT0_{j}", [P, H0, KEYS0 + 3], F32R, stack=tmp) for j in "hl"]
                qTb = sb("qTb0", [P, DK, S], BF16, stack=tmp)
                kTb = sb("kTb0", [P, DK, KEYS0 + 3], BF16, stack=tmp)
                v_aug = sb("v0", [P, NK0, DK, 3 * DH0], stack=tmp)
                first_norm_stage(b, kT)
                qkv0_stage(qT, kT, qTb, kTb, v_aug)
                attend0_stage(qT, kT, qTb, kTb, v_aug, xT)
            moe0_stage()
            with ExitStack() as tmp:
                small = small_buffers(tmp)
                small_prepare_stage("prepare1", "w1", "bo1", True, w1_q, w1_k, w1_v, "bq1", *small)
                clipped_attend_stage("attend1", small[0], small[2], small[4], small[5], xn)
            project_stage("project1", xn, w1_o, "w1", DK, 1)
            moe1_stage()
            with ExitStack() as tmp:
                kT = [sb(f"kT2_{j}", [P, H2, M], F32R, stack=tmp) for j in "hl"]
                kTb = sb("kTb2", [P, KC2, M], BF16, stack=tmp)
                v_aug = sb("v2", [P, H2, DH2 + 1], stack=tmp)
                attend2_stage(kT, kTb, v_aug)
            lora_stage()
            with ExitStack() as tmp:
                small = small_buffers(tmp)
                small_prepare_stage("prepare3", "w3", "b2_3", False, w3_q, w3_k, w3_v, "bq3", *small)
                small_attend_stage("attend3", small[0], small[2], small[4], small[5], xn)
            mlp3_stage(xn)
            dispatch_stage(b)
            if turn[0] != at_start:
                with stage("even", 0):
                    pass
        arena.close()
        with ExitStack() as tmp:
            ex = Experts(tmp)
            first_expert_stage(ex)
            with nc.Fori(0, E // 2 - 1) as i:
                expert_stage(i * 2, ex, 0, i * 2 + 1)
                expert_stage(i * 2 + 1, ex, 1, i * 2 + 2)
            expert_stage(E - 2, ex, 0, E - 1)
            expert_stage(E - 1, ex, 1, None)
        with ExitStack() as tmp:
            x2 = sb("x2", [P, 2, T, D], stack=tmp)
            got = sb("got", [P, 2 * T, D], stack=tmp)
            with nc.Fori(0, B // 2) as i:
                combine_stage(i, (x2, got))
                with stage("even_again", 0):
                    pass


def kernel(**inputs):
    import numpy as np
    import concourse.bacc as bacc
    from concourse.bass_utils import run_bass_kernel_spmd

    arrays = layout(inputs)
    nc = bacc.Bacc("TRN2", target_bir_lowering=False, num_devices=1)
    args = {n: nc.dram_tensor("in_" + n, v.shape, mybir.dt.from_np(v.dtype), kind="ExternalInput").ap()
            for n, v in arrays.items()}
    out = nc.dram_tensor("out", [B * S, D], F32, kind="ExternalOutput").ap()
    flamingo_kernel(nc, args, out)
    r = run_bass_kernel_spmd(nc, [{"in_" + n: v for n, v in arrays.items()}], core_ids=[0])
    return r.results[0]["out"].reshape(B, S, D)


def layout(inputs):
    import numpy as np

    v = {n: np.asarray(i) for n, i in inputs.items()}
    out = {n: v[n] for n in (
        "x", "ctx_768", "L0_ffn_router_w", "L0_ffn_expert_w", "L0_ffn_expert_b", "L1_xattn_Wq", "L1_xattn_Wo",
        "L1_ffn_gate_w", "L1_ffn_w1", "L1_ffn_w2", "L1_ffn_w3", "L2_xattn_Wq", "L2_xattn_Wkv", "L2_xattn_Wproj",
        "L2_ffn_kernel", "L2_ffn_a", "L2_ffn_b", "L3_xattn_Wq", "L3_xattn_W1", "L3_xattn_W2", "L3_ffn_w1",
        "L3_ffn_w2", "L3_ffn_b2")}
    out["mask"] = v["mask_BxS2_bk0"]
    out["w0_qkv"] = np.concatenate([v["L0_xattn_Wq"], v["L0_xattn_Wlkv"]]).T
    out["w0_ckv"] = v["L0_xattn_Wkv"].T
    out["w0_o"] = v["L0_xattn_Wo"].T
    for i in (1, 3):
        for w in "kv":
            out[f"w{i}_{w}"] = np.concatenate([v[f"L{i}_xattn_W{w}"], v[f"L{i}_xattn_b{w}"][None]])
    out["r3"] = v["L3_ffn_router_w"].T
    out["b1_cols"] = v["L3_ffn_b1"].reshape(E, FC, P).transpose(0, 2, 1)

    def columns(vector):
        return np.pad(vector, (0, -len(vector) % P)).reshape(-1, P).T

    def same(vector):
        return np.broadcast_to(vector, (P, len(vector)))

    out["cols"] = np.concatenate([
        same(v["g_xattn"]), same(v["g_ffn"]), same(v["L0_ffn_router_b"]), columns(v["L0_xattn_ln_x_g"]),
        columns(v["L0_xattn_ln_x_b"]), columns(v["L0_xattn_ln_l_g"]), columns(v["L0_xattn_ln_l_b"]),
        columns(np.tile(v["L0_xattn_qn_g"], 2)), columns(np.tile(v["L0_xattn_kn_g"], 2)),
        columns(v["L1_xattn_bq"]), columns(v["L3_xattn_bq"]), columns(v["L3_xattn_b1"])], axis=1)
    out["rows"] = np.concatenate([same(v[n]) for n in (
        "L0_xattn_bo", "L1_xattn_bo", "L2_xattn_bproj", "L2_ffn_bias", "L3_xattn_b2")], axis=1)
    return {n: np.ascontiguousarray(i) for n, i in out.items()}
```
